# Optimizing a Trainium2 kernel written in Bass

```python
import numpy as np
import jax
import jax.numpy as jnp

def _softmax(x, axis=-1):
    return jax.nn.softmax(x, axis=axis)

def _gelu(x):
    return jax.nn.gelu(x, approximate=True)

def _silu(x):
    return jax.nn.silu(x)

def _sigmoid(x):
    return jax.nn.sigmoid(x)

def _layernorm(x, axis=-1, eps=1e-05):
    m = jnp.mean(x, axis=axis, keepdims=True)
    v = jnp.var(x, axis=axis, keepdims=True)
    return (x - m) / jnp.sqrt(v + eps)

def _scatter_add(tgt, idx, src, axis=0):
    return tgt.at[idx].add(src)

def _segment_sum(src, seg, n):
    return jax.ops.segment_sum(src, seg, n)
kernel_name = 'mk_prb_d1_jaxref_r4_ddc688'

def setup_inputs(seed: int=0):
    np.random.seed(seed)
    _w = jnp.asarray

    def _L0_attn_setup():
        import jax, jax.numpy as jnp
        import numpy as np
        E = 256
        H = 16
        D = E // H
        WIN = 64
        STRIDE = 128
        G = 1
        B = 2
        L = 4097
        key = jax.random.key(seed)
        ks = jax.random.split(key, 9)
        s = 0.02
        return {'hidden_states': jax.random.normal(ks[0], (B, L, E), jnp.float32), 'Wq': jax.random.normal(ks[1], (E, E), jnp.float32) * s, 'bq': jnp.zeros((E,), jnp.float32), 'Wk': jax.random.normal(ks[2], (E, E), jnp.float32) * s, 'bk': jnp.zeros((E,), jnp.float32), 'Wv': jax.random.normal(ks[3], (E, E), jnp.float32) * s, 'bv': jnp.zeros((E,), jnp.float32), 'Wo': jax.random.normal(ks[4], (E, E), jnp.float32) * s, 'bo': jnp.zeros((E,), jnp.float32)}
    _L0_attn_in = _L0_attn_setup()

    def _L0_ffn_setup():
        import jax, jax.numpy as jnp
        import numpy as np
        B, S, D = (4, 1024, 256)
        H = 1024
        RH = 256
        E = 16
        K = 2
        NS = 1

        def _swiglu(x, w1, w2, w3):
            return jax.nn.silu(x @ w1) * (x @ w2) @ w3
        key = jax.random.key(seed)
        ks = jax.random.split(key, 9)
        s = 0.02
        return {'x': jax.random.normal(ks[0], (B, S, D), dtype=jnp.float32), 'router_w': jax.random.normal(ks[1], (D, E), dtype=jnp.float32) * s, 'expert_bias': jnp.zeros((E,), dtype=jnp.float32), 'shared_w1': jax.random.normal(ks[2], (NS, D, H), dtype=jnp.float32) * s, 'shared_w2': jax.random.normal(ks[3], (NS, D, H), dtype=jnp.float32) * s, 'shared_w3': jax.random.normal(ks[4], (NS, H, D), dtype=jnp.float32) * s, 'routed_w1': jax.random.normal(ks[5], (E, D, RH), dtype=jnp.float32) * s, 'routed_w2': jax.random.normal(ks[6], (E, D, RH), dtype=jnp.float32) * s, 'routed_w3': jax.random.normal(ks[7], (E, RH, D), dtype=jnp.float32) * s}
    _L0_ffn_in = _L0_ffn_setup()
    _d = {'L0_attn_hidden_states': _L0_attn_in['hidden_states'], 'L0_attn_Wq': _L0_attn_in['Wq'], 'L0_attn_bq': _L0_attn_in['bq'], 'L0_attn_Wk': _L0_attn_in['Wk'], 'L0_attn_bk': _L0_attn_in['bk'], 'L0_attn_Wv': _L0_attn_in['Wv'], 'L0_attn_bv': _L0_attn_in['bv'], 'L0_attn_Wo': _L0_attn_in['Wo'], 'L0_attn_bo': _L0_attn_in['bo'], 'L0_ffn_router_w': _L0_ffn_in['router_w'], 'L0_ffn_expert_bias': _L0_ffn_in['expert_bias'], 'L0_ffn_shared_w1': _L0_ffn_in['shared_w1'], 'L0_ffn_shared_w2': _L0_ffn_in['shared_w2'], 'L0_ffn_shared_w3': _L0_ffn_in['shared_w3'], 'L0_ffn_routed_w1': _L0_ffn_in['routed_w1'], 'L0_ffn_routed_w2': _L0_ffn_in['routed_w2'], 'L0_ffn_routed_w3': _L0_ffn_in['routed_w3']}
    _x0 = _d['L0_attn_hidden_states']
    _d['L0_attn_hidden_states'] = jax.random.normal(jax.random.fold_in(jax.random.key(seed), 1), (8, 512, 256), dtype=_x0.dtype)
    del _x0
    return _d

def reference(L0_attn_hidden_states, L0_attn_Wq, L0_attn_bq, L0_attn_Wk, L0_attn_bk, L0_attn_Wv, L0_attn_bv, L0_attn_Wo, L0_attn_bo, L0_ffn_router_w, L0_ffn_expert_bias, L0_ffn_shared_w1, L0_ffn_shared_w2, L0_ffn_shared_w3, L0_ffn_routed_w1, L0_ffn_routed_w2, L0_ffn_routed_w3):

    def _L0_attn_ref(hidden_states, Wq, bq, Wk, bk, Wv, bv, Wo, bo):
        import jax, jax.numpy as jnp
        import numpy as np
        E = 256
        H = 16
        D = E // H
        WIN = 64
        STRIDE = 128
        G = 1
        B = 2
        L = 4097
        b, seq_len, e = hidden_states.shape
        scale = 1.0 / jnp.sqrt(jnp.asarray(D, hidden_states.dtype))
        q = (hidden_states @ Wq + bq).reshape(b, seq_len, H, D)
        k = (hidden_states @ Wk + bk).reshape(b, seq_len, H, D)
        v = (hidden_states @ Wv + bv).reshape(b, seq_len, H, D)
        qg = q[:, :G]
        gw = jnp.einsum('bghd,bshd->bhgs', qg, k) * scale
        gp = jax.nn.softmax(gw, axis=-1)
        gctx = jnp.einsum('bhgs,bshd->bghd', gp, v).reshape(b, G, e)
        ql, kl, vl = (q[:, G:], k[:, G:], v[:, G:])
        Lc = seq_len - G
        num_windows = max(1, (Lc - WIN) // STRIDE + 1)
        starts = jnp.arange(num_windows) * STRIDE
        widx = starts[:, None] + jnp.arange(WIN)
        qw = ql[:, widx]
        kw = kl[:, widx]
        vw = vl[:, widx]
        aw = jnp.einsum('bwqhd,bwkhd->bwhqk', qw, kw) * scale
        ap = jax.nn.softmax(aw, axis=-1)
        ctx = jnp.einsum('bwhqk,bwkhd->bwqhd', ap, vw)
        ctx = ctx.reshape(b, num_windows * WIN, e)
        flat = widx.reshape(-1)
        local = jnp.zeros((b, Lc, e), hidden_states.dtype).at[:, flat].add(ctx)
        counts = jnp.zeros((Lc,), hidden_states.dtype).at[flat].add(1.0)
        counts = jnp.maximum(counts, 1.0)
        local = local / counts[None, :, None]
        out = jnp.concatenate([gctx, local], axis=1)
        return out @ Wo + bo

    def _L0_ffn_ref(x, router_w, expert_bias, shared_w1, shared_w2, shared_w3, routed_w1, routed_w2, routed_w3):
        import jax, jax.numpy as jnp
        import numpy as np
        B, S, D = (4, 1024, 256)
        H = 1024
        RH = 256
        E = 16
        K = 2
        NS = 1

        def _swiglu(x, w1, w2, w3):
            return jax.nn.silu(x @ w1) * (x @ w2) @ w3
        shared_out = jnp.sum(jax.vmap(lambda w1, w2, w3: _swiglu(x, w1, w2, w3))(shared_w1, shared_w2, shared_w3), axis=0)
        scores = jax.nn.sigmoid(x @ router_w)
        sel_scores = scores + expert_bias
        _, top_idx = jax.lax.top_k(sel_scores, K)
        top_scores = jnp.take_along_axis(scores, top_idx, axis=-1)
        gates = jnp.sum(jax.nn.one_hot(top_idx, E, dtype=scores.dtype) * top_scores[..., None], axis=-2)
        xf = x.reshape(-1, D)
        gf = gates.reshape(-1, E).T

        def body(acc, ws):
            w1, w2, w3, g = ws
            return (acc + _swiglu(xf, w1, w2, w3) * g[:, None], None)
        routed_out, _ = jax.lax.scan(body, jnp.zeros_like(xf), (routed_w1, routed_w2, routed_w3, gf))
        return shared_out + routed_out.reshape(x.shape)
    x = L0_attn_hidden_states
    xn = _layernorm(x, axis=-1)
    x = x + _L0_attn_ref(xn, L0_attn_Wq, L0_attn_bq, L0_attn_Wk, L0_attn_bk, L0_attn_Wv, L0_attn_bv, L0_attn_Wo, L0_attn_bo) + _L0_ffn_ref(xn, L0_ffn_router_w, L0_ffn_expert_bias, L0_ffn_shared_w1, L0_ffn_shared_w2, L0_ffn_shared_w3, L0_ffn_routed_w1, L0_ffn_routed_w2, L0_ffn_routed_w3)
    return x

_drawn_inputs = setup_inputs


def setup_inputs(seed=0):
    import zlib

    import numpy as np

    out = dict(_drawn_inputs(seed))
    spreads = {'L0_attn_bq': (0.0, 0.8),
     'L0_attn_bk': (0.0, 2.0),
     'L0_attn_bv': (0.0, 0.35),
     'L0_attn_bo': (0.0, 0.1),
     'L0_ffn_expert_bias': (0.0, 0.517)}
    factors = {'L0_attn_Wq': 8.0,
     'L0_attn_Wk': 8.0,
     'L0_attn_Wv': 6.297,
     'L0_ffn_router_w': 5.674,
     'L0_ffn_routed_w1': 4.245,
     'L0_ffn_routed_w2': 4.202,
     'L0_ffn_routed_w3': 4.196,
     'L0_ffn_shared_w1': 3.19,
     'L0_ffn_shared_w2': 3.157,
     'L0_ffn_shared_w3': 3.16}
    for name, (base, spread) in spreads.items():
        noise = np.random.default_rng([zlib.crc32(name.encode()), seed]).standard_normal(out[name].shape)
        drawn = base * np.exp(spread * noise) if base else spread * noise
        out[name] = jnp.asarray(drawn.astype(out[name].dtype))
    for name, factor in factors.items():
        out[name] = (out[name] * factor).astype(out[name].dtype)
    return out
```

```python
from contextlib import ExitStack

import numpy as np
import concourse.bass as bass
from concourse import mybir

P = 128
B, L, D = 8, 512, 256
KD = D // P
TB = L // P
NTOK = B * TB
NH, HD = 16, 16
WIN, STRIDE = 64, 128
NE, RH = 16, 256
SH = 1024
SC = SH // P
NT = (B * L * 2) // P + NE
EXPERT = 2 * KD * RH + (RH // P) * D
B_FIRST = 4
EPS = 1e-5
TOP = 64.0

F32, F16 = mybir.dt.float32, mybir.dt.float16
U32, I32 = mybir.dt.uint32, mybir.dt.int32
ALU = mybir.AluOpType
ACT = mybir.ActivationFunctionType
AX = mybir.AxisListType.X
RMAX = bass.bass_isa.ReduceOp.max

C_ID, C_EVEN, C_ODD, C_TOK, C_IE, C_HM, C_PW, C_IS = 0, 128, 129, 130, 258, 274, 306, 310
C_N = C_IS + NT


def constants():
    c = np.zeros((P, C_N), np.float32)
    p = np.arange(P)
    c[:, C_ID:C_ID + P] = np.eye(P)
    c[:, C_EVEN] = (p // HD) % 2 == 0
    c[:, C_ODD] = (p // HD) % 2 == 1
    c[:, C_TOK:C_TOK + P] = (p >= 1) & (p <= WIN)
    c[:, C_IE:C_IE + NE] = np.arange(NE)
    for m in range(KD):
        c[:, C_HM + m * NH:C_HM + (m + 1) * NH] = ((m * P + p)[:, None] // HD) == np.arange(NH)
    c[:, C_PW:C_PW + 4] = -0.5
    c[:, C_IS:C_IS + NT] = np.arange(NT)
    h = np.zeros((P, 2 * P), np.float16)
    h[:, 0:P] = p[:, None] < p[None, :]
    h[:, P:] = 1.0
    return c, h


PART1 = "DDAADADDD"
PART2 = "ADADADDDD"
U_XT, U_R, U_Q, U_K, U_V = 0, 2, 3, 5, 7
U_GT, U_U, U_PT, U_AV, U_WO = 0, 1, 2, 6, 7
RING = 3


def place(part, n):
    if part == 1:
        return 0 if isinstance(n, int) and n == 0 else n * 18 - 9
    return n * 18 + (9 if isinstance(n, int) and n == B - 1 else 18)


def emptied_before(who, part, n):
    one, two = PART1.count(who), PART2.count(who)
    if part == 1:
        return 0 if isinstance(n, int) and n == 0 else n * (one + two) - two
    if isinstance(n, int) and n == B - 1:
        return one * B + two * (B - 1)
    return n * (one + two) + 2 * one


def emptied(who, part, n, u):
    return emptied_before(who, part, n) + (PART1 if part == 1 else PART2)[:u + 1].count(who)


def moe_layer(nc, a, out):
    with ExitStack() as ctx:
        def sb(name, shape, dt=F32):
            return ctx.enter_context(nc.sbuf_tensor(name, shape, dt))[:]

        def sem(name):
            return ctx.enter_context(nc.semaphore(name))

        xs_dram = nc.dram_tensor("rows_by_slot", (NT * P, D), F32, kind="Internal").ap()
        ys_dram = nc.dram_tensor("routed_by_slot", (NT * P, D), F32, kind="Internal").ap()
        y1_dram = nc.dram_tensor("x_plus_attention", (B * L, D), F32, kind="Internal").ap()
        y2_dram = nc.dram_tensor("plus_shared", (B * L, D), F32, kind="Internal").ap()
        x_rows = a["L0_attn_hidden_states"].rearrange("b (t p) d -> b p t d", p=P)
        y1_rows = y1_dram.rearrange("(b t p) d -> b p t d", p=P, t=TB)
        y2_rows = y2_dram.rearrange("(b t p) d -> b p t d", p=P, t=TB)
        out_rows = out.rearrange("b (t p) d -> b p t d", p=P)

        cf = sb("const_f32", [P, C_N])
        ch = sb("const_f16", [P, 2 * P], F16)
        ident = cf[:, C_ID:C_ID + P]
        wa = [sb(f"attn_w_{x}", [P, 4, KD, D], F16) for x in ("high", "low")]
        wr = [sb(f"router_w_{x}", [P, KD, NE], F16) for x in ("high", "low")]
        w12 = [sb(f"shared_w12_{x}", [P, 2, KD, SH], F16) for x in ("high", "low")]
        w3 = [sb(f"shared_w3_{x}", [P, SC, D], F16) for x in ("high", "low")]
        XPAD = WIN
        xT = [sb(f"xn_T_{x}", [P, KD, XPAD + B * L], F16) for x in ("high", "low")]
        mx = sb("w_max", [P, 12])
        pw = sb("w_pow", [P, 12])
        inv = sb("w_inv", [P, 12])
        scl = sb("w_scale", [P, 12])
        der = sb("w_derived", [P, 12])
        D_QE, D_QO, D_O, D_Y, D_HS, D_RY, D_RHS = range(7)
        bqkv = sb("bqkv_columns", [P, 3 * KD])
        bq, bk, bv = (bqkv[:, i * KD:(i + 1) * KD] for i in range(3))
        bqp = sb("bq_by_parity", [P, 2, KD])
        bias_tile = sb("out_bias", [P, D]); bv_out = sb("bv_times_wo", [B, D])
        eb = sb("expert_bias", [P, NE])
        logits = sb("router_logits", [P, NTOK, NE])
        gate = sb("gates", [P, 2, NTOK])
        slots = sb("slots", [P, 2, NTOK], U32)
        etab = sb("expert_offset_of_tile", [1, NT], I32)
        uT = [sb(f"u_T_{x}", [P, KD, B, NH], F16) for x in ("high", "low")]
        zero = sb("zeros", [P, D])

        arena = sb("arena", [P, (NE + 1) * EXPERT])
        at = [0]

        def cut(*dims, dt=F32):
            n = int(np.prod(dims))
            fl = n if dt == F32 else n // 2
            v = arena[:, at[0]:at[0] + fl]
            at[0] += fl
            if dt != F32:
                v = v.bitcast(dt)
            if len(dims) == 2:
                v = v.rearrange("p (a b) -> p a b", a=dims[0])
            if len(dims) == 3:
                v = v.rearrange("p (a b c) -> p a b c", a=dims[0], b=dims[1])
            return v

        E = [cut(4, 8, WIN) for _ in range(2)]
        route_area = arena[:, 0:2 * 4 * 8 * WIN]
        PT = cut(4, 4, P)
        QT = [cut(KD, TB * (WIN + 1)) for _ in range(2)]
        KT = cut(KD, L)
        VB = [cut(TB, 8, 32) for _ in range(2)]
        xr = [cut(TB, D) for _ in range(2)]
        xb = [cut(TB, D) for _ in range(2)]
        xnr = [cut(TB, D) for _ in range(2)]
        cT = [cut(KD, TB, P, dt=F16) for _ in range(2)]
        assert at[0] <= (NE + 1) * EXPERT - NTOK * D, at[0]
        xn = arena[:, (NE + 1) * EXPERT - NTOK * D:].rearrange("p (t d) -> p t d", t=NTOK)
        ar16 = arena[:, :].bitcast(F16)

        work = sb("work", [P, 2080 + 2 * KD * SH])
        wa_raw = work[:, 0:4 * KD * D].rearrange("p (i k d) -> p i k d", i=4, k=KD)
        wr_raw = work[:, 2048:2048 + KD * NE].rearrange("p (k e) -> p k e", k=KD)
        w12_raw = work[:, 2080:2080 + 2 * KD * SH].rearrange("p (i k h) -> p i k h", i=2, k=KD)
        w3_raw = E[1].rearrange("p g k c -> p (g k c)").rearrange("p (c d) -> p c d", c=SC)
        wat = [0]

        def wcut(n, dt=F32):
            v = work[:, wat[0]:wat[0] + n]
            wat[0] += n
            return v.bitcast(dt) if dt != F32 else v

        s_silu = [wcut(L) for _ in range(2)]
        s_h = [wcut(L) for _ in range(2)]
        s_hh = [[wcut(L // 2, F16) for _ in range(2)] for _ in range(2)]
        s_y = [wcut(TB * D).rearrange("p (t d) -> p t d", t=TB) for _ in range(2)]
        assert wat[0] <= 2080 + 2 * KD * SH
        wat[0] = 0
        xs = [wcut(D) for _ in range(2)]
        r_x = [[wcut(D // 2, F16) for _ in range(2)] for _ in range(2)]
        r_silu = [wcut(RH) for _ in range(2)]
        r_h = [wcut(RH) for _ in range(2)]
        r_hh = [[wcut(RH // 2, F16) for _ in range(2)] for _ in range(2)]
        ys = [wcut(D) for _ in range(2)]
        assert wat[0] <= 6 * L, wat[0]

        gs = sb("global_p", [P, L])
        q0 = sb("global_q", [P, KD, NH])
        gp = sb("global_p_T", [P, TB, NH])
        rmx = sb("routed_w_max", [P, 3, NE])
        tick = sb("tick", [1, 16])
        st = sb("ln_stats", [P, TB, 6]); mv = sb("ln_mean_var", [P, TB, 2])
        ve = sb("ln_var_eps", [P, TB]); rstd = sb("ln_rstd", [P, TB]); nmr = sb("ln_shift", [P, TB])
        smx = sb("softmax_max", [P, 4, 8]); ssum = sb("softmax_sum", [P, 4, 8]); srec = sb("softmax_rec", [P, 4, 8])
        gmx = sb("global_neg_max", [NH, 1]); gsum = sb("global_sum", [NH, 1]); grec = sb("global_rec", [NH, 1])
        c0f = sb("ctx0_f32", [P, KD, B]); c0 = [sb(f"ctx0_{x}", [P, KD, B], F16) for x in ("high", "low")]
        c0m = sb("ctx0_masked", [P, B, NH]); out0 = sb("out0", [B, D])
        bvm = PT[:, 0, 0:KD, :]

        g1 = [[arena[:, (2 * k + i) * D:(2 * k + i + 1) * D] for i in range(2)] for k in range(2)]
        c_y = [arena[:, (4 + i) * D:(5 + i) * D] for i in range(2)]

        ra = [route_area[:, i * 512:(i + 1) * 512].rearrange("p (t e) -> p t e", e=NE) for i in range(8)]
        sc_, sel, oh1, oh2, tmp, cumA, cumB, posn = ra
        mx8 = arena[:, 4096:4352].rearrange("p (t e) -> p t e", e=8)
        ix8 = arena[:, 4352:4608].bitcast(U32).rearrange("p (t e) -> p t e", e=8)
        ixf = sb("top_indices_f32", [P, NTOK, 2])
        ohm = arena[:, 4608:4864].bitcast(F16).rearrange("p (t e) -> p t e", e=NE)
        tl = [sb(f"tiles_{i}", [P, NE]) for i in range(5)]
        slf = sb("slots_f32", [P, 2, NTOK])
        ecount = arena[0:1, 4864:4864 + NT * NE].rearrange("p (t e) -> p t e", e=NE)
        ef = sb("expert_of_tile", [1, NT])

        ps = ctx.enter_context(nc.psum_tensor("ps", [P, 8, 512], F32))
        S = ps[:, 0:4, :]
        G = ps[:, 4, :]

        def T(pos):
            return ps[:, 5 + pos % RING, :]

        s = {n: sem(n) for n in (
            "consts_in attn_w_in shared_w_in bias_in zeros_ready xs_zeroed "
            "attn_max attn_all_max shared_max shared_all_max routed_max routed_all_max "
            "scale_ready attn_high attn_low shared_high shared_low routed_high routed_low setup "
            "bias_psum bias_ready pads_ready "
            "x_in0 x_in1 ln_stats ln_mv ln_var ln_rstd ln_shift xn_made xn_kept xb_made xT_high "
            "unit_full act_empty dve_empty s_full s_max s_taken s_exp s_summed soft_sum vector_step routed_each p_ready "
            "q0_half q0_ready g_full g_max g_exp g_rec g_ready u_high ctx_high "
            "y1_stored0 y1_stored1 c0_full c0_step c0_ready out0_full out0_ready out0_added "
            "scores_ready route chosen_ready prefix_full slots_ready table_ready scattered "
            "raw_in a_full silu_done h_done hh_high hh_low y_full y_in0 y_in1 y_done y2_stored0 y2_stored1 "
            "xs_in0 xs_in1 rx_full rx_high rx_low ab_full r_silu_done r_h_done rh_full rh_high rh_low "
            "ry_full ry_done ys_stored0 ys_stored1 "
            "pick_in0 pick_in1 base_in0 base_in1 mixed one_added out_stored0 out_stored1").split()}
        block = ctx.enter_context(nc.Block())

        SPLIT = ((0, 0), (1, 0), (0, 1))

        def pairs(eng, body, first, last):
            with eng.Fori(first // 2, last // 2) as i:
                for par in range(2):
                    body(i * 2 + par, par)

        @block.sync
        def _(sp):
            sp.dma_start(wa_raw[:, 0], a["L0_attn_Wq"].rearrange("(k p) d -> p k d", p=P)).then_inc(s["attn_w_in"], 16)
            sp.dma_start(wa_raw[:, 1], a["L0_attn_Wk"].rearrange("(k p) d -> p k d", p=P)).then_inc(s["attn_w_in"], 16)
            sp.dma_start(wa_raw[:, 2], a["L0_attn_Wv"].rearrange("(k p) d -> p k d", p=P)).then_inc(s["attn_w_in"], 16)
            sp.dma_start(wa_raw[:, 3], a["L0_attn_Wo"].rearrange("(k p) d -> p k d", p=P)).then_inc(s["attn_w_in"], 16)
            sp.dma_start(wr_raw, a["L0_ffn_router_w"].rearrange("(k p) e -> p k e", p=P)).then_inc(s["attn_w_in"], 16)
            for n in range(2):
                sp.dma_start(xr[n], x_rows[n]).then_inc(s[f"x_in{n}"], 16)
            for i, name in enumerate(("shared_w1", "shared_w2")):
                sp.dma_start(w12_raw[:, i], a[f"L0_ffn_{name}"].rearrange("o (k p) h -> p (o k) h", p=P)).then_inc(s["shared_w_in"], 16)
            sp.dma_start(w3_raw, a["L0_ffn_shared_w3"].rearrange("o (c p) d -> p (o c) d", p=P)).then_inc(s["shared_w_in"], 16)
            sp.wait_ge(s["zeros_ready"], 1)
            sp.dma_start(xs_dram.rearrange("(p a) d -> p a d", p=P),
                         zero[:, :].unsqueeze(1).to_broadcast([P, NT, D])).then_inc(s["xs_zeroed"], 16)

            def attention(n, par, load=True):
                if load:
                    sp.wait_ge(s["xn_made"], n + 1)
                    sp.wait_ge(s["xb_made"], n + 1)
                    sp.dma_start(xr[par], x_rows[bass.ds(n + 2, 1)].rearrange("a p t d -> p (a t) d")).then_inc(s[f"x_in{par}"], 16)
                sp.wait_ge(s["dve_empty"], emptied("D", 2, n, U_WO + 1))
                sp.dma_start(y1_rows[bass.ds(n, 1)].rearrange("a p t d -> p (a t) d"), xb[par]).then_inc(s[f"y1_stored{par}"], 16)

            pairs(sp, attention, 0, B - 2)
            attention(B - 2, 0, load=False)
            attention(B - 1, 1, load=False)

            def shared(b0, b1):
                def load(b, par):
                    sp.dma_start(s_y[par], y1_rows[b]).then_inc(s[f"y_in{par}"], 16)
                for b in range(b0, b1):
                    par = b % 2
                    if b == b0:
                        if b >= 2:
                            sp.wait_ge(s[f"y2_stored{par}"], 16 * (b // 2))
                        load(b, par)
                    if b + 1 < b1:
                        if b >= 1:
                            sp.wait_ge(s[f"y2_stored{1 - par}"], 16 * ((b + 1) // 2))
                        load(b + 1, 1 - par)
                    sp.wait_ge(s["y_done"], b + 3)
                    sp.dma_start(y2_rows[b], s_y[par]).then_inc(s[f"y2_stored{par}"], 16)

            for par in range(2):
                sp.wait_ge(s[f"y1_stored{par}"], 16 * (B // 2))
            sp.wait_ge(s["out0_added"], 16)
            sp.wait_ge(s["shared_low"], 1)
            shared(0, B_FIRST)

            sp.wait_ge(s["scattered"], 16 * 2 * NTOK)
            sp.wait_ge(s["route"], 1)
            for e in range(NE):
                raw = arena[:, (e + 1) * EXPERT:(e + 2) * EXPERT]
                r12 = raw[:, 0:2 * KD * RH].rearrange("p (k i h) -> p k i h", k=KD, i=2)
                sp.dma_start(r12[:, :, 0, :], a["L0_ffn_routed_w1"][e].rearrange("(k p) h -> p k h", p=P)).then_inc(s["raw_in"], 16)
                sp.dma_start(r12[:, :, 1, :], a["L0_ffn_routed_w2"][e].rearrange("(k p) h -> p k h", p=P)).then_inc(s["raw_in"], 16)
                sp.dma_start(raw[:, 2 * KD * RH:].rearrange("p (c d) -> p c d", d=D),
                             a["L0_ffn_routed_w3"][e].rearrange("(c p) d -> p c d", p=P)).then_inc(s["raw_in"], 16)

            def load_rows(t, par):
                sp.dma_start(xs[par], xs_dram[bass.ds(t * P, P)] if not isinstance(t, int) else xs_dram[t * P:(t + 1) * P]).then_inc(s[f"xs_in{par}"], 16)

            def store_rows(t, par):
                sp.wait_ge(s["ry_done"], t + 1)
                sp.dma_start(ys_dram[bass.ds(t * P, P)] if not isinstance(t, int) else ys_dram[t * P:(t + 1) * P], ys[par]).then_inc(s[f"ys_stored{par}"], 16)

            sp.wait_ge(s["y_done"], B_FIRST + 2)
            load_rows(0, 0)
            load_rows(1, 1)

            def routed(t, par):
                sp.wait_ge(s["rx_full"], t - 1)
                load_rows(t, par)
                store_rows(t - 3, 1 - par)

            for t in (2, 3):
                sp.wait_ge(s["rx_full"], t - 1)
                load_rows(t, t % 2)
            store_rows(0, 0)
            pairs(sp, routed, 4, NT)
            store_rows(NT - 3, 1)
            store_rows(NT - 2, 0)
            store_rows(NT - 1, 1)
            shared(B_FIRST, B)

            for t in range(NTOK + 1):
                if t < NTOK:
                    par = t % 2
                    b = t // TB
                    sp.wait_ge(s[f"y2_stored{b % 2}"], 16 * (b // 2 + 1))
                    if t >= 2:
                        sp.wait_ge(s[f"out_stored{par}"], 16 * (t // 2))
                    sp.dma_start(c_y[par], y2_rows[b][:, t % TB]).then_inc(s[f"base_in{par}"], 16)
                if t >= 1:
                    q = (t - 1) % 2
                    sp.wait_ge(s["mixed"], t)
                    sp.dma_start(out_rows[(t - 1) // TB][:, (t - 1) % TB], c_y[q]).then_inc(s[f"out_stored{q}"], 16)
            for par in range(2):
                sp.wait_ge(s[f"out_stored{par}"], 16 * (NTOK // 2))

        @block.gpsimd
        def _(pool):
            pool.dma_start(cf[:, :], a["const_f32"]).then_inc(s["consts_in"], 16)
            pool.dma_start(ch[:, :], a["const_f16"]).then_inc(s["consts_in"], 16)
            pool.dma_start(bqkv[:, :], a["bias_columns"]).then_inc(s["bias_in"], 16)
            pool.dma_start(bias_tile[:, :], a["L0_attn_bo"].unsqueeze(0).to_broadcast([P, D])).then_inc(s["bias_in"], 16)
            pool.dma_start(eb[:, :], a["L0_ffn_expert_bias"].unsqueeze(0).to_broadcast([P, NE])).then_inc(s["bias_in"], 16)
            nc.gpsimd.memset(zero[:, :], 0.0).then_inc(s["zeros_ready"], 1)
            for v in VB:
                nc.gpsimd.memset(v, 0.0)
            nc.gpsimd.memset(cT[0], 0.0)
            for x in xT:
                nc.gpsimd.memset(x[:, :, 0:XPAD], 0.0)
            nc.gpsimd.memset(cT[1], 0.0).then_inc(s["pads_ready"], 1)
            pool.wait_ge(s["attn_max"], 2)
            nc.gpsimd.partition_all_reduce(pw[:, 0:5], mx[:, 0:5], P, RMAX).then_inc(s["attn_all_max"], 1)

            def rstd_of(n):
                pool.wait_ge(s["ln_var"], n + 1)
                nc.gpsimd.tensor_tensor(rstd[:, :], ve[:, :], cf[:, C_PW:C_PW + TB], ALU.pow).then_inc(s["ln_rstd"], 1)

            def rows_of(n, par, stored):
                if stored:
                    pool.wait_ge(s[f"y1_stored{par}"], (n + (-par)) * 8)
                nc.gpsimd.tensor_tensor(xb[par], xr[par], bias_tile[:, :].unsqueeze(1).to_broadcast([P, TB, D]),
                                        ALU.add).then_inc(s["xb_made"], 1)
                pool.wait_ge(s["xn_made"], n + 1)
                dst = xn[:, n * TB:(n + 1) * TB, :] if isinstance(n, int) else xn[:, bass.ds(n * TB, TB), :]
                nc.gpsimd.tensor_copy(dst, xnr[par]).then_inc(s["xn_kept"], 1)

            def normalise(n, par):
                pool.wait_ge(s["s_summed"], n + 1)
                e = E[par].rearrange("p g k c -> p (g k) c")
                r = srec[:, :, :].rearrange("p g k -> p (g k)").unsqueeze(2).to_broadcast([P, 32, WIN])
                nc.gpsimd.tensor_tensor(e, e, r, ALU.mult).then_inc(s["p_ready"], 1)

            pool.wait_ge(s["consts_in"], 32)
            rstd_of(0)
            pool.wait_ge(s["bias_ready"], 1)
            rows_of(0, 0, False)
            rstd_of(1)
            rows_of(1, 1, False)
            pool.wait_ge(s["shared_max"], 2)
            nc.gpsimd.partition_all_reduce(pw[:, 5:8], mx[:, 5:8], P, RMAX).then_inc(s["shared_all_max"], 1)
            normalise(0, 0)

            def turn(n, par):
                rstd_of(n)
                rows_of(n, par, True)
                normalise(n - 1, 1 - par)

            pairs(pool, turn, 2, B)
            normalise(B - 1, 1)

            for par in range(2):
                pool.wait_ge(s[f"y1_stored{par}"], 16 * (B // 2))
            pool.wait_ge(s["out0_ready"], 1)
            pool.dma_start(y1_dram.rearrange("(b l) d -> b l d", l=L)[:, 0, :], out0[:, :],
                           accum_op=ALU.add).then_inc(s["out0_added"], 16)

            pool.wait_ge(s["xs_zeroed"], 16)
            pool.wait_ge(s["slots_ready"], 1)
            for t in range(NTOK):
                for k in range(2):
                    pool.indirect_dma_start(out=xs_dram, out_offset=bass.IndirectOffsetOnAxis(ap=slots[:, k, t:t + 1], axis=0),
                                            in_=xn[:, t, :], in_offset=None).then_inc(s["scattered"], 16)

            pool.wait_ge(s["routed_max"], 1)
            nc.gpsimd.partition_all_reduce(pw[:, 8:11], mx[:, 8:11], P, RMAX).then_inc(s["routed_all_max"], 1)

            for par in range(2):
                pool.wait_ge(s[f"ys_stored{par}"], 16 * (NT // 2))
            for t in range(NTOK):
                par = t % 2
                if t >= 2:
                    pool.wait_ge(s["mixed"], t - 1)
                for k in range(2):
                    pool.indirect_dma_start(out=g1[k][par][:, :], out_offset=None, in_=ys_dram,
                                            in_offset=bass.IndirectOffsetOnAxis(ap=slots[:, k, t:t + 1], axis=0)).then_inc(s[f"pick_in{par}"], 16)

        @block.scalar
        def _(act):
            ev = nc.scalar

            def split_high(dst, src, col, name, inc=True):
                i = ev.activation(dst, src, ACT.Identity, scale=scl[:, col:col + 1])
                if inc:
                    i.then_inc(s[name], 1)

            act.wait_ge(s["attn_w_in"], 80)
            act.wait_ge(s["scale_ready"], 1)
            for i in range(4):
                split_high(wa[0][:, i], wa_raw[:, i], i, "attn_high")
            split_high(wr[0][:, :, :], wr_raw, 4, "attn_high")

            def part1(n, par):
                pos = place(1, n)
                nsl = (lambda: slice(XPAD + n * L, XPAD + (n + 1) * L)) if isinstance(n, int) else (lambda: bass.ds(n * L + XPAD, L))
                for k in range(KD):
                    act.wait_ge(s["unit_full"], pos + U_XT + k + 1)
                    ev.activation(xT[0][:, k, nsl()], ps[:, 5 + (U_XT + k) % RING, :], ACT.Identity).then_inc(s["xT_high"], 1)
                act.wait_ge(s["unit_full"], pos + U_R + 1)
                lsl = slice(n * TB, (n + 1) * TB) if isinstance(n, int) else bass.ds(n * TB, TB)
                ev.activation(logits[:, lsl, :], T(U_R)[:, 0:TB * NE].rearrange("p (t e) -> p t e", e=NE),
                              ACT.Identity, scale=inv[:, 4:5]).then_inc(s["act_empty"], 1)
                act.wait_ge(s["unit_full"], pos + U_Q + 1)
                for o in range(2):
                    q = ev.activation(QT[o][:, 0, :], T(U_Q)[:, 0:TB * (WIN + 1)], ACT.Identity,
                                      bias=bqp[:, o, 0:1], scale=der[:, D_QE + o:D_QE + o + 1])
                q.then_inc(s["act_empty"], 1)
                act.wait_ge(s["unit_full"], pos + U_K + 1)
                ev.activation(KT[:, 0, :], T(U_K), ACT.Identity, bias=bk[:, 0:1], scale=inv[:, 1:2]).then_inc(s["act_empty"], 1)

            def soft(n, par):
                act.wait_ge(s["s_taken"], n + 1)
                e = E[par].rearrange("p g k c -> p (g k c)")
                ev.activation(e, e, ACT.Exp).then_inc(s["s_exp"], 1)
                act.wait_ge(s["g_max"], n + 1)
                ev.activation(gs[0:NH, :], G[0:NH, :], ACT.Exp, bias=gmx[:, :], accum_out=gsum[:, :]).then_inc(s["g_exp"], 1)

            def part2(n, par):
                pos = place(2, n)
                act.wait_ge(s["unit_full"], pos + U_GT + 1)
                ev.activation(gp, T(U_GT)[:, 0:TB * NH].rearrange("p (t e) -> p t e", e=NH), ACT.Identity).then_inc(s["act_empty"], 1)
                act.wait_ge(s["unit_full"], pos + U_U + 1)
                usl = slice(n, n + 1) if isinstance(n, int) else bass.ds(n, 1)
                ev.activation(uT[0][:, :, usl, :].rearrange("p k o e -> p k (o e)"),
                              T(U_U)[:, 0:KD * NH].rearrange("p (k e) -> p k e", e=NH), ACT.Identity).then_inc(s["u_high"], 1)
                for j in (0, 2):
                    act.wait_ge(s["unit_full"], pos + U_PT + j + 1)
                    ev.activation(PT[:, j], T(U_PT + j).rearrange("p (g q) -> p g q", g=4), ACT.Identity).then_inc(s["act_empty"], 1)
                act.wait_ge(s["unit_full"], pos + U_AV + 1)
                ev.activation(cT[0][:, :, :, 1:1 + WIN], T(U_AV).rearrange("p (m w q) -> p m w q", m=KD, w=TB),
                              ACT.Identity).then_inc(s["ctx_high"], 1)

            act.wait_ge(s["setup"], 1)
            part1(0, 0)
            act.wait_ge(s["shared_w_in"], 48)
            act.wait_ge(s["scale_ready"], 2)
            for i in range(2):
                split_high(w12[0][:, i], w12_raw[:, i], 5 + i, "shared_high")
            split_high(w3[0][:, :, :], w3_raw, 7, "shared_high")
            soft(0, 0)
            part1(1, 1)
            part2(0, 0)
            soft(1, 1)

            def turn(n, par):
                part1(n, par)
                part2(n - 1, 1 - par)
                soft(n, par)

            act.wait_ge(s["pads_ready"], 1)
            pairs(act, turn, 2, B)
            part2(B - 1, 1)

            ev.activation(sc_, logits[:, :, :], ACT.Sigmoid).then_inc(s["scores_ready"], 1)

            def chunk(b, c):
                n, q = b * SC + c, c % 2
                act.wait_ge(s["a_full"], n + 1)
                ev.activation(s_silu[q], ps[:, 2 * q, :], ACT.Silu, scale=inv[:, 5:6]).then_inc(s["silu_done"], 1)
                act.wait_ge(s["h_done"], n + 3)
                ev.activation(s_hh[0][q], s_h[q], ACT.Identity).then_inc(s["hh_high"], 1)

            def shared(b0, b1):
                with act.Fori(b0, b1) as b:
                    for c in range(SC):
                        chunk(b, c)

            act.wait_ge(s["shared_low"], 1)
            shared(0, B_FIRST)
            act.wait_ge(s["scale_ready"], 3)
            for e in range(NE):
                if e >= 1:
                    act.wait_ge(s["routed_low"], e)
                raw = arena[:, (e + 1) * EXPERT:(e + 2) * EXPERT]
                hi = ar16[:, 2 * e * EXPERT:(2 * e + 1) * EXPERT]
                for i in range(2):
                    ev.activation(hi[:, 0:2 * KD * RH].rearrange("p (k i h) -> p k i h", k=KD, i=2)[:, :, i],
                                  raw[:, 0:2 * KD * RH].rearrange("p (k i h) -> p k i h", k=KD, i=2)[:, :, i],
                                  ACT.Identity, scale=scl[:, 8 + i:9 + i])
                ev.activation(hi[:, 2 * KD * RH:], raw[:, 2 * KD * RH:], ACT.Identity, scale=scl[:, 10:11]).then_inc(s["routed_high"], 1)

            def gated(t, par):
                act.wait_ge(s["ab_full"], t + 1)
                ev.activation(r_silu[par], ps[:, par, 0:RH], ACT.Silu, scale=inv[:, 8:9]).then_inc(s["r_silu_done"], 1)

            def x_high(t, par):
                act.wait_ge(s["rx_full"], t + 1)
                ev.activation(r_x[0][par], ps[:, 2 + par, 0:D], ACT.Identity).then_inc(s["rx_high"], 1)

            def h_high(t, par):
                act.wait_ge(s["rh_full"], t + 1)
                ev.activation(r_hh[0][par], ps[:, 4 + par, 0:RH], ACT.Identity).then_inc(s["rh_high"], 1)

            def y_out(t, par, stored):
                act.wait_ge(s["ry_full"], t + 1)
                if stored:
                    act.wait_ge(s[f"ys_stored{par}"], (t + (-par)) * 8)
                ev.activation(ys[par], ps[:, 6 + par, 0:D], ACT.Identity, scale=der[:, D_RY:D_RY + 1]).then_inc(s["ry_done"], 1)

            x_high(0, 0)
            for t in range(4):
                gated(t, t % 2)
                x_high(t + 1, (t + 1) % 2)
                if t >= 1:
                    h_high(t - 1, (t - 1) % 2)
                if t >= 2:
                    y_out(t - 2, t % 2, False)

            def routed(t, par):
                gated(t, par)
                x_high(t + 1, 1 - par)
                h_high(t - 1, 1 - par)
                y_out(t - 2, par, True)

            pairs(act, routed, 4, NT - 2)
            routed(NT - 2, 0)
            gated(NT - 1, 1)
            h_high(NT - 2, 0)
            y_out(NT - 3, 1, True)
            h_high(NT - 1, 1)
            y_out(NT - 2, 0, True)
            y_out(NT - 1, 1, True)
            for par in range(2):
                act.wait_ge(s[f"ys_stored{par}"], 16 * (NT // 2))
            shared(B_FIRST, B)

        @block.vector
        def _(dve):
            v = nc.vector
            steps = [0]

            def link(i):
                steps[0] += 1
                i.then_inc(s["vector_step"], 1)
                dve.wait_ge(s["vector_step"], steps[0])

            marks = [0]

            def signal(name, n=1):
                marks[0] += 1
                v.memset(tick[:, marks[0]:marks[0] + 1], 0.0).then_inc(s[name], n)

            def scales(lo, hi, reduced, count):
                dve.wait_ge(s[reduced], 1)
                link(v.tensor_scalar(pw[:, lo:hi], pw[:, lo:hi], 2.0 ** -40, None, ALU.max))
                link(v.tensor_scalar(pw[:, lo:hi].bitcast(I32), pw[:, lo:hi].bitcast(I32), 0x7F800000, None, ALU.bitwise_and))
                link(v.tensor_scalar(inv[:, lo:hi], pw[:, lo:hi], 1.0 / TOP, None, ALU.mult))
                link(v.reciprocal(scl[:, lo:hi], inv[:, lo:hi]))

            def ln(n, par, kept):
                x = xr[par]
                dve.wait_ge(s[f"x_in{par}"], (n + (-par)) * 8 + 16)
                for t in range(TB):
                    i = v.bn_stats(st[:, t, :], x[:, t, :])
                i.then_inc(s["ln_stats"], 1)
                dve.wait_ge(s["ln_stats"], n + 1)
                v.memset(tick[:, 0:1], 0.0)
                for t in range(TB):
                    i = v.bn_aggr(mv[:, t, :], st[:, t, :])
                i.then_inc(s["ln_mv"], 1)
                dve.wait_ge(s["ln_mv"], n + 1)
                v.tensor_scalar(ve[:, :], mv[:, :, 1], EPS, None, ALU.add).then_inc(s["ln_var"], 1)
                dve.wait_ge(s["ln_rstd"], n + 1)
                v.scalar_tensor_tensor(out=nmr[:, :], in0=mv[:, :, 0], scalar=-1.0, in1=rstd[:, :],
                                       op0=ALU.mult, op1=ALU.mult).then_inc(s["ln_shift"], 1)
                dve.wait_ge(s["ln_shift"], n + 1)
                if kept:
                    dve.wait_ge(s["xn_kept"], n - 1)
                for t in range(TB):
                    i = v.tensor_scalar(xnr[par][:, t, :], x[:, t, :], rstd[:, t:t + 1], nmr[:, t:t + 1], ALU.mult, ALU.add)
                i.then_inc(s["xn_made"], 1)

            def part1(n, par):
                pos = place(1, n)
                nsl = (lambda: slice(XPAD + n * L, XPAD + (n + 1) * L)) if isinstance(n, int) else (lambda: bass.ds(n * L + XPAD, L))
                for k in range(KD):
                    dve.wait_ge(s["xT_high"], n * 2 + k + 1)
                    v.tensor_tensor(xT[1][:, k, nsl()], T(U_XT + k), xT[0][:, k, nsl()], ALU.subtract).then_inc(s["dve_empty"], 1)
                dve.wait_ge(s["unit_full"], pos + U_Q + 1 + 1)
                for o in range(2):
                    i = v.tensor_scalar(QT[o][:, 1, :], T(U_Q + 1)[:, 0:TB * (WIN + 1)], der[:, D_QE + o:D_QE + o + 1],
                                        bqp[:, o, 1:2], ALU.mult, ALU.add)
                i.then_inc(s["dve_empty"], 1)
                dve.wait_ge(s["act_empty"], emptied("A", 1, n, U_Q))
                dve.wait_ge(s["dve_empty"], emptied("D", 1, n, U_Q + 1))
                hm = cf[:, C_HM:C_HM + KD * NH].rearrange("p (m h) -> p m h", h=NH)
                for m in range(KD):
                    i = v.tensor_scalar(q0[:, m, :], hm[:, m, :], QT[0][:, m, 0:1], None, ALU.mult)
                i.then_inc(s["q0_half"], 1)
                dve.wait_ge(s["q0_half"], n + 1)
                for m in range(KD):
                    i = v.scalar_tensor_tensor(out=q0[:, m, :], in0=hm[:, m, :], scalar=QT[1][:, m, 0:1], in1=q0[:, m, :],
                                               op0=ALU.mult, op1=ALU.add)
                i.then_inc(s["q0_ready"], 1)
                dve.wait_ge(s["unit_full"], pos + U_K + 1 + 1)
                v.tensor_scalar(KT[:, 1, :], T(U_K + 1), inv[:, 1:2], bk[:, 1:2], ALU.mult, ALU.add).then_inc(s["dve_empty"], 1)
                for c in range(2):
                    dve.wait_ge(s["unit_full"], pos + U_V + c + 1)
                    src = T(U_V + c).rearrange("p (w o j d) -> p w o j d", w=2, j=8, o=2)
                    for o in range(2):
                        for w in range(2):
                            i = v.tensor_copy(VB[par][64 * o:64 * o + 64, 2 * c + w, :, HD * o:HD * o + HD],
                                              src[64 * o:64 * o + 64, w, o, :, :])
                    i.then_inc(s["dve_empty"], 1)

            def soft(n, par):
                e = E[par].rearrange("p g k c -> p (g k) c")
                sv = S.rearrange("p g (k c) -> p (g k) c", c=WIN)
                flat = "p g k -> p (g k)"
                dve.wait_ge(s["s_full"], n + 1)
                v.tensor_reduce(smx[:, :, :].rearrange(flat), sv, AX, ALU.max).then_inc(s["s_max"], 1)
                dve.wait_ge(s["s_max"], n + 1)
                v.tensor_tensor(e, sv, smx[:, :, :].rearrange(flat).unsqueeze(2).to_broadcast([P, 32, WIN]),
                                ALU.subtract).then_inc(s["s_taken"], 1)
                dve.wait_ge(s["g_full"], n + 1)
                v.tensor_reduce(gmx[:, :], G[0:NH, :], AX, ALU.max, negate=True).then_inc(s["g_max"], 1)
                dve.wait_ge(s["s_exp"], n + 1)
                v.tensor_reduce(ssum[:, :, :].rearrange(flat), e, AX, ALU.add).then_inc(s["soft_sum"], 1)
                dve.wait_ge(s["soft_sum"], n + 1)
                v.reciprocal(srec[:, :, :], ssum[:, :, :]).then_inc(s["s_summed"], 1)
                dve.wait_ge(s["g_exp"], n + 1)
                v.reciprocal(grec[:, :], gsum[:, :]).then_inc(s["g_rec"], 1)
                dve.wait_ge(s["g_rec"], n + 1)
                v.tensor_scalar(gs[0:NH, :], gs[0:NH, :], grec[:, :], None, ALU.mult).then_inc(s["g_ready"], 1)

            def part2(n, par, between=None):
                pos = place(2, n)
                dve.wait_ge(s["u_high"], n + 1)
                usl = slice(n, n + 1) if isinstance(n, int) else bass.ds(n, 1)
                v.tensor_tensor(uT[1][:, :, usl, :].rearrange("p k o e -> p k (o e)"),
                                T(U_U)[:, 0:KD * NH].rearrange("p (k e) -> p k e", e=NH),
                                uT[0][:, :, usl, :].rearrange("p k o e -> p k (o e)"), ALU.subtract).then_inc(s["dve_empty"], 1)
                if between is not None:
                    between()
                for j in (1, 3):
                    dve.wait_ge(s["unit_full"], pos + U_PT + j + 1)
                    v.tensor_copy(PT[:, j], T(U_PT + j).rearrange("p (g q) -> p g q", g=4)).then_inc(s["dve_empty"], 1)
                dve.wait_ge(s["ctx_high"], n + 1)
                src = T(U_AV).rearrange("p (m w q) -> p m w q", m=KD, w=TB)
                for m in range(KD):
                    i = v.tensor_tensor(cT[1][:, m, :, 1:1 + WIN], src[:, m], cT[0][:, m, :, 1:1 + WIN], ALU.subtract)
                i.then_inc(s["dve_empty"], 1)
                for c in range(2):
                    dve.wait_ge(s["unit_full"], pos + U_WO + c + 1)
                    dve.wait_ge(s["xb_made"], n + 1)
                    dst = xb[par][:, 2 * c:2 * c + 2, :].rearrange("p t d -> p (t d)")
                    i = v.scalar_tensor_tensor(out=dst, in0=T(U_WO + c), scalar=der[:, D_O:D_O + 1], in1=dst,
                                               op0=ALU.mult, op1=ALU.add)
                    i.then_inc(s["dve_empty"], 1)

            for name in ("h_done", "y_done"):
                signal(name, 2)

            dve.wait_ge(s["attn_w_in"], 80)
            v.tensor_reduce(mx[:, 0:4], wa_raw.rearrange("p i k d -> p i (k d)"), AX, ALU.max,
                            apply_absolute_value=True).then_inc(s["attn_max"], 1)
            v.tensor_reduce(mx[:, 4:5], wr_raw.rearrange("p k e -> p (k e)"), AX, ALU.max,
                            apply_absolute_value=True).then_inc(s["attn_max"], 1)
            scales(0, 5, "attn_all_max", 1)
            signal("scale_ready")
            dve.wait_ge(s["consts_in"], 32)
            dve.wait_ge(s["bias_in"], 48)
            for o, c in ((0, C_EVEN), (1, C_ODD)):
                link(v.tensor_scalar(der[:, D_QE + o:D_QE + o + 1], cf[:, c:c + 1], inv[:, 0:1], HD ** -0.5, ALU.mult, ALU.mult))
                link(v.tensor_scalar(bqp[:, o, :], bq[:, :], cf[:, c:c + 1], HD ** -0.5, ALU.mult, ALU.mult))
            link(v.tensor_tensor(der[:, D_O:D_O + 1], inv[:, 2:3], inv[:, 3:4], ALU.mult))
            for m in range(KD):
                link(v.tensor_scalar(bvm[:, m, :], cf[:, C_TOK:C_TOK + P], bv[:, m:m + 1], None, ALU.mult))
            signal("setup")
            dve.wait_ge(s["bias_psum"], 1)
            link(v.tensor_tensor(bias_tile[:, :], ps[:, 4, 0:D], bias_tile[:, :], ALU.add))
            v.tensor_copy(bv_out[:, :], ps[0:B, 4, D:2 * D]).then_inc(s["bias_ready"], 1)
            ln(0, 0, False)
            for i in range(4):
                dve.wait_ge(s["attn_high"], i + 1)
                v.scalar_tensor_tensor(out=wa[1][:, i].rearrange("p k d -> p (k d)"), in0=wa_raw[:, i].rearrange("p k d -> p (k d)"),
                                       scalar=scl[:, i:i + 1], in1=wa[0][:, i].rearrange("p k d -> p (k d)"),
                                       op0=ALU.mult, op1=ALU.subtract)
            dve.wait_ge(s["attn_high"], 5)
            v.scalar_tensor_tensor(out=wr[1][:, :, :], in0=wr_raw, scalar=scl[:, 4:5], in1=wr[0][:, :, :],
                                   op0=ALU.mult, op1=ALU.subtract).then_inc(s["attn_low"], 1)
            part1(0, 0)
            ln(1, 1, False)
            dve.wait_ge(s["shared_w_in"], 48)
            v.tensor_reduce(mx[:, 5:7], w12_raw.rearrange("p i k h -> p i (k h)"), AX, ALU.max,
                            apply_absolute_value=True).then_inc(s["shared_max"], 1)
            v.tensor_reduce(mx[:, 7:8], w3_raw.rearrange("p c d -> p (c d)"), AX, ALU.max,
                            apply_absolute_value=True).then_inc(s["shared_max"], 1)
            scales(5, 8, "shared_all_max", 1)
            link(v.tensor_scalar(der[:, D_HS:D_HS + 1], scl[:, 5:6], 2.0 ** -15, None, ALU.mult))
            link(v.tensor_tensor(der[:, D_Y:D_Y + 1], inv[:, 5:6], inv[:, 6:7], ALU.mult))
            link(v.tensor_scalar(der[:, D_Y:D_Y + 1], der[:, D_Y:D_Y + 1], inv[:, 7:8], 2.0 ** 15, ALU.mult, ALU.mult))
            signal("scale_ready")
            for i in range(2):
                dve.wait_ge(s["shared_high"], i + 1)
                v.scalar_tensor_tensor(out=w12[1][:, i].rearrange("p k d -> p (k d)"), in0=w12_raw[:, i].rearrange("p k d -> p (k d)"),
                                       scalar=scl[:, 5 + i:6 + i], in1=w12[0][:, i].rearrange("p k d -> p (k d)"),
                                       op0=ALU.mult, op1=ALU.subtract)
            dve.wait_ge(s["shared_high"], 3)
            v.scalar_tensor_tensor(out=w3[1][:, :, :], in0=w3_raw, scalar=scl[:, 7:8], in1=w3[0][:, :, :],
                                   op0=ALU.mult, op1=ALU.subtract).then_inc(s["shared_low"], 1)
            soft(0, 0)
            part1(1, 1)
            dve.wait_ge(s["pads_ready"], 1)
            part2(0, 0, lambda: ln(2, 0, True))
            soft(1, 1)

            def turn(n, par):
                part1(n, par)
                part2(n - 1, 1 - par, lambda: ln(n + 1, 1 - par, True))
                soft(n, par)

            pairs(dve, turn, 2, B - 2)
            turn(B - 2, 0)
            part1(B - 1, 1)
            part2(B - 2, 0)
            soft(B - 1, 1)
            part2(B - 1, 1)

            dve.wait_ge(s["c0_full"], 1)
            for m in range(KD):
                src = ps[:, 6, m * P:(m + 1) * P].rearrange("p (b h) -> p b h", h=NH)
                link(v.tensor_tensor(c0m[:, :, :], src, cf[:, C_HM + m * NH:C_HM + (m + 1) * NH].unsqueeze(1).to_broadcast([P, B, NH]), ALU.mult))
                link(v.tensor_reduce(c0f[:, m, :], c0m[:, :, :], AX, ALU.add))
            link(v.tensor_copy(c0[0][:, :, :], c0f[:, :, :]))
            v.tensor_tensor(c0[1][:, :, :], c0f[:, :, :], c0[0][:, :, :], ALU.subtract).then_inc(s["c0_ready"], 1)
            dve.wait_ge(s["out0_full"], 1)
            v.scalar_tensor_tensor(out=out0[:, :], in0=ps[0:B, 7, 0:D], scalar=der[0:B, D_O:D_O + 1], in1=bv_out[:, :],
                                   op0=ALU.mult, op1=ALU.add).then_inc(s["out0_ready"], 1)

            dve.wait_ge(s["scores_ready"], 1)
            link(v.tensor_tensor(sel, sc_, eb[:, :].unsqueeze(1).to_broadcast([P, NTOK, NE]), ALU.add))
            for t in range(NTOK):
                i = v.max(mx8[:, t, :], sel[:, t, :])
            link(i)
            for t in range(NTOK):
                i = v.max_index(ix8[:, t, :], mx8[:, t, :], sel[:, t, :])
            link(i)
            link(v.tensor_copy(ixf[:, :, :], ix8[:, :, 0:2]))
            ie = cf[:, C_IE:C_IE + NE].unsqueeze(1).to_broadcast([P, NTOK, NE])
            for k, oh in ((0, oh1), (1, oh2)):
                link(v.tensor_tensor(oh, ie, ixf[:, :, k:k + 1].to_broadcast([P, NTOK, NE]), ALU.is_equal))
            v.tensor_tensor(ohm[:, :, :], oh1, oh2, ALU.add).then_inc(s["chosen_ready"], 1)
            for k, oh in ((0, oh1), (1, oh2)):
                link(v.tensor_tensor(tmp, oh, sc_, ALU.mult))
                link(v.tensor_reduce(gate[:, k, :], tmp, AX, ALU.add))
            dve.wait_ge(s["prefix_full"], 2)
            before = ps[:, 6, :].rearrange("p (t e) -> p t e", e=NE)
            total = ps[:, 7, :].rearrange("p (t e) -> p t e", e=NE)
            link(v.tensor_copy(cumA, total))
            src, dst, d = cumA, cumB, 1
            while d < NTOK:
                link(v.tensor_copy(dst[:, 0:d, :], src[:, 0:d, :]))
                link(v.tensor_tensor(dst[:, d:, :], src[:, d:, :], src[:, 0:NTOK - d, :], ALU.add))
                src, dst, d = dst, src, 2 * d
            need, ta, tb_, t3, first = (x[:, :] for x in tl)
            link(v.tensor_scalar(need, src[:, NTOK - 1, :], P - 1.0, 1.0 / P, ALU.add, ALU.mult))
            link(v.tensor_scalar(need, need, -0.5 + 0.5 / P, 2.0 ** 23, ALU.add, ALU.add))
            link(v.tensor_scalar(need, need, -(2.0 ** 23), None, ALU.add))
            link(v.tensor_copy(ta, need))
            s1, s2, d = ta, tb_, 1
            while d < NE:
                link(v.tensor_copy(s2[:, 0:d], s1[:, 0:d]))
                link(v.tensor_tensor(s2[:, d:], s1[:, d:], s1[:, 0:NE - d], ALU.add))
                s1, s2, d = s2, s1, 2 * d
            link(v.tensor_tensor(first, s1, need, ALU.subtract))
            link(v.tensor_scalar(first, first, float(P), None, ALU.mult))
            link(v.tensor_tensor(posn, src, total, ALU.subtract))
            link(v.tensor_tensor(posn, before, posn, ALU.add))
            link(v.tensor_tensor(posn, posn, first.unsqueeze(1).to_broadcast([P, NTOK, NE]), ALU.add))
            for k, oh in ((0, oh1), (1, oh2)):
                link(v.tensor_tensor(tmp, oh, posn, ALU.mult))
                link(v.tensor_reduce(slf[:, k, :], tmp, AX, ALU.add))
            v.tensor_copy(slots[:, :, :], slf[:, :, :]).then_inc(s["slots_ready"], 1)
            link(v.tensor_tensor(ecount[:, :, :], s1[0:1].unsqueeze(1).to_broadcast([1, NT, NE]),
                                 cf[0:1, C_IS:C_IS + NT].unsqueeze(2).to_broadcast([1, NT, NE]), ALU.is_le))
            link(v.tensor_reduce(ef[:, :], ecount[:, :, :], AX, ALU.add))
            link(v.tensor_scalar(ef[:, :], ef[:, :], NE - 1.0, 2.0 * EXPERT, ALU.min, ALU.mult))
            v.tensor_copy(etab[:, :], ef[:, :]).then_inc(s["table_ready"], 1)
            signal("route")

            def chunk(b, c):
                n, q = b * SC + c, c % 2
                dve.wait_ge(s["silu_done"], n + 1)
                v.scalar_tensor_tensor(out=s_h[q], in0=ps[:, 2 * q + 1, :], scalar=der[:, D_HS:D_HS + 1], in1=s_silu[q],
                                       op0=ALU.mult, op1=ALU.mult).then_inc(s["h_done"], 1)
                dve.wait_ge(s["hh_high"], n + 1)
                v.tensor_tensor(s_hh[1][q], s_h[q], s_hh[0][q], ALU.subtract).then_inc(s["hh_low"], 1)

            def shared(b0, b1):
                def batch(b, par):
                    for c in range(SC):
                        chunk(b, c)
                    dve.wait_ge(s["y_full"], b + 1)
                    dve.wait_ge(s[f"y_in{par}"], (b + (-par)) * 8 + 16)
                    y = s_y[par].rearrange("p t d -> p (t d)")
                    v.scalar_tensor_tensor(out=y, in0=ps[:, 4 + 2 * par:6 + 2 * par, :].rearrange("p a d -> p (a d)"),
                                           scalar=der[:, D_Y:D_Y + 1], in1=y, op0=ALU.mult, op1=ALU.add).then_inc(s["y_done"], 1)

                pairs(dve, batch, b0, b1)

            shared(0, B_FIRST)

            for e in range(NE):
                raw = arena[:, (e + 1) * EXPERT:(e + 2) * EXPERT]
                dve.wait_ge(s["raw_in"], 48 * NE)
                r12 = raw[:, 0:2 * KD * RH].rearrange("p (k i h) -> p i k h", k=KD, i=2)
                v.tensor_reduce(rmx[:, 0:2, e], r12, mybir.AxisListType.XY, ALU.max, apply_absolute_value=True).then_inc(s["routed_each"], 1)
                v.tensor_reduce(rmx[:, 2:3, e], raw[:, 2 * KD * RH:], AX, ALU.max, apply_absolute_value=True).then_inc(s["routed_each"], 1)
            dve.wait_ge(s["routed_each"], 2 * NE)
            v.tensor_reduce(mx[:, 8:11], rmx[:, :, :], AX, ALU.max).then_inc(s["routed_max"], 1)
            scales(8, 11, "routed_all_max", 1)
            link(v.tensor_scalar(der[:, D_RHS:D_RHS + 1], scl[:, 8:9], 2.0 ** -15, None, ALU.mult))
            link(v.tensor_tensor(der[:, D_RY:D_RY + 1], inv[:, 8:9], inv[:, 9:10], ALU.mult))
            link(v.tensor_scalar(der[:, D_RY:D_RY + 1], der[:, D_RY:D_RY + 1], inv[:, 10:11], 2.0 ** 15, ALU.mult, ALU.mult))
            signal("scale_ready")
            for e in range(NE):
                dve.wait_ge(s["routed_high"], e + 1)
                raw = arena[:, (e + 1) * EXPERT:(e + 2) * EXPERT]
                hi = ar16[:, 2 * e * EXPERT:(2 * e + 1) * EXPERT]
                lo = ar16[:, (2 * e + 1) * EXPERT:(2 * e + 2) * EXPERT]
                pat = "p (k i h) -> p k i h"
                for i in range(2):
                    part = [z[:, 0:2 * KD * RH].rearrange(pat, k=KD, i=2)[:, :, i] for z in (lo, raw, hi)]
                    v.scalar_tensor_tensor(out=part[0], in0=part[1], scalar=scl[:, 8 + i:9 + i], in1=part[2],
                                           op0=ALU.mult, op1=ALU.subtract)
                v.scalar_tensor_tensor(out=lo[:, 2 * KD * RH:], in0=raw[:, 2 * KD * RH:], scalar=scl[:, 10:11],
                                       in1=hi[:, 2 * KD * RH:], op0=ALU.mult, op1=ALU.subtract).then_inc(s["routed_low"], 1)

            def gated(t, par):
                dve.wait_ge(s["r_silu_done"], t + 1)
                v.scalar_tensor_tensor(out=r_h[par], in0=ps[:, par, RH:2 * RH], scalar=der[:, D_RHS:D_RHS + 1], in1=r_silu[par],
                                       op0=ALU.mult, op1=ALU.mult).then_inc(s["r_h_done"], 1)

            def x_low(t, par):
                dve.wait_ge(s["rx_high"], t + 1)
                v.tensor_tensor(r_x[1][par], ps[:, 2 + par, 0:D], r_x[0][par], ALU.subtract).then_inc(s["rx_low"], 1)

            def h_low(t, par):
                dve.wait_ge(s["rh_high"], t + 1)
                v.tensor_tensor(r_hh[1][par], ps[:, 4 + par, 0:RH], r_hh[0][par], ALU.subtract).then_inc(s["rh_low"], 1)

            x_low(0, 0)
            gated(0, 0)
            x_low(1, 1)

            def routed(t, par):
                gated(t, par)
                x_low(t + 1, 1 - par)
                h_low(t - 1, 1 - par)

            routed(1, 1)
            pairs(dve, routed, 2, NT - 2)
            routed(NT - 2, 0)
            gated(NT - 1, 1)
            h_low(NT - 2, 0)
            h_low(NT - 1, 1)
            shared(B_FIRST, B)

            for t in range(NTOK):
                par = t % 2
                dve.wait_ge(s[f"base_in{par}"], 16 * (t // 2 + 1))
                dve.wait_ge(s[f"pick_in{par}"], 32 * (t // 2 + 1))
                v.scalar_tensor_tensor(out=c_y[par][:, :], in0=g1[0][par][:, :], scalar=gate[:, 0, t:t + 1], in1=c_y[par][:, :],
                                       op0=ALU.mult, op1=ALU.add).then_inc(s["one_added"], 1)
                dve.wait_ge(s["one_added"], t + 1)
                v.scalar_tensor_tensor(out=c_y[par][:, :], in0=g1[1][par][:, :], scalar=gate[:, 1, t:t + 1], in1=c_y[par][:, :],
                                       op0=ALU.mult, op1=ALU.add).then_inc(s["mixed"], 1)

        @block.tensor
        def _(pe):
            mm = nc.tensor.matmul
            pe.wait_ge(s["attn_w_in"], 80)
            pe.wait_ge(s["setup"], 1)
            for m in range(KD):
                mm(ps[:, 4, 0:D], bvm[:, m, :], wa_raw[:, 3, m, :], start=(m == 0), stop=(m == KD - 1))
            for m in range(KD):
                i = mm(ps[0:B, 4, D:2 * D], bvm[:, m, 1:1 + B], wa_raw[:, 3, m, :], start=(m == 0), stop=(m == KD - 1))
            i.then_inc(s["bias_psum"], 1)

            def claim(part, n, u):
                kinds = PART1 if part == 1 else PART2
                if u >= RING:
                    who = kinds[u - RING]
                    pe.wait_ge(s["act_empty" if who == "A" else "dve_empty"], emptied(who, part, n, u - RING))
                elif not (part == 1 and isinstance(n, int) and n == 0):
                    pe.wait_ge(s["dve_empty"], emptied_before("D", part, n) - (RING - 1 - u))

            def part1(n, par):
                nsl = slice(XPAD + n * L, XPAD + (n + 1) * L) if isinstance(n, int) else bass.ds(n * L + XPAD, L)
                xk = lambda x, k: xT[x][:, k, nsl]
                pe.wait_ge(s["xn_made"], n + 1)
                for k in range(KD):
                    claim(1, n, U_XT + k)
                    for t in range(TB):
                        i = nc.tensor.transpose(T(U_XT + k)[:, t * P:(t + 1) * P], xnr[par][:, t, k * P:(k + 1) * P], ident)
                    i.then_inc(s["unit_full"], 1)
                claim(1, n, U_R)
                pe.wait_ge(s["dve_empty"], emptied("D", 1, n, U_XT + 1))
                for t in range(TB):
                    for j, (x, w) in enumerate(((0, 0), (0, 1), (1, 0))):
                        for k in range(KD):
                            tsl = slice(XPAD + n * L + t * P, XPAD + n * L + (t + 1) * P) if isinstance(n, int) else bass.ds(n * L + (XPAD + t * P), P)
                            i = mm(T(U_R)[:, t * NE:(t + 1) * NE], xT[x][:, k, tsl], wr[w][:, k, :],
                                   start=(j == 0 and k == 0), stop=(j == 2 and k == KD - 1))
                i.then_inc(s["unit_full"], 1)
                for m in range(KD):
                    claim(1, n, U_Q + m)
                    for j, (w, x) in enumerate(SPLIT):
                        for k in range(KD):
                            rhs = xk(x, k).rearrange("p (w c) -> p w c", w=TB)[:, :, 0:WIN + 1]
                            i = mm(T(U_Q + m)[:, 0:TB * (WIN + 1)].rearrange("p (w c) -> p w c", w=TB),
                                   wa[w][:, 0, k, m * P:(m + 1) * P], rhs, start=(j == 0 and k == 0), stop=(j == 2 and k == KD - 1))
                    i.then_inc(s["unit_full"], 1)
                for m in range(KD):
                    claim(1, n, U_K + m)
                    for j, (w, x) in enumerate(SPLIT):
                        for k in range(KD):
                            i = mm(T(U_K + m), wa[w][:, 1, k, m * P:(m + 1) * P], xk(x, k),
                                   start=(j == 0 and k == 0), stop=(j == 2 and k == KD - 1))
                    i.then_inc(s["unit_full"], 1)
                for c in range(2):
                    claim(1, n, U_V + c)
                    for w2 in range(2):
                        o = (2 * c + w2) * STRIDE + 1
                        for par2 in range(2):
                            at_ = XPAD + o - WIN * par2
                            rows = P - 1 + par2
                            wsl = slice(n * L + at_, n * L + at_ + rows) if isinstance(n, int) else bass.ds(n * L + at_, rows)
                            dst = T(U_V + c)[0:rows, w2 * D + par2 * P:w2 * D + (par2 + 1) * P].rearrange("p (j d) -> p j d", d=HD)
                            for j, (w, x) in enumerate(SPLIT):
                                for k in range(KD):
                                    i = mm(dst, xT[x][:, k, wsl],
                                           wa[w][:, 2, k, :].rearrange("p (j o d) -> p o j d", o=2, d=HD)[:, par2],
                                           start=(j == 0 and k == 0), stop=(j == 2 and k == KD - 1))
                    i.then_inc(s["unit_full"], 1)
                pe.wait_ge(s["act_empty"], emptied("A", 1, n, U_K))
                pe.wait_ge(s["dve_empty"], emptied("D", 1, n, U_K + 1))
                if not (isinstance(n, int) and n == 0):
                    pe.wait_ge(s["s_taken"], n)
                for w in range(TB):
                    for m in range(KD):
                        for o in range(2):
                            for g in range(4):
                                row = slice(32 * g, 32 * g + 32)
                                col = (((w // 2) * 2 + m) * 2 + o) * WIN
                                i = mm(S[64 * (w % 2):64 * (w % 2) + 64, g, col:col + WIN],
                                       QT[o][row, m, w * (WIN + 1) + 1:(w + 1) * (WIN + 1)],
                                       KT[row, m, w * STRIDE + 1:w * STRIDE + 1 + WIN], start=True, stop=True)
                i.then_inc(s["s_full"], 1)
                pe.wait_ge(s["q0_ready"], n + 1)
                if isinstance(n, int) and n == 0:
                    pe.wait_ge(s["bias_ready"], 1)
                else:
                    pe.wait_ge(s["g_exp"], n)
                for m in range(KD):
                    i = mm(G[0:NH, :], q0[:, m, :], KT[:, m, :], start=(m == 0), stop=(m == KD - 1))
                i.then_inc(s["g_full"], 1)

            def part2(n, par):
                claim(2, n, U_GT)
                pe.wait_ge(s["g_ready"], n + 1)
                for t in range(TB):
                    i = mm(T(U_GT)[:, t * NH:(t + 1) * NH], gs[0:NH, t * P:(t + 1) * P], ident[0:NH, 0:NH], start=True, stop=True)
                i.then_inc(s["unit_full"], 1)
                claim(2, n, U_U)
                pe.wait_ge(s["act_empty"], emptied("A", 2, n, U_GT))
                for k in range(KD):
                    for t in range(TB):
                        i = mm(T(U_U)[:, k * NH:(k + 1) * NH], xnr[par][:, t, k * P:(k + 1) * P], gp[:, t, :],
                               start=(t == 0), stop=(t == TB - 1))
                i.then_inc(s["unit_full"], 1)
                pe.wait_ge(s["p_ready"], n + 1)
                for j in range(4):
                    claim(2, n, U_PT + j)
                    for g in range(4):
                        src = E[par][:, g, 2 * j:2 * j + 2, :].rearrange("p o c -> p (o c)")
                        i = nc.tensor.transpose(T(U_PT + j)[:, g * P:(g + 1) * P], src, ident)
                    i.then_inc(s["unit_full"], 1)
                claim(2, n, U_AV)
                pe.wait_ge(s["act_empty"], emptied("A", 2, n, U_PT + 2))
                pe.wait_ge(s["dve_empty"], emptied("D", 2, n, U_PT + 3))
                for m in range(KD):
                    for w in range(TB):
                        for g in range(4):
                            i = mm(T(U_AV)[32 * g:32 * g + 32, (m * TB + w) * WIN:(m * TB + w + 1) * WIN],
                                   VB[par][:, w, 4 * m + g, :], PT[:, (w // 2) * 2 + m, g, (w % 2) * WIN:(w % 2 + 1) * WIN],
                                   start=True, stop=True)
                i.then_inc(s["unit_full"], 1)
                for c in range(2):
                    claim(2, n, U_WO + c)
                    if c == 0:
                        pe.wait_ge(s["dve_empty"], emptied("D", 2, n, U_AV))
                    for t2 in range(2):
                        for j, (w, x) in enumerate(SPLIT):
                            for m in range(KD):
                                i = mm(T(U_WO + c)[:, t2 * D:(t2 + 1) * D], cT[x][:, m, 2 * c + t2, :], wa[w][:, 3, m, :],
                                       start=(j == 0 and m == 0), stop=(j == 2 and m == KD - 1))
                    i.then_inc(s["unit_full"], 1)

            pe.wait_ge(s["attn_low"], 1)
            pe.wait_ge(s["pads_ready"], 1)
            part1(0, 0)
            part1(1, 1)
            part2(0, 0)

            def turn(n, par):
                part1(n, par)
                part2(n - 1, 1 - par)

            pairs(pe, turn, 2, B)
            part2(B - 1, 1)

            pe.wait_ge(s["dve_empty"], emptied("D", 2, B - 1, U_WO + 1))
            for m in range(KD):
                for j, (w, x) in enumerate(SPLIT):
                    for k in range(KD):
                        i = mm(ps[:, 6, m * P:(m + 1) * P], wa[w][:, 2, k, m * P:(m + 1) * P],
                               uT[x][:, k, :, :].rearrange("p b h -> p (b h)"), start=(j == 0 and k == 0), stop=(j == 2 and k == KD - 1))
            i.then_inc(s["c0_full"], 1)
            pe.wait_ge(s["c0_ready"], 1)
            for j, (w, x) in enumerate(SPLIT):
                for m in range(KD):
                    i = mm(ps[0:B, 7, 0:D], c0[x][:, m, :], wa[w][:, 3, m, :], start=(j == 0 and m == 0), stop=(j == 2 and m == KD - 1))
            i.then_inc(s["out0_full"], 1)
            pe.wait_ge(s["chosen_ready"], 1)
            pe.wait_ge(s["out0_ready"], 1)
            for i_ in range(2):
                mm(ps[:, 6 + i_, :], ch[:, i_ * P:(i_ + 1) * P], ohm[:, :, :].rearrange("p t e -> p (t e)"),
                   start=True, stop=True).then_inc(s["prefix_full"], 1)

            def up(b, c):
                n, q = b * SC + c, c % 2
                pe.wait_ge(s["h_done"], n + 1)
                bsl = slice(XPAD + b * L, XPAD + (b + 1) * L) if isinstance(b, int) else bass.ds(b * L + XPAD, L)
                for i2 in range(2):
                    for j, (w, x) in enumerate(SPLIT):
                        for k in range(KD):
                            i = mm(ps[:, 2 * q + i2, :], w12[w][:, i2, k, c * P:(c + 1) * P], xT[x][:, k, bsl],
                                   start=(j == 0 and k == 0), stop=(j == 2 and k == KD - 1))
                i.then_inc(s["a_full"], 1)

            def down(b, par, c):
                n, q = b * SC + c, c % 2
                if c == 0:
                    pe.wait_ge(s["y_done"], b + 1)
                for j, (x, w) in enumerate(((0, 0), (0, 1), (1, 0))):
                    if j == 0:
                        pe.wait_ge(s["hh_high"], n + 1)
                    if j == 2:
                        pe.wait_ge(s["hh_low"], n + 1)
                    for t in range(TB):
                        i = mm(ps[:, 4 + 2 * par + t // 2, (t % 2) * D:(t % 2 + 1) * D], s_hh[x][q][:, t * P:(t + 1) * P], w3[w][:, c, :],
                               start=(c == 0 and j == 0 and t % 2 == 0), stop=(c == SC - 1 and j == 2), skip_group_check=True)
                if c == SC - 1:
                    i.then_inc(s["y_full"], 1)

            def shared(b0, b1):
                def batch(b, par, last=False):
                    for c in range(SC):
                        if c < SC - 1:
                            up(b, c + 1)
                        elif not last:
                            up(b + 1, 0)
                        down(b, par, c)

                up(b0, 0)
                if b1 - b0 > 2:
                    pairs(pe, batch, b0, b1 - 2)
                batch(b1 - 2, 0)
                batch(b1 - 1, 1, last=True)

            pe.wait_ge(s["shared_low"], 1)
            pe.wait_ge(s["route"], 1)
            shared(0, B_FIRST)

            pe.wait_ge(s["y_done"], B_FIRST + 2)
            pe.wait_ge(s["routed_low"], NE)
            pe.wait_ge(s["table_ready"], 1)

            def x_transposed(t, par, free):
                if free:
                    pe.wait_ge(s["rx_low"], t - 1)
                pe.wait_ge(s[f"xs_in{par}"], (t + (-par)) * 8 + 16)
                for k in range(KD):
                    i = nc.tensor.transpose(ps[:, 2 + par, k * P:(k + 1) * P], xs[par][:, k * P:(k + 1) * P], ident)
                i.then_inc(s["rx_full"], 1)

            def expert_of(t):
                tsl = slice(t, t + 1) if isinstance(t, int) else bass.ds(t, 1)
                return pe.value_load(etab[0:1, tsl], min_val=0, max_val=2 * EXPERT * (NE - 1))

            def gate_up(t, par, free):
                if free:
                    pe.wait_ge(s["r_h_done"], t - 1)
                pe.wait_ge(s["rx_low"], t + 1)
                e = expert_of(t)
                for j, (x, w) in enumerate(((0, 0), (0, 1), (1, 0))):
                    for k in range(KD):
                        i = mm(ps[:, par, :], r_x[x][par][:, k * P:(k + 1) * P], ar16[:, bass.ds(e + (w * EXPERT + k * 2 * RH), 2 * RH)],
                               start=(j == 0 and k == 0), stop=(j == 2 and k == KD - 1))
                i.then_inc(s["ab_full"], 1)

            def h_transposed(t, par, free):
                if free:
                    pe.wait_ge(s["rh_low"], t - 1)
                pe.wait_ge(s["r_h_done"], t + 1)
                for k in range(RH // P):
                    i = nc.tensor.transpose(ps[:, 4 + par, k * P:(k + 1) * P], r_h[par][:, k * P:(k + 1) * P], ident)
                i.then_inc(s["rh_full"], 1)

            def routed_down(t, par, free):
                if free:
                    pe.wait_ge(s["ry_done"], t - 1)
                pe.wait_ge(s["rh_low"], t + 1)
                e = expert_of(t)
                for j, (x, w) in enumerate(((0, 0), (0, 1), (1, 0))):
                    for k in range(RH // P):
                        i = mm(ps[:, 6 + par, 0:D], r_hh[x][par][:, k * P:(k + 1) * P],
                               ar16[:, bass.ds(e + (w * EXPERT + 2 * KD * RH + k * D), D)],
                               start=(j == 0 and k == 0), stop=(j == 2 and k == RH // P - 1))
                i.then_inc(s["ry_full"], 1)

            x_transposed(0, 0, False)
            for t in range(4):
                gate_up(t, t % 2, t >= 2)
                x_transposed(t + 1, (t + 1) % 2, t + 1 >= 2)
                if t >= 1:
                    h_transposed(t - 1, (t - 1) % 2, t - 1 >= 2)
                if t >= 2:
                    routed_down(t - 2, t % 2, t - 2 >= 2)

            def routed(t, par, steady=True):
                gate_up(t, par, True)
                x_transposed(t + 1, 1 - par, True)
                h_transposed(t - 1, 1 - par, True)
                routed_down(t - 2, par, steady)

            routed(4, 0)
            routed(5, 1)
            pairs(pe, routed, 6, NT - 2)
            routed(NT - 2, 0)
            gate_up(NT - 1, 1, True)
            h_transposed(NT - 2, 0, True)
            routed_down(NT - 3, 1, True)
            h_transposed(NT - 1, 1, True)
            routed_down(NT - 2, 0, True)
            routed_down(NT - 1, 1, True)
            pe.wait_ge(s["ry_done"], NT)
            shared(B_FIRST, B)


_INS = ['L0_attn_hidden_states', 'L0_attn_Wq', 'L0_attn_bq', 'L0_attn_Wk', 'L0_attn_bk', 'L0_attn_Wv', 'L0_attn_bv',
        'L0_attn_Wo', 'L0_attn_bo', 'L0_ffn_router_w', 'L0_ffn_expert_bias', 'L0_ffn_shared_w1', 'L0_ffn_shared_w2',
        'L0_ffn_shared_w3', 'L0_ffn_routed_w1', 'L0_ffn_routed_w2', 'L0_ffn_routed_w3']


def kernel(**inputs):
    import numpy as _np
    import concourse.bacc as _bacc
    from concourse import mybir as _mybir
    from concourse.bass_utils import run_bass_kernel_spmd as _run

    nc = _bacc.Bacc("TRN2", target_bir_lowering=False, num_devices=1)
    arrays, args = {}, {}
    f32, f16 = constants()
    given = {name: _np.ascontiguousarray(inputs[name]) for name in _INS}
    columns = _np.ascontiguousarray(_np.stack([given[f"L0_attn_b{c}"].reshape(KD, P) for c in "qkv"]).reshape(3 * KD, P).T)
    for name, x in {**given, "bias_columns": columns, "const_f32": f32, "const_f16": f16}.items():
        arrays[f"in_{name}_dram"] = x
        args[name] = nc.dram_tensor(f"in_{name}_dram", x.shape, _mybir.dt.from_np(x.dtype), kind="ExternalInput").ap()
    out = nc.dram_tensor("out_0_dram", (B, L, D), _mybir.dt.float32, kind="ExternalOutput").ap()
    moe_layer(nc, args, out)
    r = _run(nc, [arrays], core_ids=[0])
    return r.results[0]["out_0_dram"]
```

```python
from contextlib import ExitStack

import numpy as np
import concourse.bass as bass
from concourse import mybir

P = 128
B, L, D = 8, 512, 256
KD = D // P
TB = L // P
NTOK = B * TB
NH, HD = 16, 16
WIN, STRIDE = 64, 128
NE, RH = 16, 256
SH = 1024
SC = SH // P
NT = (B * L * 2) // P + NE
E_EARLY = 10
NR = NT // 2
EXPERT = 2 * KD * RH + (RH // P) * D
B_FIRST = 6
EPS = 1e-5
TOP = 64.0

F32, F16 = mybir.dt.float32, mybir.dt.float16
U32, I32 = mybir.dt.uint32, mybir.dt.int32
ALU = mybir.AluOpType
ACT = mybir.ActivationFunctionType
AX = mybir.AxisListType.X
RMAX = bass.bass_isa.ReduceOp.max

C_ID, C_EVEN, C_ODD, C_TOK, C_IE, C_HM, C_PW, C_IS = 0, 128, 129, 130, 258, 274, 306, 310
C_N = C_IS + NT


def constants():
    c = np.zeros((P, C_N), np.float32)
    p = np.arange(P)
    c[:, C_ID:C_ID + P] = np.eye(P)
    c[:, C_EVEN] = (p // HD) % 2 == 0
    c[:, C_ODD] = (p // HD) % 2 == 1
    c[:, C_TOK:C_TOK + P] = (p >= 1) & (p <= WIN)
    c[:, C_IE:C_IE + NE] = np.arange(NE)
    for m in range(KD):
        c[:, C_HM + m * NH:C_HM + (m + 1) * NH] = ((m * P + p)[:, None] // HD) == np.arange(NH)
    c[:, C_PW:C_PW + 4] = -0.5
    c[:, C_IS:C_IS + NT] = np.arange(NT)
    h = np.zeros((P, 2 * P), np.float16)
    h[:, 0:P] = p[:, None] < p[None, :]
    h[:, P:] = 1.0
    return c, h


PART1 = "DDAADADDD"
PART2 = "ADADADDDD"
U_XT, U_R, U_Q, U_K, U_V = 0, 2, 3, 5, 7
U_GT, U_U, U_PT, U_AV, U_WO = 0, 1, 2, 6, 7
RING = 3


def place(part, n):
    if part == 1:
        return 0 if isinstance(n, int) and n == 0 else n * 18 - 9
    return n * 18 + (9 if isinstance(n, int) and n == B - 1 else 18)


def emptied_before(who, part, n):
    one, two = PART1.count(who), PART2.count(who)
    if part == 1:
        return 0 if isinstance(n, int) and n == 0 else n * (one + two) - two
    if isinstance(n, int) and n == B - 1:
        return one * B + two * (B - 1)
    return n * (one + two) + 2 * one


def emptied(who, part, n, u):
    return emptied_before(who, part, n) + (PART1 if part == 1 else PART2)[:u + 1].count(who)


def moe_layer(nc, a, out):
    with ExitStack() as ctx:
        def sb(name, shape, dt=F32):
            return ctx.enter_context(nc.sbuf_tensor(name, shape, dt))[:]

        def sem(name):
            return ctx.enter_context(nc.semaphore(name))

        xs_dram = nc.dram_tensor("rows_by_slot", (NT * P, D), F32, kind="Internal").ap()
        ys_dram = nc.dram_tensor("routed_by_slot", (NT * P, D), F32, kind="Internal").ap()
        y1_dram = nc.dram_tensor("x_plus_attention", (B * L, D), F32, kind="Internal").ap()
        y2_dram = nc.dram_tensor("plus_shared", (B * L, D), F32, kind="Internal").ap()
        x_rows = a["L0_attn_hidden_states"].rearrange("b (t p) d -> b p t d", p=P)
        xs_pairs = xs_dram.rearrange("(r t p) d -> r p t d", p=P, t=2)
        ys_pairs = ys_dram.rearrange("(r t p) d -> r p t d", p=P, t=2)
        y1_rows = y1_dram.rearrange("(b t p) d -> b p t d", p=P, t=TB)
        y2_rows = y2_dram.rearrange("(b t p) d -> b p t d", p=P, t=TB)
        out_rows = out.rearrange("b (t p) d -> b p t d", p=P)

        cf = sb("const_f32", [P, C_N])
        ch = sb("const_f16", [P, 2 * P], F16)
        ident = cf[:, C_ID:C_ID + P]
        wa = [sb(f"attn_w_{x}", [P, 4, KD, D], F16) for x in ("high", "low")]
        wr = [sb(f"router_w_{x}", [P, KD, NE], F16) for x in ("high", "low")]
        w12 = [sb(f"shared_w12_{x}", [P, 2, KD, SH], F16) for x in ("high", "low")]
        w3 = [sb(f"shared_w3_{x}", [P, SC, D], F16) for x in ("high", "low")]
        XPAD = WIN
        xT = [sb(f"xn_T_{x}", [P, KD, XPAD + B * L], F16) for x in ("high", "low")]
        mx = sb("w_max", [P, 12])
        pw = sb("w_pow", [P, 12])
        inv = sb("w_inv", [P, 12])
        scl = sb("w_scale", [P, 12])
        der = sb("w_derived", [P, 12])
        D_QE, D_QO, D_O, D_Y, D_HS, D_RY, D_RHS = range(7)
        bqkv = sb("bqkv_columns", [P, 3 * KD])
        bq, bk, bv = (bqkv[:, i * KD:(i + 1) * KD] for i in range(3))
        bqp = sb("bq_by_parity", [P, 2, KD])
        bias_tile = sb("out_bias", [P, D]); bv_out = sb("bv_times_wo", [B, D])
        eb = sb("expert_bias", [P, NE])
        logits = sb("router_logits", [P, NTOK, NE])
        gate = sb("gates", [P, 2, NTOK])
        slots = sb("slots", [P, 2, NTOK], U32)
        etab = sb("expert_offset_of_tile", [1, NT], I32)
        uT = [sb(f"u_T_{x}", [P, KD, B, NH], F16) for x in ("high", "low")]
        zero = sb("zeros", [P, D])

        arena = sb("arena", [P, (NE + 1) * EXPERT])
        at = [0]

        def cut(*dims, dt=F32):
            n = int(np.prod(dims))
            fl = n if dt == F32 else n // 2
            v = arena[:, at[0]:at[0] + fl]
            at[0] += fl
            if dt != F32:
                v = v.bitcast(dt)
            if len(dims) == 2:
                v = v.rearrange("p (a b) -> p a b", a=dims[0])
            if len(dims) == 3:
                v = v.rearrange("p (a b c) -> p a b c", a=dims[0], b=dims[1])
            return v

        E = [cut(4, 8, WIN) for _ in range(2)]
        route_area = arena[:, 0:2 * 4 * 8 * WIN]
        PT = cut(4, 4, P)
        QT = [cut(KD, TB * (WIN + 1)) for _ in range(2)]
        KT = cut(KD, L)
        VB = [cut(TB, 8, 32) for _ in range(2)]
        xr = [cut(TB, D) for _ in range(2)]
        xb = [cut(TB, D) for _ in range(2)]
        xnr = [cut(TB, D) for _ in range(2)]
        cT = [cut(KD, TB, P, dt=F16) for _ in range(2)]
        assert at[0] <= (NE + 1) * EXPERT - NTOK * D, at[0]
        xn = arena[:, (NE + 1) * EXPERT - NTOK * D:].rearrange("p (t d) -> p t d", t=NTOK)
        assert (E_EARLY + 1) * EXPERT <= (NE + 1) * EXPERT - NTOK * D
        ar16 = arena[:, :].bitcast(F16)

        work = sb("work", [P, 2080 + 2 * KD * SH])
        wa_raw = work[:, 0:4 * KD * D].rearrange("p (i k d) -> p i k d", i=4, k=KD)
        wr_raw = work[:, 2048:2048 + KD * NE].rearrange("p (k e) -> p k e", k=KD)
        w12_raw = work[:, 2080:2080 + 2 * KD * SH].rearrange("p (i k h) -> p i k h", i=2, k=KD)
        w3_raw = E[1].rearrange("p g k c -> p (g k c)").rearrange("p (c d) -> p c d", c=SC)
        wat = [0]

        def wcut(n, dt=F32):
            v = work[:, wat[0]:wat[0] + n]
            wat[0] += n
            return v.bitcast(dt) if dt != F32 else v

        s_silu = [wcut(L) for _ in range(2)]
        s_h = [wcut(L) for _ in range(2)]
        s_hh = [[wcut(L // 2, F16) for _ in range(2)] for _ in range(2)]
        s_y = [wcut(TB * D).rearrange("p (t d) -> p t d", t=TB) for _ in range(2)]
        assert wat[0] <= 2080 + 2 * KD * SH
        wat[0] = 0
        xs = [wcut(2 * D).rearrange("p (t d) -> p t d", t=2) for _ in range(2)]
        r_x = [[wcut(D, F16) for _ in range(2)] for _ in range(2)]
        r_silu = [wcut(RH) for _ in range(2)]
        r_h = [wcut(2 * RH) for _ in range(2)]
        r_hh = [[wcut(RH, F16) for _ in range(2)] for _ in range(2)]
        ys = [wcut(2 * D).rearrange("p (t d) -> p t d", t=2) for _ in range(2)]
        assert wat[0] <= 2080 + 2 * KD * SH, wat[0]

        gs = sb("global_p", [P, L])
        q0 = sb("global_q", [P, KD, NH])
        gp = sb("global_p_T", [P, TB, NH])
        rmx = sb("routed_w_max", [P, 3, NE])
        tick = sb("tick", [1, 16])
        st = sb("ln_stats", [P, TB, 6]); mv = sb("ln_mean_var", [P, TB, 2])
        ve = sb("ln_var_eps", [P, TB]); rstd = sb("ln_rstd", [P, TB]); nmr = sb("ln_shift", [P, TB])
        smx = sb("softmax_max", [P, 4, 8]); ssum = sb("softmax_sum", [P, 4, 8]); srec = sb("softmax_rec", [P, 4, 8])
        gmx = sb("global_neg_max", [NH, 1]); gsum = sb("global_sum", [NH, 1]); grec = sb("global_rec", [NH, 1])
        c0f = sb("ctx0_f32", [P, KD, B]); c0 = [sb(f"ctx0_{x}", [P, KD, B], F16) for x in ("high", "low")]
        c0m = sb("ctx0_masked", [P, B, NH]); out0 = sb("out0", [B, D])
        bvm = PT[:, 0, 0:KD, :]

        picked = arena[:, 0:2 * NTOK * D].rearrange("p (k t d) -> p k t d", k=2, t=NTOK)
        c_y = [arena[:, (2 * NTOK + b * TB) * D:(2 * NTOK + (b + 1) * TB) * D].rearrange("p (t d) -> p t d", t=TB)
               for b in range(B_FIRST)]

        ra = [route_area[:, i * 512:(i + 1) * 512].rearrange("p (t e) -> p t e", e=NE) for i in range(8)]
        sc_, sel, oh1, oh2, tmp = ra[:5]
        cum, posn, restart = (route_area[:, i * 512:(i + 1) * 512].rearrange("p (e t) -> p e t", e=NE) for i in (5, 6, 7))
        mx8 = arena[:, 4096:4352].rearrange("p (t e) -> p t e", e=8)
        ix8 = arena[:, 4352:4608].bitcast(U32).rearrange("p (t e) -> p t e", e=8)
        ixf = sb("top_indices_f32", [P, NTOK, 2])
        ohm = arena[:, 4608:4864].bitcast(F16).rearrange("p (e t) -> p e t", e=NE)
        tl = [sb(f"tiles_{i}", [P, NE]) for i in range(3)]
        slf = sb("slots_f32", [P, 2, NTOK])
        ecount = arena[0:1, 4864:4864 + NT * NE].rearrange("p (t e) -> p t e", e=NE)
        ef = sb("expert_of_tile", [1, NT])

        ps = ctx.enter_context(nc.psum_tensor("ps", [P, 8, 512], F32))
        S = ps[:, 0:4, :]
        G = ps[:, 4, :]

        def T(pos):
            return ps[:, 5 + pos % RING, :]

        s = {n: sem(n) for n in (
            "consts_in attn_w_in shared_w_in bias_in zeros_ready xs_zeroed "
            "attn_max attn_all_max shared_max shared_all_max routed_max routed_all_max "
            "scale_ready attn_high attn_low shared_high shared_low routed_high routed_low setup "
            "bias_psum bias_ready pads_ready "
            "x_in0 x_in1 ln_stats ln_mv ln_var ln_rstd ln_shift xn_made xn_kept xb_made xT_high "
            "unit_full act_empty dve_empty s_full s_max s_taken s_exp s_summed soft_sum vector_step routed_each p_ready "
            "q0_half q0_ready g_full g_max g_exp g_rec g_ready u_high ctx_high "
            "y1_stored0 y1_stored1 c0_full c0_step c0_ready out0_full out0_ready out0_added "
            "scores_ready route chosen_ready prefix_full slots_ready table_ready scattered "
            "raw_in_early raw_in_late a_full silu_done h_done hh_high hh_low y_full y_in0 y_in1 y_done y2_stored0 y2_stored1 "
            "xs_in0 xs_in1 rx_full rx_high rx_low ab_full r_silu_done r_h_done rh_full rh_high rh_low "
            "ry_full ry_done ys_stored0 ys_stored1 "
            "base_in mixed one_added out_stored").split()}
        pick_in = [sem(f"picked_in_{b}") for b in range(B)]
        block = ctx.enter_context(nc.Block())

        SPLIT = ((0, 0), (1, 0), (0, 1))

        def pairs(eng, body, first, last):
            with eng.Fori(first // 2, last // 2) as i:
                for par in range(2):
                    body(i * 2 + par, par)

        @block.sync
        def _(sp):
            sp.dma_start(wa_raw[:, 0], a["L0_attn_Wq"].rearrange("(k p) d -> p k d", p=P)).then_inc(s["attn_w_in"], 16)
            sp.dma_start(wa_raw[:, 1], a["L0_attn_Wk"].rearrange("(k p) d -> p k d", p=P)).then_inc(s["attn_w_in"], 16)
            sp.dma_start(wa_raw[:, 2], a["L0_attn_Wv"].rearrange("(k p) d -> p k d", p=P)).then_inc(s["attn_w_in"], 16)
            sp.dma_start(wa_raw[:, 3], a["L0_attn_Wo"].rearrange("(k p) d -> p k d", p=P)).then_inc(s["attn_w_in"], 16)
            sp.dma_start(wr_raw, a["L0_ffn_router_w"].rearrange("(k p) e -> p k e", p=P)).then_inc(s["attn_w_in"], 16)
            for n in range(2):
                sp.dma_start(xr[n], x_rows[n]).then_inc(s[f"x_in{n}"], 16)
            for i, name in enumerate(("shared_w1", "shared_w2")):
                sp.dma_start(w12_raw[:, i], a[f"L0_ffn_{name}"].rearrange("o (k p) h -> p (o k) h", p=P)).then_inc(s["shared_w_in"], 16)
            sp.dma_start(w3_raw, a["L0_ffn_shared_w3"].rearrange("o (c p) d -> p (o c) d", p=P)).then_inc(s["shared_w_in"], 16)
            sp.wait_ge(s["zeros_ready"], 1)
            sp.dma_start(xs_dram.rearrange("(p a) d -> p a d", p=P),
                         zero[:, :].unsqueeze(1).to_broadcast([P, NT, D])).then_inc(s["xs_zeroed"], 16)

            def attention(n, par, load=True):
                if load:
                    sp.wait_ge(s["xn_made"], n + 1)
                    sp.wait_ge(s["xb_made"], n + 1)
                    sp.dma_start(xr[par], x_rows[bass.ds(n + 2, 1)].rearrange("a p t d -> p (a t) d")).then_inc(s[f"x_in{par}"], 16)
                sp.wait_ge(s["dve_empty"], emptied("D", 2, n, U_WO + 1))
                sp.dma_start(y1_rows[bass.ds(n, 1)].rearrange("a p t d -> p (a t) d"), xb[par]).then_inc(s[f"y1_stored{par}"], 16)

            pairs(sp, attention, 0, B - 2)
            attention(B - 2, 0, load=False)
            attention(B - 1, 1, load=False)

            def shared(b0, b1):
                def load(b, par):
                    sp.dma_start(s_y[par], y1_rows[b]).then_inc(s[f"y_in{par}"], 16)
                for b in range(b0, b1):
                    par = b % 2
                    if b == b0:
                        if b >= 2:
                            sp.wait_ge(s[f"y2_stored{par}"], 16 * (b // 2))
                        load(b, par)
                    if b + 1 < b1:
                        if b >= 1:
                            sp.wait_ge(s[f"y2_stored{1 - par}"], 16 * ((b + 1) // 2))
                        load(b + 1, 1 - par)
                    if b < B_FIRST:
                        sp.wait_ge(s["y_done"], b + 3)
                        sp.dma_start(y2_rows[b], s_y[par]).then_inc(s[f"y2_stored{par}"], 16)

            for par in range(2):
                sp.wait_ge(s[f"y1_stored{par}"], 16 * (B // 2))
            sp.wait_ge(s["out0_added"], 16)
            sp.wait_ge(s["shared_low"], 1)
            def raw_weights(first, last, name):
                for e in range(first, last):
                    raw = arena[:, (e + 1) * EXPERT:(e + 2) * EXPERT]
                    r12 = raw[:, 0:2 * KD * RH].rearrange("p (k i h) -> p k i h", k=KD, i=2)
                    sp.dma_start(r12[:, :, 0, :], a["L0_ffn_routed_w1"][e].rearrange("(k p) h -> p k h", p=P)).then_inc(s[name], 16)
                    sp.dma_start(r12[:, :, 1, :], a["L0_ffn_routed_w2"][e].rearrange("(k p) h -> p k h", p=P)).then_inc(s[name], 16)
                    sp.dma_start(raw[:, 2 * KD * RH:].rearrange("p (c d) -> p c d", d=D),
                                 a["L0_ffn_routed_w3"][e].rearrange("(c p) d -> p c d", p=P)).then_inc(s[name], 16)

            shared(0, 1)
            sp.wait_ge(s["route"], 1)
            raw_weights(0, E_EARLY, "raw_in_early")
            shared(1, 3)
            sp.wait_ge(s["scattered"], 16 * 2 * NTOK)
            raw_weights(E_EARLY, NE, "raw_in_late")
            shared(3, B_FIRST)

            def load_rows(r, par):
                sp.dma_start(xs[par], xs_pairs[r] if isinstance(r, int) else
                             xs_pairs[bass.ds(r, 1)].rearrange("a p t d -> p (a t) d")).then_inc(s[f"xs_in{par}"], 16)

            def store_rows(r, par):
                sp.wait_ge(s["ry_done"], r + 1)
                sp.dma_start(ys_pairs[r] if isinstance(r, int) else
                             ys_pairs[bass.ds(r, 1)].rearrange("a p t d -> p (a t) d"), ys[par]).then_inc(s[f"ys_stored{par}"], 16)

            for par in range(2):
                sp.wait_ge(s[f"y2_stored{par}"], 16 * (B_FIRST // 2))
            load_rows(0, 0)
            load_rows(1, 1)

            LAG = 5

            def routed(r, par):
                sp.wait_ge(s["rx_full"], r - 1)
                load_rows(r, par)
                store_rows(r - LAG, 1 - par)

            for r in range(2, LAG + 1):
                sp.wait_ge(s["rx_full"], r - 1)
                load_rows(r, r % 2)
            store_rows(0, 0)
            pairs(sp, routed, LAG + 1, NR)
            for r in range(NR - LAG, NR):
                store_rows(r, r % 2)
            for par in range(2):
                sp.wait_ge(s[f"ys_stored{par}"], 16 * (NR // 2))
            shared(B_FIRST, B)
            for b in range(B_FIRST):
                sp.dma_start(c_y[b], y2_rows[b]).then_inc(s["base_in"], 16)

            for b in range(B):
                sp.wait_ge(s["mixed"], TB * (b + 1))
                sp.dma_start(out_rows[b], c_y[b] if b < B_FIRST else s_y[b % 2]).then_inc(s["out_stored"], 16)
            sp.wait_ge(s["out_stored"], 16 * B)

        @block.gpsimd
        def _(pool):
            pool.dma_start(cf[:, :], a["const_f32"]).then_inc(s["consts_in"], 16)
            pool.dma_start(ch[:, :], a["const_f16"]).then_inc(s["consts_in"], 16)
            pool.dma_start(bqkv[:, :], a["bias_columns"]).then_inc(s["bias_in"], 16)
            pool.dma_start(bias_tile[:, :], a["L0_attn_bo"].unsqueeze(0).to_broadcast([P, D])).then_inc(s["bias_in"], 16)
            pool.dma_start(eb[:, :], a["L0_ffn_expert_bias"].unsqueeze(0).to_broadcast([P, NE])).then_inc(s["bias_in"], 16)
            nc.gpsimd.memset(zero[:, :], 0.0).then_inc(s["zeros_ready"], 1)
            for v in VB:
                nc.gpsimd.memset(v, 0.0)
            nc.gpsimd.memset(cT[0], 0.0)
            for x in xT:
                nc.gpsimd.memset(x[:, :, 0:XPAD], 0.0)
            nc.gpsimd.memset(cT[1], 0.0).then_inc(s["pads_ready"], 1)
            pool.wait_ge(s["attn_max"], 2)
            nc.gpsimd.partition_all_reduce(pw[:, 0:5], mx[:, 0:5], P, RMAX).then_inc(s["attn_all_max"], 1)

            def rstd_of(n):
                pool.wait_ge(s["ln_var"], n + 1)
                nc.gpsimd.tensor_tensor(rstd[:, :], ve[:, :], cf[:, C_PW:C_PW + TB], ALU.pow).then_inc(s["ln_rstd"], 1)

            def rows_of(n, par, stored):
                if stored:
                    pool.wait_ge(s[f"y1_stored{par}"], (n + (-par)) * 8)
                nc.gpsimd.tensor_tensor(xb[par], xr[par], bias_tile[:, :].unsqueeze(1).to_broadcast([P, TB, D]),
                                        ALU.add).then_inc(s["xb_made"], 1)
                pool.wait_ge(s["xn_made"], n + 1)
                dst = xn[:, n * TB:(n + 1) * TB, :] if isinstance(n, int) else xn[:, bass.ds(n * TB, TB), :]
                nc.gpsimd.tensor_copy(dst, xnr[par]).then_inc(s["xn_kept"], 1)

            def normalise(n, par):
                pool.wait_ge(s["s_summed"], n + 1)
                e = E[par].rearrange("p g k c -> p (g k) c")
                r = srec[:, :, :].rearrange("p g k -> p (g k)").unsqueeze(2).to_broadcast([P, 32, WIN])
                nc.gpsimd.tensor_tensor(e, e, r, ALU.mult).then_inc(s["p_ready"], 1)

            pool.wait_ge(s["consts_in"], 32)
            rstd_of(0)
            pool.wait_ge(s["bias_ready"], 1)
            rows_of(0, 0, False)
            rstd_of(1)
            rows_of(1, 1, False)
            pool.wait_ge(s["shared_max"], 2)
            nc.gpsimd.partition_all_reduce(pw[:, 5:8], mx[:, 5:8], P, RMAX).then_inc(s["shared_all_max"], 1)
            normalise(0, 0)

            def turn(n, par):
                rstd_of(n)
                rows_of(n, par, True)
                normalise(n - 1, 1 - par)

            pairs(pool, turn, 2, B)
            normalise(B - 1, 1)

            for par in range(2):
                pool.wait_ge(s[f"y1_stored{par}"], 16 * (B // 2))
            pool.wait_ge(s["out0_ready"], 1)
            pool.dma_start(y1_dram.rearrange("(b l) d -> b l d", l=L)[:, 0, :], out0[:, :],
                           accum_op=ALU.add).then_inc(s["out0_added"], 16)

            pool.wait_ge(s["xs_zeroed"], 16)
            pool.wait_ge(s["slots_ready"], 1)
            for t in range(NTOK):
                for k in range(2):
                    pool.indirect_dma_start(out=xs_dram, out_offset=bass.IndirectOffsetOnAxis(ap=slots[:, k, t:t + 1], axis=0),
                                            in_=xn[:, t, :], in_offset=None).then_inc(s["scattered"], 16)

            pool.wait_ge(s["routed_max"], 1)
            nc.gpsimd.partition_all_reduce(pw[:, 8:11], mx[:, 8:11], P, RMAX).then_inc(s["routed_all_max"], 1)

            for par in range(2):
                pool.wait_ge(s[f"ys_stored{par}"], 16 * (NR // 2))
            for t in range(NTOK):
                for k in range(2):
                    pool.indirect_dma_start(out=picked[:, k, t, :], out_offset=None, in_=ys_dram,
                                            in_offset=bass.IndirectOffsetOnAxis(ap=slots[:, k, t:t + 1], axis=0)).then_inc(pick_in[t // TB], 16)

        @block.scalar
        def _(act):
            ev = nc.scalar

            def split_high(dst, src, col, name, inc=True):
                i = ev.activation(dst, src, ACT.Identity, scale=scl[:, col:col + 1])
                if inc:
                    i.then_inc(s[name], 1)

            act.wait_ge(s["attn_w_in"], 80)
            act.wait_ge(s["scale_ready"], 1)
            for i in range(4):
                split_high(wa[0][:, i], wa_raw[:, i], i, "attn_high")
            split_high(wr[0][:, :, :], wr_raw, 4, "attn_high")

            def part1(n, par):
                pos = place(1, n)
                nsl = (lambda: slice(XPAD + n * L, XPAD + (n + 1) * L)) if isinstance(n, int) else (lambda: bass.ds(n * L + XPAD, L))
                for k in range(KD):
                    act.wait_ge(s["unit_full"], pos + U_XT + k + 1)
                    ev.activation(xT[0][:, k, nsl()], ps[:, 5 + (U_XT + k) % RING, :], ACT.Identity).then_inc(s["xT_high"], 1)
                act.wait_ge(s["unit_full"], pos + U_R + 1)
                lsl = slice(n * TB, (n + 1) * TB) if isinstance(n, int) else bass.ds(n * TB, TB)
                ev.activation(logits[:, lsl, :], T(U_R)[:, 0:TB * NE].rearrange("p (t e) -> p t e", e=NE),
                              ACT.Identity, scale=inv[:, 4:5]).then_inc(s["act_empty"], 1)
                act.wait_ge(s["unit_full"], pos + U_Q + 1)
                for o in range(2):
                    q = ev.activation(QT[o][:, 0, :], T(U_Q)[:, 0:TB * (WIN + 1)], ACT.Identity,
                                      bias=bqp[:, o, 0:1], scale=der[:, D_QE + o:D_QE + o + 1])
                q.then_inc(s["act_empty"], 1)
                act.wait_ge(s["unit_full"], pos + U_K + 1)
                ev.activation(KT[:, 0, :], T(U_K), ACT.Identity, bias=bk[:, 0:1], scale=inv[:, 1:2]).then_inc(s["act_empty"], 1)

            def soft(n, par):
                act.wait_ge(s["s_taken"], n + 1)
                e = E[par].rearrange("p g k c -> p (g k c)")
                ev.activation(e, e, ACT.Exp).then_inc(s["s_exp"], 1)
                act.wait_ge(s["g_max"], n + 1)
                ev.activation(gs[0:NH, :], G[0:NH, :], ACT.Exp, bias=gmx[:, :], accum_out=gsum[:, :]).then_inc(s["g_exp"], 1)

            def part2(n, par):
                pos = place(2, n)
                act.wait_ge(s["unit_full"], pos + U_GT + 1)
                ev.activation(gp, T(U_GT)[:, 0:TB * NH].rearrange("p (t e) -> p t e", e=NH), ACT.Identity).then_inc(s["act_empty"], 1)
                act.wait_ge(s["unit_full"], pos + U_U + 1)
                usl = slice(n, n + 1) if isinstance(n, int) else bass.ds(n, 1)
                ev.activation(uT[0][:, :, usl, :].rearrange("p k o e -> p k (o e)"),
                              T(U_U)[:, 0:KD * NH].rearrange("p (k e) -> p k e", e=NH), ACT.Identity).then_inc(s["u_high"], 1)
                for j in (0, 2):
                    act.wait_ge(s["unit_full"], pos + U_PT + j + 1)
                    ev.activation(PT[:, j], T(U_PT + j).rearrange("p (g q) -> p g q", g=4), ACT.Identity).then_inc(s["act_empty"], 1)
                act.wait_ge(s["unit_full"], pos + U_AV + 1)
                ev.activation(cT[0][:, :, :, 1:1 + WIN], T(U_AV).rearrange("p (m w q) -> p m w q", m=KD, w=TB),
                              ACT.Identity).then_inc(s["ctx_high"], 1)

            act.wait_ge(s["setup"], 1)
            part1(0, 0)
            act.wait_ge(s["shared_w_in"], 48)
            act.wait_ge(s["scale_ready"], 2)
            for i in range(2):
                split_high(w12[0][:, i], w12_raw[:, i], 5 + i, "shared_high")
            split_high(w3[0][:, :, :], w3_raw, 7, "shared_high")
            soft(0, 0)
            part1(1, 1)
            part2(0, 0)
            soft(1, 1)

            def turn(n, par):
                part1(n, par)
                part2(n - 1, 1 - par)
                soft(n, par)

            act.wait_ge(s["pads_ready"], 1)
            pairs(act, turn, 2, B)
            part2(B - 1, 1)

            ev.activation(sc_, logits[:, :, :], ACT.Sigmoid).then_inc(s["scores_ready"], 1)

            def chunk(b, c):
                n, q = b * SC + c, c % 2
                act.wait_ge(s["a_full"], n + 1)
                ev.activation(s_silu[q], ps[:, 2 * q, :], ACT.Silu, scale=inv[:, 5:6]).then_inc(s["silu_done"], 1)
                act.wait_ge(s["h_done"], n + 3)
                ev.activation(s_hh[0][q], s_h[q], ACT.Identity).then_inc(s["hh_high"], 1)

            def shared(b0, b1):
                with act.Fori(b0, b1) as b:
                    for c in range(SC):
                        chunk(b, c)

            act.wait_ge(s["shared_low"], 1)
            shared(0, 4)
            act.wait_ge(s["scale_ready"], 3)
            with act.Fori(4, B_FIRST) as b:
                for c in range(SC):
                    chunk(b, c)
                    act.wait_ge(s["routed_low"], b * SC + (c + 1 - 4 * SC))
                    raw = lambda lo, n: arena[:, bass.ds(b * (SC * EXPERT) + ((c + 1 - 4 * SC) * EXPERT + lo), n)]
                    high = lambda lo, n: ar16[:, bass.ds(b * (2 * SC * EXPERT) + (2 * (c - 4 * SC) * EXPERT + lo), n)]
                    for i in range(2):
                        ev.activation(high(0, 2 * KD * RH).rearrange("p (k i h) -> p k i h", k=KD, i=2)[:, :, i],
                                      raw(0, 2 * KD * RH).rearrange("p (k i h) -> p k i h", k=KD, i=2)[:, :, i],
                                      ACT.Identity, scale=scl[:, 8 + i:9 + i])
                    ev.activation(high(2 * KD * RH, 2 * D), raw(2 * KD * RH, 2 * D), ACT.Identity,
                                  scale=scl[:, 10:11]).then_inc(s["routed_high"], 1)

            def x_high(r, par):
                act.wait_ge(s["rx_full"], r + 1)
                ev.activation(r_x[0][par], ps[:, 2 + par, :], ACT.Identity).then_inc(s["rx_high"], 1)

            def gated(r, par):
                for j in range(2):
                    act.wait_ge(s["ab_full"], 2 * r + j + 1)
                    ev.activation(r_silu[j], ps[:, j, 0:RH], ACT.Silu, scale=inv[:, 8:9]).then_inc(s["r_silu_done"], 1)

            def h_high(r, par):
                act.wait_ge(s["rh_full"], r + 1)
                ev.activation(r_hh[0][par], ps[:, 4 + par, :], ACT.Identity).then_inc(s["rh_high"], 1)

            def y_out(r, par, stored=True):
                act.wait_ge(s["ry_full"], r + 1)
                if stored:
                    act.wait_ge(s[f"ys_stored{par}"], (r + (-par)) * 8)
                ev.activation(ys[par].rearrange("p t d -> p (t d)"), ps[:, 6 + par, :], ACT.Identity,
                              scale=der[:, D_RY:D_RY + 1]).then_inc(s["ry_done"], 1)

            x_high(0, 0)
            for r in range(4):
                x_high(r + 1, (r + 1) % 2)
                gated(r, r % 2)
                if r >= 1:
                    h_high(r - 1, (r - 1) % 2)
                if r >= 2:
                    y_out(r - 2, r % 2, stored=False)

            def routed(r, par):
                x_high(r + 1, 1 - par)
                gated(r, par)
                h_high(r - 1, 1 - par)
                y_out(r - 2, par)

            pairs(act, routed, 4, NR - 2)
            routed(NR - 2, 0)
            gated(NR - 1, 1)
            h_high(NR - 2, 0)
            y_out(NR - 3, 1)
            h_high(NR - 1, 1)
            y_out(NR - 2, 0)
            y_out(NR - 1, 1)
            for par in range(2):
                act.wait_ge(s[f"ys_stored{par}"], 16 * (NR // 2))
            shared(B_FIRST, B)

        @block.vector
        def _(dve):
            v = nc.vector
            steps = [0]

            def link(i):
                steps[0] += 1
                i.then_inc(s["vector_step"], 1)
                dve.wait_ge(s["vector_step"], steps[0])

            marks = [0]

            def signal(name, n=1):
                marks[0] += 1
                v.memset(tick[:, marks[0]:marks[0] + 1], 0.0).then_inc(s[name], n)

            def scales(lo, hi, reduced, count):
                dve.wait_ge(s[reduced], 1)
                link(v.tensor_scalar(pw[:, lo:hi], pw[:, lo:hi], 2.0 ** -40, None, ALU.max))
                link(v.tensor_scalar(pw[:, lo:hi].bitcast(I32), pw[:, lo:hi].bitcast(I32), 0x7F800000, None, ALU.bitwise_and))
                link(v.tensor_scalar(inv[:, lo:hi], pw[:, lo:hi], 1.0 / TOP, None, ALU.mult))
                link(v.reciprocal(scl[:, lo:hi], inv[:, lo:hi]))

            def ln(n, par, kept):
                x = xr[par]
                dve.wait_ge(s[f"x_in{par}"], (n + (-par)) * 8 + 16)
                for t in range(TB):
                    i = v.bn_stats(st[:, t, :], x[:, t, :])
                i.then_inc(s["ln_stats"], 1)
                dve.wait_ge(s["ln_stats"], n + 1)
                v.memset(tick[:, 0:1], 0.0)
                for t in range(TB):
                    i = v.bn_aggr(mv[:, t, :], st[:, t, :])
                i.then_inc(s["ln_mv"], 1)
                dve.wait_ge(s["ln_mv"], n + 1)
                v.tensor_scalar(ve[:, :], mv[:, :, 1], EPS, None, ALU.add).then_inc(s["ln_var"], 1)
                dve.wait_ge(s["ln_rstd"], n + 1)
                v.scalar_tensor_tensor(out=nmr[:, :], in0=mv[:, :, 0], scalar=-1.0, in1=rstd[:, :],
                                       op0=ALU.mult, op1=ALU.mult).then_inc(s["ln_shift"], 1)
                dve.wait_ge(s["ln_shift"], n + 1)
                if kept:
                    dve.wait_ge(s["xn_kept"], n - 1)
                for t in range(TB):
                    i = v.tensor_scalar(xnr[par][:, t, :], x[:, t, :], rstd[:, t:t + 1], nmr[:, t:t + 1], ALU.mult, ALU.add)
                i.then_inc(s["xn_made"], 1)

            def part1(n, par):
                pos = place(1, n)
                nsl = (lambda: slice(XPAD + n * L, XPAD + (n + 1) * L)) if isinstance(n, int) else (lambda: bass.ds(n * L + XPAD, L))
                for k in range(KD):
                    dve.wait_ge(s["xT_high"], n * 2 + k + 1)
                    v.tensor_tensor(xT[1][:, k, nsl()], T(U_XT + k), xT[0][:, k, nsl()], ALU.subtract).then_inc(s["dve_empty"], 1)
                dve.wait_ge(s["unit_full"], pos + U_Q + 1 + 1)
                for o in range(2):
                    i = v.tensor_scalar(QT[o][:, 1, :], T(U_Q + 1)[:, 0:TB * (WIN + 1)], der[:, D_QE + o:D_QE + o + 1],
                                        bqp[:, o, 1:2], ALU.mult, ALU.add)
                i.then_inc(s["dve_empty"], 1)
                dve.wait_ge(s["act_empty"], emptied("A", 1, n, U_Q))
                dve.wait_ge(s["dve_empty"], emptied("D", 1, n, U_Q + 1))
                hm = cf[:, C_HM:C_HM + KD * NH].rearrange("p (m h) -> p m h", h=NH)
                for m in range(KD):
                    i = v.tensor_scalar(q0[:, m, :], hm[:, m, :], QT[0][:, m, 0:1], None, ALU.mult)
                i.then_inc(s["q0_half"], 1)
                dve.wait_ge(s["q0_half"], n + 1)
                for m in range(KD):
                    i = v.scalar_tensor_tensor(out=q0[:, m, :], in0=hm[:, m, :], scalar=QT[1][:, m, 0:1], in1=q0[:, m, :],
                                               op0=ALU.mult, op1=ALU.add)
                i.then_inc(s["q0_ready"], 1)
                dve.wait_ge(s["unit_full"], pos + U_K + 1 + 1)
                v.tensor_scalar(KT[:, 1, :], T(U_K + 1), inv[:, 1:2], bk[:, 1:2], ALU.mult, ALU.add).then_inc(s["dve_empty"], 1)
                for c in range(2):
                    dve.wait_ge(s["unit_full"], pos + U_V + c + 1)
                    src = T(U_V + c).rearrange("p (w o j d) -> p w o j d", w=2, j=8, o=2)
                    for o in range(2):
                        for w in range(2):
                            i = v.tensor_copy(VB[par][64 * o:64 * o + 64, 2 * c + w, :, HD * o:HD * o + HD],
                                              src[64 * o:64 * o + 64, w, o, :, :])
                    i.then_inc(s["dve_empty"], 1)

            def soft(n, par):
                e = E[par].rearrange("p g k c -> p (g k) c")
                sv = S.rearrange("p g (k c) -> p (g k) c", c=WIN)
                flat = "p g k -> p (g k)"
                dve.wait_ge(s["s_full"], n + 1)
                v.tensor_reduce(smx[:, :, :].rearrange(flat), sv, AX, ALU.max).then_inc(s["s_max"], 1)
                dve.wait_ge(s["s_max"], n + 1)
                v.tensor_tensor(e, sv, smx[:, :, :].rearrange(flat).unsqueeze(2).to_broadcast([P, 32, WIN]),
                                ALU.subtract).then_inc(s["s_taken"], 1)
                dve.wait_ge(s["g_full"], n + 1)
                v.tensor_reduce(gmx[:, :], G[0:NH, :], AX, ALU.max, negate=True).then_inc(s["g_max"], 1)
                dve.wait_ge(s["s_exp"], n + 1)
                v.tensor_reduce(ssum[:, :, :].rearrange(flat), e, AX, ALU.add).then_inc(s["soft_sum"], 1)
                dve.wait_ge(s["soft_sum"], n + 1)
                v.reciprocal(srec[:, :, :], ssum[:, :, :]).then_inc(s["s_summed"], 1)
                dve.wait_ge(s["g_exp"], n + 1)
                v.reciprocal(grec[:, :], gsum[:, :]).then_inc(s["g_rec"], 1)
                dve.wait_ge(s["g_rec"], n + 1)
                v.tensor_scalar(gs[0:NH, :], gs[0:NH, :], grec[:, :], None, ALU.mult).then_inc(s["g_ready"], 1)

            def part2(n, par, between=None):
                pos = place(2, n)
                dve.wait_ge(s["u_high"], n + 1)
                usl = slice(n, n + 1) if isinstance(n, int) else bass.ds(n, 1)
                v.tensor_tensor(uT[1][:, :, usl, :].rearrange("p k o e -> p k (o e)"),
                                T(U_U)[:, 0:KD * NH].rearrange("p (k e) -> p k e", e=NH),
                                uT[0][:, :, usl, :].rearrange("p k o e -> p k (o e)"), ALU.subtract).then_inc(s["dve_empty"], 1)
                if between is not None:
                    between()
                for j in (1, 3):
                    dve.wait_ge(s["unit_full"], pos + U_PT + j + 1)
                    v.tensor_copy(PT[:, j], T(U_PT + j).rearrange("p (g q) -> p g q", g=4)).then_inc(s["dve_empty"], 1)
                dve.wait_ge(s["ctx_high"], n + 1)
                src = T(U_AV).rearrange("p (m w q) -> p m w q", m=KD, w=TB)
                for m in range(KD):
                    i = v.tensor_tensor(cT[1][:, m, :, 1:1 + WIN], src[:, m], cT[0][:, m, :, 1:1 + WIN], ALU.subtract)
                i.then_inc(s["dve_empty"], 1)
                for c in range(2):
                    dve.wait_ge(s["unit_full"], pos + U_WO + c + 1)
                    dve.wait_ge(s["xb_made"], n + 1)
                    dst = xb[par][:, 2 * c:2 * c + 2, :].rearrange("p t d -> p (t d)")
                    i = v.scalar_tensor_tensor(out=dst, in0=T(U_WO + c), scalar=der[:, D_O:D_O + 1], in1=dst,
                                               op0=ALU.mult, op1=ALU.add)
                    i.then_inc(s["dve_empty"], 1)

            for name in ("h_done", "y_done"):
                signal(name, 2)

            dve.wait_ge(s["attn_w_in"], 80)
            v.tensor_reduce(mx[:, 0:4], wa_raw.rearrange("p i k d -> p i (k d)"), AX, ALU.max,
                            apply_absolute_value=True).then_inc(s["attn_max"], 1)
            v.tensor_reduce(mx[:, 4:5], wr_raw.rearrange("p k e -> p (k e)"), AX, ALU.max,
                            apply_absolute_value=True).then_inc(s["attn_max"], 1)
            scales(0, 5, "attn_all_max", 1)
            signal("scale_ready")
            dve.wait_ge(s["consts_in"], 32)
            dve.wait_ge(s["bias_in"], 48)
            for o, c in ((0, C_EVEN), (1, C_ODD)):
                link(v.tensor_scalar(der[:, D_QE + o:D_QE + o + 1], cf[:, c:c + 1], inv[:, 0:1], HD ** -0.5, ALU.mult, ALU.mult))
                link(v.tensor_scalar(bqp[:, o, :], bq[:, :], cf[:, c:c + 1], HD ** -0.5, ALU.mult, ALU.mult))
            link(v.tensor_tensor(der[:, D_O:D_O + 1], inv[:, 2:3], inv[:, 3:4], ALU.mult))
            for m in range(KD):
                link(v.tensor_scalar(bvm[:, m, :], cf[:, C_TOK:C_TOK + P], bv[:, m:m + 1], None, ALU.mult))
            signal("setup")
            dve.wait_ge(s["bias_psum"], 1)
            link(v.tensor_tensor(bias_tile[:, :], ps[:, 4, 0:D], bias_tile[:, :], ALU.add))
            v.tensor_copy(bv_out[:, :], ps[0:B, 4, D:2 * D]).then_inc(s["bias_ready"], 1)
            ln(0, 0, False)
            for i in range(4):
                dve.wait_ge(s["attn_high"], i + 1)
                v.scalar_tensor_tensor(out=wa[1][:, i].rearrange("p k d -> p (k d)"), in0=wa_raw[:, i].rearrange("p k d -> p (k d)"),
                                       scalar=scl[:, i:i + 1], in1=wa[0][:, i].rearrange("p k d -> p (k d)"),
                                       op0=ALU.mult, op1=ALU.subtract)
            dve.wait_ge(s["attn_high"], 5)
            v.scalar_tensor_tensor(out=wr[1][:, :, :], in0=wr_raw, scalar=scl[:, 4:5], in1=wr[0][:, :, :],
                                   op0=ALU.mult, op1=ALU.subtract).then_inc(s["attn_low"], 1)
            part1(0, 0)
            ln(1, 1, False)
            dve.wait_ge(s["shared_w_in"], 48)
            v.tensor_reduce(mx[:, 5:7], w12_raw.rearrange("p i k h -> p i (k h)"), AX, ALU.max,
                            apply_absolute_value=True).then_inc(s["shared_max"], 1)
            v.tensor_reduce(mx[:, 7:8], w3_raw.rearrange("p c d -> p (c d)"), AX, ALU.max,
                            apply_absolute_value=True).then_inc(s["shared_max"], 1)
            scales(5, 8, "shared_all_max", 1)
            link(v.tensor_scalar(der[:, D_HS:D_HS + 1], scl[:, 5:6], 2.0 ** -15, None, ALU.mult))
            link(v.tensor_tensor(der[:, D_Y:D_Y + 1], inv[:, 5:6], inv[:, 6:7], ALU.mult))
            link(v.tensor_scalar(der[:, D_Y:D_Y + 1], der[:, D_Y:D_Y + 1], inv[:, 7:8], 2.0 ** 15, ALU.mult, ALU.mult))
            signal("scale_ready")
            for i in range(2):
                dve.wait_ge(s["shared_high"], i + 1)
                v.scalar_tensor_tensor(out=w12[1][:, i].rearrange("p k d -> p (k d)"), in0=w12_raw[:, i].rearrange("p k d -> p (k d)"),
                                       scalar=scl[:, 5 + i:6 + i], in1=w12[0][:, i].rearrange("p k d -> p (k d)"),
                                       op0=ALU.mult, op1=ALU.subtract)
            dve.wait_ge(s["shared_high"], 3)
            v.scalar_tensor_tensor(out=w3[1][:, :, :], in0=w3_raw, scalar=scl[:, 7:8], in1=w3[0][:, :, :],
                                   op0=ALU.mult, op1=ALU.subtract).then_inc(s["shared_low"], 1)
            soft(0, 0)
            part1(1, 1)
            dve.wait_ge(s["pads_ready"], 1)
            part2(0, 0, lambda: ln(2, 0, True))
            soft(1, 1)

            def turn(n, par):
                part1(n, par)
                part2(n - 1, 1 - par, lambda: ln(n + 1, 1 - par, True))
                soft(n, par)

            pairs(dve, turn, 2, B - 2)
            turn(B - 2, 0)
            part1(B - 1, 1)
            part2(B - 2, 0)
            soft(B - 1, 1)
            part2(B - 1, 1)

            dve.wait_ge(s["c0_full"], 1)
            for m in range(KD):
                src = ps[:, 6, m * P:(m + 1) * P].rearrange("p (b h) -> p b h", h=NH)
                link(v.tensor_tensor(c0m[:, :, :], src, cf[:, C_HM + m * NH:C_HM + (m + 1) * NH].unsqueeze(1).to_broadcast([P, B, NH]), ALU.mult))
                link(v.tensor_reduce(c0f[:, m, :], c0m[:, :, :], AX, ALU.add))
            link(v.tensor_copy(c0[0][:, :, :], c0f[:, :, :]))
            v.tensor_tensor(c0[1][:, :, :], c0f[:, :, :], c0[0][:, :, :], ALU.subtract).then_inc(s["c0_ready"], 1)
            dve.wait_ge(s["out0_full"], 1)
            v.scalar_tensor_tensor(out=out0[:, :], in0=ps[0:B, 7, 0:D], scalar=der[0:B, D_O:D_O + 1], in1=bv_out[:, :],
                                   op0=ALU.mult, op1=ALU.add).then_inc(s["out0_ready"], 1)

            def chunk(b, c):
                n, q = b * SC + c, c % 2
                dve.wait_ge(s["silu_done"], n + 1)
                v.scalar_tensor_tensor(out=s_h[q], in0=ps[:, 2 * q + 1, :], scalar=der[:, D_HS:D_HS + 1], in1=s_silu[q],
                                       op0=ALU.mult, op1=ALU.mult).then_inc(s["h_done"], 1)
                dve.wait_ge(s["hh_high"], n + 1)
                v.tensor_tensor(s_hh[1][q], s_h[q], s_hh[0][q], ALU.subtract).then_inc(s["hh_low"], 1)

            def shared_out(b, par):
                dve.wait_ge(s["y_full"], b + 1)
                dve.wait_ge(s[f"y_in{par}"], (b + (-par)) * 8 + 16)
                y = s_y[par].rearrange("p t d -> p (t d)")
                v.scalar_tensor_tensor(out=y, in0=ps[:, 4 + 2 * par:6 + 2 * par, :].rearrange("p a d -> p (a d)"),
                                       scalar=der[:, D_Y:D_Y + 1], in1=y, op0=ALU.mult, op1=ALU.add).then_inc(s["y_done"], 1)

            before = ps[:, 6, :].rearrange("p (e t) -> p e t", e=NE)
            total = ps[:, 7, :].rearrange("p (e t) -> p e t", e=NE)
            need, ends, first = (x[:, :] for x in tl)
            by_token = "p e t -> p t e"

            def best_scores():
                dve.wait_ge(s["scores_ready"], 1)
                link(v.tensor_tensor(sel, sc_, eb[:, :].unsqueeze(1).to_broadcast([P, NTOK, NE]), ALU.add))
                for t in range(NTOK):
                    i = v.max(mx8[:, t, :], sel[:, t, :])
                link(i)

            def best_experts():
                for t in range(NTOK):
                    i = v.max_index(ix8[:, t, :], mx8[:, t, :], sel[:, t, :])
                link(i)
                link(v.tensor_copy(ixf[:, :, :], ix8[:, :, 0:2]))

            def one_hots():
                ie = cf[:, C_IE:C_IE + NE].unsqueeze(1).to_broadcast([P, NTOK, NE])
                for k, oh in ((0, oh1), (1, oh2)):
                    link(v.tensor_tensor(oh, ie, ixf[:, :, k:k + 1].to_broadcast([P, NTOK, NE]), ALU.is_equal))
                v.tensor_tensor(ohm.rearrange(by_token), oh1, oh2, ALU.add).then_inc(s["chosen_ready"], 1)

            def gates():
                for k, oh in ((0, oh1), (1, oh2)):
                    link(v.tensor_tensor(tmp, oh, sc_, ALU.mult))
                    link(v.tensor_reduce(gate[:, k, :], tmp, AX, ALU.add))

            def groups():
                link(v.memset(restart, 1.0))
                link(v.memset(restart[:, :, 0:1], 0.0))
                dve.wait_ge(s["prefix_full"], 2)
                flat = "p e t -> p (e t)"
                link(v.tensor_tensor_scan(cum.rearrange(flat), restart.rearrange(flat), total.rearrange(flat), 0.0, ALU.mult, ALU.add))
                link(v.tensor_scalar(need, cum[:, :, NTOK - 1], P - 1.0, 1.0 / P, ALU.add, ALU.mult))
                link(v.tensor_scalar(need, need, -0.5 + 0.5 / P, 2.0 ** 23, ALU.add, ALU.add))
                link(v.tensor_scalar(need, need, -(2.0 ** 23), None, ALU.add))
                link(v.tensor_tensor_scan(ends, restart[:, 0, 1:1 + NE], need, 0.0, ALU.mult, ALU.add))
                link(v.tensor_tensor(first, ends, need, ALU.subtract))
                link(v.tensor_scalar(first, first, float(P), None, ALU.mult))

            def positions():
                link(v.tensor_tensor(posn, cum, total, ALU.subtract))
                link(v.tensor_tensor(posn, before, posn, ALU.add))
                link(v.tensor_tensor(posn, posn, first.unsqueeze(2).to_broadcast([P, NE, NTOK]), ALU.add))

            def slots_of_tokens():
                for k, oh in ((0, oh1), (1, oh2)):
                    link(v.tensor_tensor(tmp, oh, posn.rearrange(by_token), ALU.mult))
                    link(v.tensor_reduce(slf[:, k, :], tmp, AX, ALU.add))
                v.tensor_copy(slots[:, :, :], slf[:, :, :]).then_inc(s["slots_ready"], 1)

            def expert_table():
                link(v.tensor_tensor(ecount[:, :, :], ends[0:1].unsqueeze(1).to_broadcast([1, NT, NE]),
                                     cf[0:1, C_IS:C_IS + NT].unsqueeze(2).to_broadcast([1, NT, NE]), ALU.is_le))
                link(v.tensor_reduce(ef[:, :], ecount[:, :, :], AX, ALU.add))
                link(v.tensor_scalar(ef[:, :], ef[:, :], NE - 1.0, 2.0 * EXPERT, ALU.min, ALU.mult))
                v.tensor_copy(etab[:, :], ef[:, :]).then_inc(s["table_ready"], 1)
                signal("route")

            chunk(0, 0)
            best_scores()
            chunk(0, 1)
            best_experts()
            chunk(0, 2)
            one_hots()
            chunk(0, 3)
            chunk(0, 4)
            groups()
            chunk(0, 5)
            positions()
            chunk(0, 6)
            slots_of_tokens()
            chunk(0, 7)
            gates()
            shared_out(0, 0)
            expert_table()
            for c in range(SC):
                chunk(1, c)
            shared_out(1, 1)

            def largest(e):
                raw = arena[:, (e + 1) * EXPERT:(e + 2) * EXPERT]
                r12 = raw[:, 0:2 * KD * RH].rearrange("p (k i h) -> p i k h", k=KD, i=2)
                v.tensor_reduce(rmx[:, 0:2, e], r12, mybir.AxisListType.XY, ALU.max, apply_absolute_value=True).then_inc(s["routed_each"], 1)
                v.tensor_reduce(rmx[:, 2:3, e], raw[:, 2 * KD * RH:], AX, ALU.max, apply_absolute_value=True).then_inc(s["routed_each"], 1)

            dve.wait_ge(s["raw_in_early"], 48 * E_EARLY)
            for c in range(SC):
                chunk(2, c)
                largest(c)
            shared_out(2, 0)
            for c in range(SC):
                chunk(3, c)
                if c < 2:
                    largest(SC + c)
                if 4 <= c < 7:
                    if c == 4:
                        dve.wait_ge(s["raw_in_late"], 48 * (NE - E_EARLY))
                    largest(E_EARLY + 2 * (c - 4))
                    largest(E_EARLY + 2 * (c - 4) + 1)
            dve.wait_ge(s["routed_each"], 2 * NE)
            v.tensor_reduce(mx[:, 8:11], rmx[:, :, :], AX, ALU.max).then_inc(s["routed_max"], 1)
            shared_out(3, 1)
            scales(8, 11, "routed_all_max", 1)
            link(v.tensor_scalar(der[:, D_RHS:D_RHS + 1], scl[:, 8:9], 2.0 ** -15, None, ALU.mult))
            link(v.tensor_tensor(der[:, D_RY:D_RY + 1], inv[:, 8:9], inv[:, 9:10], ALU.mult))
            link(v.tensor_scalar(der[:, D_RY:D_RY + 1], der[:, D_RY:D_RY + 1], inv[:, 10:11], 2.0 ** 15, ALU.mult, ALU.mult))
            signal("routed_low")
            signal("scale_ready")

            def low_parts(b, par):
                for c in range(SC):
                    chunk(b, c)
                    dve.wait_ge(s["routed_high"], b * SC + (c + 1 - 4 * SC))
                    raw = lambda lo, n: arena[:, bass.ds(b * (SC * EXPERT) + ((c + 1 - 4 * SC) * EXPERT + lo), n)]
                    part = lambda w, lo, n: ar16[:, bass.ds(b * (2 * SC * EXPERT) + ((2 * (c - 4 * SC) + w) * EXPERT + lo), n)]
                    for i in range(2):
                        lo, r, hi = (z.rearrange("p (k i h) -> p k i h", k=KD, i=2)[:, :, i]
                                     for z in (part(1, 0, 2 * KD * RH), raw(0, 2 * KD * RH), part(0, 0, 2 * KD * RH)))
                        v.scalar_tensor_tensor(out=lo, in0=r, scalar=scl[:, 8 + i:9 + i], in1=hi, op0=ALU.mult, op1=ALU.subtract)
                    at_ = (2 * KD * RH, 2 * D)
                    v.scalar_tensor_tensor(out=part(1, *at_), in0=raw(*at_), scalar=scl[:, 10:11], in1=part(0, *at_),
                                           op0=ALU.mult, op1=ALU.subtract).then_inc(s["routed_low"], 1)
                shared_out(b, par)

            pairs(dve, low_parts, 4, B_FIRST)

            def x_low(r, par):
                dve.wait_ge(s["rx_high"], r + 1)
                v.tensor_tensor(r_x[1][par], ps[:, 2 + par, :], r_x[0][par], ALU.subtract).then_inc(s["rx_low"], 1)

            def gated(r, par):
                for j in range(2):
                    dve.wait_ge(s["r_silu_done"], 2 * r + j + 1)
                    v.scalar_tensor_tensor(out=r_h[par][:, j * RH:(j + 1) * RH], in0=ps[:, j, RH:2 * RH], scalar=der[:, D_RHS:D_RHS + 1],
                                           in1=r_silu[j], op0=ALU.mult, op1=ALU.mult).then_inc(s["r_h_done"], 1)

            def h_low(r, par):
                dve.wait_ge(s["rh_high"], r + 1)
                v.tensor_tensor(r_hh[1][par], ps[:, 4 + par, :], r_hh[0][par], ALU.subtract).then_inc(s["rh_low"], 1)

            x_low(0, 0)
            x_low(1, 1)
            gated(0, 0)

            def routed(r, par):
                x_low(r + 1, 1 - par)
                gated(r, par)
                h_low(r - 1, 1 - par)

            routed(1, 1)
            pairs(dve, routed, 2, NR - 2)
            routed(NR - 2, 0)
            gated(NR - 1, 1)
            h_low(NR - 2, 0)
            h_low(NR - 1, 1)
            def combine(t):
                b = t // TB
                y = (c_y[b] if b < B_FIRST else s_y[b % 2])[:, t % TB, :]
                if t % TB == 0:
                    dve.wait_ge(pick_in[b], 16 * 2 * TB)
                v.scalar_tensor_tensor(out=y, in0=picked[:, 0, t, :], scalar=gate[:, 0, t:t + 1], in1=y,
                                       op0=ALU.mult, op1=ALU.add).then_inc(s["one_added"], 1)
                dve.wait_ge(s["one_added"], t + 1)
                v.scalar_tensor_tensor(out=y, in0=picked[:, 1, t, :], scalar=gate[:, 1, t:t + 1], in1=y,
                                       op0=ALU.mult, op1=ALU.add).then_inc(s["mixed"], 1)

            done = 0
            for b in range(B_FIRST, B):
                for c in range(SC):
                    chunk(b, c)
                    if c % 2 == 1 and (b > B_FIRST or c > 1):
                        if done == 0:
                            dve.wait_ge(s["base_in"], 16 * B_FIRST)
                        for t in range(done, done + 3):
                            combine(t)
                        done += 3
                shared_out(b, b % 2)
            dve.wait_ge(s["y_done"], B + 2)
            for t in range(done, NTOK):
                combine(t)

        @block.tensor
        def _(pe):
            mm = nc.tensor.matmul
            pe.wait_ge(s["attn_w_in"], 80)
            pe.wait_ge(s["setup"], 1)
            for m in range(KD):
                mm(ps[:, 4, 0:D], bvm[:, m, :], wa_raw[:, 3, m, :], start=(m == 0), stop=(m == KD - 1))
            for m in range(KD):
                i = mm(ps[0:B, 4, D:2 * D], bvm[:, m, 1:1 + B], wa_raw[:, 3, m, :], start=(m == 0), stop=(m == KD - 1))
            i.then_inc(s["bias_psum"], 1)

            def claim(part, n, u):
                kinds = PART1 if part == 1 else PART2
                if u >= RING:
                    who = kinds[u - RING]
                    pe.wait_ge(s["act_empty" if who == "A" else "dve_empty"], emptied(who, part, n, u - RING))
                elif not (part == 1 and isinstance(n, int) and n == 0):
                    pe.wait_ge(s["dve_empty"], emptied_before("D", part, n) - (RING - 1 - u))

            def part1(n, par):
                nsl = slice(XPAD + n * L, XPAD + (n + 1) * L) if isinstance(n, int) else bass.ds(n * L + XPAD, L)
                xk = lambda x, k: xT[x][:, k, nsl]
                pe.wait_ge(s["xn_made"], n + 1)
                for k in range(KD):
                    claim(1, n, U_XT + k)
                    for t in range(TB):
                        i = nc.tensor.transpose(T(U_XT + k)[:, t * P:(t + 1) * P], xnr[par][:, t, k * P:(k + 1) * P], ident)
                    i.then_inc(s["unit_full"], 1)
                claim(1, n, U_R)
                pe.wait_ge(s["dve_empty"], emptied("D", 1, n, U_XT + 1))
                for t in range(TB):
                    for j, (x, w) in enumerate(((0, 0), (0, 1), (1, 0))):
                        for k in range(KD):
                            tsl = slice(XPAD + n * L + t * P, XPAD + n * L + (t + 1) * P) if isinstance(n, int) else bass.ds(n * L + (XPAD + t * P), P)
                            i = mm(T(U_R)[:, t * NE:(t + 1) * NE], xT[x][:, k, tsl], wr[w][:, k, :],
                                   start=(j == 0 and k == 0), stop=(j == 2 and k == KD - 1))
                i.then_inc(s["unit_full"], 1)
                for m in range(KD):
                    claim(1, n, U_Q + m)
                    for j, (w, x) in enumerate(SPLIT):
                        for k in range(KD):
                            rhs = xk(x, k).rearrange("p (w c) -> p w c", w=TB)[:, :, 0:WIN + 1]
                            i = mm(T(U_Q + m)[:, 0:TB * (WIN + 1)].rearrange("p (w c) -> p w c", w=TB),
                                   wa[w][:, 0, k, m * P:(m + 1) * P], rhs, start=(j == 0 and k == 0), stop=(j == 2 and k == KD - 1))
                    i.then_inc(s["unit_full"], 1)
                for m in range(KD):
                    claim(1, n, U_K + m)
                    for j, (w, x) in enumerate(SPLIT):
                        for k in range(KD):
                            i = mm(T(U_K + m), wa[w][:, 1, k, m * P:(m + 1) * P], xk(x, k),
                                   start=(j == 0 and k == 0), stop=(j == 2 and k == KD - 1))
                    i.then_inc(s["unit_full"], 1)
                for c in range(2):
                    claim(1, n, U_V + c)
                    for w2 in range(2):
                        o = (2 * c + w2) * STRIDE + 1
                        for par2 in range(2):
                            at_ = XPAD + o - WIN * par2
                            rows = P - 1 + par2
                            wsl = slice(n * L + at_, n * L + at_ + rows) if isinstance(n, int) else bass.ds(n * L + at_, rows)
                            dst = T(U_V + c)[0:rows, w2 * D + par2 * P:w2 * D + (par2 + 1) * P].rearrange("p (j d) -> p j d", d=HD)
                            for j, (w, x) in enumerate(SPLIT):
                                for k in range(KD):
                                    i = mm(dst, xT[x][:, k, wsl],
                                           wa[w][:, 2, k, :].rearrange("p (j o d) -> p o j d", o=2, d=HD)[:, par2],
                                           start=(j == 0 and k == 0), stop=(j == 2 and k == KD - 1))
                    i.then_inc(s["unit_full"], 1)
                pe.wait_ge(s["act_empty"], emptied("A", 1, n, U_K))
                pe.wait_ge(s["dve_empty"], emptied("D", 1, n, U_K + 1))
                if not (isinstance(n, int) and n == 0):
                    pe.wait_ge(s["s_taken"], n)
                for w in range(TB):
                    for m in range(KD):
                        for o in range(2):
                            for g in range(4):
                                row = slice(32 * g, 32 * g + 32)
                                col = (((w // 2) * 2 + m) * 2 + o) * WIN
                                i = mm(S[64 * (w % 2):64 * (w % 2) + 64, g, col:col + WIN],
                                       QT[o][row, m, w * (WIN + 1) + 1:(w + 1) * (WIN + 1)],
                                       KT[row, m, w * STRIDE + 1:w * STRIDE + 1 + WIN], start=True, stop=True)
                i.then_inc(s["s_full"], 1)
                pe.wait_ge(s["q0_ready"], n + 1)
                if isinstance(n, int) and n == 0:
                    pe.wait_ge(s["bias_ready"], 1)
                else:
                    pe.wait_ge(s["g_exp"], n)
                for m in range(KD):
                    i = mm(G[0:NH, :], q0[:, m, :], KT[:, m, :], start=(m == 0), stop=(m == KD - 1))
                i.then_inc(s["g_full"], 1)

            def part2(n, par):
                claim(2, n, U_GT)
                pe.wait_ge(s["g_ready"], n + 1)
                for t in range(TB):
                    i = mm(T(U_GT)[:, t * NH:(t + 1) * NH], gs[0:NH, t * P:(t + 1) * P], ident[0:NH, 0:NH], start=True, stop=True)
                i.then_inc(s["unit_full"], 1)
                claim(2, n, U_U)
                pe.wait_ge(s["act_empty"], emptied("A", 2, n, U_GT))
                for k in range(KD):
                    for t in range(TB):
                        i = mm(T(U_U)[:, k * NH:(k + 1) * NH], xnr[par][:, t, k * P:(k + 1) * P], gp[:, t, :],
                               start=(t == 0), stop=(t == TB - 1))
                i.then_inc(s["unit_full"], 1)
                pe.wait_ge(s["p_ready"], n + 1)
                for j in range(4):
                    claim(2, n, U_PT + j)
                    for g in range(4):
                        src = E[par][:, g, 2 * j:2 * j + 2, :].rearrange("p o c -> p (o c)")
                        i = nc.tensor.transpose(T(U_PT + j)[:, g * P:(g + 1) * P], src, ident)
                    i.then_inc(s["unit_full"], 1)
                claim(2, n, U_AV)
                pe.wait_ge(s["act_empty"], emptied("A", 2, n, U_PT + 2))
                pe.wait_ge(s["dve_empty"], emptied("D", 2, n, U_PT + 3))
                for m in range(KD):
                    for w in range(TB):
                        for g in range(4):
                            i = mm(T(U_AV)[32 * g:32 * g + 32, (m * TB + w) * WIN:(m * TB + w + 1) * WIN],
                                   VB[par][:, w, 4 * m + g, :], PT[:, (w // 2) * 2 + m, g, (w % 2) * WIN:(w % 2 + 1) * WIN],
                                   start=True, stop=True)
                i.then_inc(s["unit_full"], 1)
                for c in range(2):
                    claim(2, n, U_WO + c)
                    if c == 0:
                        pe.wait_ge(s["dve_empty"], emptied("D", 2, n, U_AV))
                    for t2 in range(2):
                        for j, (w, x) in enumerate(SPLIT):
                            for m in range(KD):
                                i = mm(T(U_WO + c)[:, t2 * D:(t2 + 1) * D], cT[x][:, m, 2 * c + t2, :], wa[w][:, 3, m, :],
                                       start=(j == 0 and m == 0), stop=(j == 2 and m == KD - 1))
                    i.then_inc(s["unit_full"], 1)

            pe.wait_ge(s["attn_low"], 1)
            pe.wait_ge(s["pads_ready"], 1)
            part1(0, 0)
            part1(1, 1)
            part2(0, 0)

            def turn(n, par):
                part1(n, par)
                part2(n - 1, 1 - par)

            pairs(pe, turn, 2, B)
            part2(B - 1, 1)

            def up(b, c):
                n, q = b * SC + c, c % 2
                pe.wait_ge(s["h_done"], n + 1)
                bsl = slice(XPAD + b * L, XPAD + (b + 1) * L) if isinstance(b, int) else bass.ds(b * L + XPAD, L)
                for i2 in range(2):
                    for j, (w, x) in enumerate(SPLIT):
                        for k in range(KD):
                            i = mm(ps[:, 2 * q + i2, :], w12[w][:, i2, k, c * P:(c + 1) * P], xT[x][:, k, bsl],
                                   start=(j == 0 and k == 0), stop=(j == 2 and k == KD - 1))
                i.then_inc(s["a_full"], 1)

            def down(b, par, c):
                n, q = b * SC + c, c % 2
                if c == 0:
                    pe.wait_ge(s["y_done"], b + 1)
                for j, (x, w) in enumerate(((0, 0), (0, 1), (1, 0))):
                    if j == 0:
                        pe.wait_ge(s["hh_high"], n + 1)
                    if j == 2:
                        pe.wait_ge(s["hh_low"], n + 1)
                    for t in range(TB):
                        i = mm(ps[:, 4 + 2 * par + t // 2, (t % 2) * D:(t % 2 + 1) * D], s_hh[x][q][:, t * P:(t + 1) * P], w3[w][:, c, :],
                               start=(c == 0 and j == 0 and t % 2 == 0), stop=(c == SC - 1 and j == 2), skip_group_check=True)
                if c == SC - 1:
                    i.then_inc(s["y_full"], 1)

            def batch(b, par, last=False):
                for c in range(SC):
                    if c < SC - 1:
                        up(b, c + 1)
                    elif not last:
                        up(b + 1, 0)
                    down(b, par, c)

            pe.wait_ge(s["dve_empty"], emptied("D", 2, B - 1, U_WO + 1))
            for m in range(KD):
                for j, (w, x) in enumerate(SPLIT):
                    for k in range(KD):
                        i = mm(ps[:, 6, m * P:(m + 1) * P], wa[w][:, 2, k, m * P:(m + 1) * P],
                               uT[x][:, k, :, :].rearrange("p b h -> p (b h)"), start=(j == 0 and k == 0), stop=(j == 2 and k == KD - 1))
            i.then_inc(s["c0_full"], 1)
            pe.wait_ge(s["s_taken"], B)
            pe.wait_ge(s["shared_low"], 1)
            up(0, 0)
            pe.wait_ge(s["c0_ready"], 1)
            for j, (w, x) in enumerate(SPLIT):
                for m in range(KD):
                    i = mm(ps[0:B, 7, 0:D], c0[x][:, m, :], wa[w][:, 3, m, :], start=(j == 0 and m == 0), stop=(j == 2 and m == KD - 1))
            i.then_inc(s["out0_full"], 1)
            for c in range(SC):
                up(c // (SC - 1), (c + 1) % SC)
                down(0, 0, c)
                if c == 3:
                    pe.wait_ge(s["chosen_ready"], 1)
                    pe.wait_ge(s["out0_ready"], 1)
                    for i_ in range(2):
                        mm(ps[:, 6 + i_, :], ch[:, i_ * P:(i_ + 1) * P], ohm[:, :, :].rearrange("p e t -> p (e t)"),
                           start=True, stop=True).then_inc(s["prefix_full"], 1)
            pe.wait_ge(s["slots_ready"], 1)
            batch(1, 1)
            pairs(pe, batch, 2, B_FIRST - 2)
            batch(B_FIRST - 2, 0)
            batch(B_FIRST - 1, 1, last=True)

            pe.wait_ge(s["y_done"], B_FIRST + 2)
            pe.wait_ge(s["routed_low"], NE + 1)
            pe.wait_ge(s["table_ready"], 1)

            def x_transposed(r, par, free=True):
                if free:
                    pe.wait_ge(s["rx_low"], r - 1)
                pe.wait_ge(s[f"xs_in{par}"], (r + (-par)) * 8 + 16)
                for j in range(2):
                    for k in range(KD):
                        at_ = (2 * j + k) * P
                        i = nc.tensor.transpose(ps[:, 2 + par, at_:at_ + P], xs[par][:, j, k * P:(k + 1) * P], ident)
                i.then_inc(s["rx_full"], 1)

            def expert_of(t):
                tsl = slice(t, t + 1) if isinstance(t, int) else bass.ds(t, 1)
                return pe.value_load(etab[0:1, tsl], min_val=0, max_val=2 * EXPERT * (NE - 1))

            def gate_up(r, par, free=True):
                pe.wait_ge(s["rx_low"], r + 1)
                for j in range(2):
                    if free:
                        pe.wait_ge(s["r_h_done"], 2 * r + j - 1)
                    e = expert_of(2 * r + j)
                    for n, (x, w) in enumerate(((0, 0), (0, 1), (1, 0))):
                        for k in range(KD):
                            at_ = (2 * j + k) * P
                            i = mm(ps[:, j, :], r_x[x][par][:, at_:at_ + P], ar16[:, bass.ds(e + (w * EXPERT + k * 2 * RH), 2 * RH)],
                                   start=(n == 0 and k == 0), stop=(n == 2 and k == KD - 1))
                    i.then_inc(s["ab_full"], 1)

            def h_transposed(r, par, free=True):
                if free:
                    pe.wait_ge(s["rh_low"], r - 1)
                pe.wait_ge(s["r_h_done"], 2 * r + 2)
                for k in range(2 * RH // P):
                    i = nc.tensor.transpose(ps[:, 4 + par, k * P:(k + 1) * P], r_h[par][:, k * P:(k + 1) * P], ident)
                i.then_inc(s["rh_full"], 1)

            def routed_down(r, par, free=True):
                if free:
                    pe.wait_ge(s["ry_done"], r - 1)
                pe.wait_ge(s["rh_low"], r + 1)
                for j in range(2):
                    e = expert_of(2 * r + j)
                    for n, (x, w) in enumerate(((0, 0), (0, 1), (1, 0))):
                        for k in range(RH // P):
                            at_ = (2 * j + k) * P
                            i = mm(ps[:, 6 + par, j * D:(j + 1) * D], r_hh[x][par][:, at_:at_ + P],
                                   ar16[:, bass.ds(e + (w * EXPERT + 2 * KD * RH + k * D), D)],
                                   start=(n == 0 and k == 0), stop=(n == 2 and k == RH // P - 1))
                i.then_inc(s["ry_full"], 1)

            x_transposed(0, 0, free=False)
            for r in range(4):
                x_transposed(r + 1, (r + 1) % 2, free=r >= 1)
                gate_up(r, r % 2, free=r >= 1)
                if r >= 1:
                    h_transposed(r - 1, (r - 1) % 2, free=r >= 3)
                if r >= 2:
                    routed_down(r - 2, r % 2, free=False)

            def routed(r, par, free=True):
                x_transposed(r + 1, 1 - par)
                gate_up(r, par)
                h_transposed(r - 1, 1 - par)
                routed_down(r - 2, par, free)

            pairs(pe, routed, 4, NR - 2)
            routed(NR - 2, 0)
            gate_up(NR - 1, 1)
            h_transposed(NR - 2, 0)
            routed_down(NR - 3, 1)
            h_transposed(NR - 1, 1)
            routed_down(NR - 2, 0)
            routed_down(NR - 1, 1)
            pe.wait_ge(s["ry_done"], NR)
            up(B_FIRST, 0)
            batch(B_FIRST, 0)
            batch(B - 1, 1, last=True)


_INS = ['L0_attn_hidden_states', 'L0_attn_Wq', 'L0_attn_bq', 'L0_attn_Wk', 'L0_attn_bk', 'L0_attn_Wv', 'L0_attn_bv',
        'L0_attn_Wo', 'L0_attn_bo', 'L0_ffn_router_w', 'L0_ffn_expert_bias', 'L0_ffn_shared_w1', 'L0_ffn_shared_w2',
        'L0_ffn_shared_w3', 'L0_ffn_routed_w1', 'L0_ffn_routed_w2', 'L0_ffn_routed_w3']


def kernel(**inputs):
    import numpy as _np
    import concourse.bacc as _bacc
    from concourse import mybir as _mybir
    from concourse.bass_utils import run_bass_kernel_spmd as _run

    nc = _bacc.Bacc("TRN2", target_bir_lowering=False, num_devices=1)
    arrays, args = {}, {}
    f32, f16 = constants()
    given = {name: _np.ascontiguousarray(inputs[name]) for name in _INS}
    columns = _np.ascontiguousarray(_np.stack([given[f"L0_attn_b{c}"].reshape(KD, P) for c in "qkv"]).reshape(3 * KD, P).T)
    for name, x in {**given, "bias_columns": columns, "const_f32": f32, "const_f16": f16}.items():
        arrays[f"in_{name}_dram"] = x
        args[name] = nc.dram_tensor(f"in_{name}_dram", x.shape, _mybir.dt.from_np(x.dtype), kind="ExternalInput").ap()
    out = nc.dram_tensor("out_0_dram", (B, L, D), _mybir.dt.float32, kind="ExternalOutput").ap()
    moe_layer(nc, args, out)
    r = _run(nc, [arrays], core_ids=[0])
    return r.results[0]["out_0_dram"]
```

```python
from contextlib import ExitStack

import numpy as np
import concourse.bass as bass
from concourse import mybir

P = 128
B, L, D = 8, 512, 256
KD = D // P
TB = L // P
NTOK = B * TB
NH, HD = 16, 16
WIN, STRIDE = 64, 128
NE, RH = 16, 256
SH = 1024
SC = SH // P
NT = (B * L * 2) // P + NE
E_EARLY = 10
GROUPS = 4
E_ROUTE = 3
NR = NT // 2
EXPERT = 2 * KD * RH + (RH // P) * D
B_FIRST = 6
B_SPLIT = B_FIRST - NE // SC
LAG = 5
EPS = 1e-5
TOP = 64.0

F32, F16 = mybir.dt.float32, mybir.dt.float16
U32, I32 = mybir.dt.uint32, mybir.dt.int32
ALU = mybir.AluOpType
ACT = mybir.ActivationFunctionType
AX = mybir.AxisListType.X
RMAX = bass.bass_isa.ReduceOp.max

C_ID, C_EVEN, C_ODD, C_TOK, C_IE, C_HM, C_PW, C_IS = 0, 128, 129, 130, 258, 274, 306, 310
C_N = C_IS + NT


def constants():
    c = np.zeros((P, C_N), np.float32)
    p = np.arange(P)
    c[:, C_ID:C_ID + P] = np.eye(P)
    c[:, C_EVEN] = (p // HD) % 2 == 0
    c[:, C_ODD] = (p // HD) % 2 == 1
    c[:, C_TOK:C_TOK + P] = (p >= 1) & (p <= WIN)
    c[:, C_IE:C_IE + NE] = np.arange(NE)
    for m in range(KD):
        c[:, C_HM + m * NH:C_HM + (m + 1) * NH] = ((m * P + p)[:, None] // HD) == np.arange(NH)
    c[:, C_PW:C_PW + 4] = -0.5
    c[:, C_IS:C_IS + NT] = np.arange(NT)
    h = np.zeros((P, 2 * P), np.float16)
    h[:, 0:P] = p[:, None] < p[None, :]
    h[:, P:] = 1.0
    return c, h


UNITS = (("router", 0, "A"), ("q0", 0, "A"), ("q1", 0, "D"), ("p0", -1, "A"), ("k0", 0, "A"), ("k1", 0, "D"),
         ("u", -1, "D"), ("v0", 0, "D"), ("v1", 0, "D"), ("pT0", -1, "A"), ("pT1", -1, "D"), ("pT2", -1, "A"),
         ("pT3", -1, "D"), ("xT0", 1, "D"), ("xT1", 1, "D"), ("ctx", -1, "D"), ("out0", -1, "D"), ("out1", -1, "D"))
WHO = {name: who for name, _, who in UNITS}
ORDER = [("xT0", 0), ("xT1", 0)] + [(name, n + back) for n in range(B + 1) for name, back, _ in UNITS if 0 <= n + back < B]
RING = 3
LOOP_FROM, LOOP_TO = 3, 7


def by_batch(f, b):
    if isinstance(b, int):
        return f(b)
    step = f(LOOP_FROM + 2) - f(LOOP_FROM + 1)
    return b * step + (f(LOOP_FROM + 1) - (LOOP_FROM + 1) * step)


def made(name, b):
    return by_batch(lambda k: ORDER.index((name, k)) + 1, b)


def emptied(name, b):
    return by_batch(lambda k: sum(WHO[u] == WHO[name] for u, _ in ORDER[:ORDER.index((name, k)) + 1]), b)


def bank(name, b):
    return 5 + ORDER.index((name, b if isinstance(b, int) else LOOP_FROM + 1)) % RING


def last_in_bank(name, b):
    at = ORDER.index((name, b if isinstance(b, int) else LOOP_FROM + 1)) - RING
    if at < 0:
        return None
    who = WHO[ORDER[at][0]]
    return who, by_batch(lambda k: sum(WHO[u] == who for u, _ in ORDER[:ORDER.index((name, k)) - RING + 1]), b)


def moe_layer(nc, a, out):
    with ExitStack() as ctx:
        def sb(name, shape, dt=F32):
            return ctx.enter_context(nc.sbuf_tensor(name, shape, dt))[:]

        def sem(name):
            return ctx.enter_context(nc.semaphore(name))

        xs_dram = nc.dram_tensor("rows_by_slot", (NT * P, D), F32, kind="Internal").ap()
        ys_dram = nc.dram_tensor("routed_by_slot", (NT * P, D), F32, kind="Internal").ap()
        y1_dram = nc.dram_tensor("x_plus_attention", (B * L, D), F32, kind="Internal").ap()
        y2_dram = nc.dram_tensor("plus_shared", (B * L, D), F32, kind="Internal").ap()
        x_rows = a["L0_attn_hidden_states"].rearrange("b (t p) d -> b p t d", p=P)
        xs_pairs = xs_dram.rearrange("(r t p) d -> r p t d", p=P, t=2)
        ys_pairs = ys_dram.rearrange("(r t p) d -> r p t d", p=P, t=2)
        y1_rows = y1_dram.rearrange("(b t p) d -> b p t d", p=P, t=TB)
        y2_rows = y2_dram.rearrange("(b t p) d -> b p t d", p=P, t=TB)
        out_rows = out.rearrange("b (t p) d -> b p t d", p=P)

        cf = sb("const_f32", [P, C_N])
        ch = sb("const_f16", [P, 2 * P], F16)
        ident = cf[:, C_ID:C_ID + P]
        wa = [sb(f"attn_w_{x}", [P, 4, KD, D], F16) for x in ("high", "low")]
        wr = [sb(f"router_w_{x}", [P, KD, NE], F16) for x in ("high", "low")]
        w12 = [sb(f"shared_w12_{x}", [P, 2, KD, SH], F16) for x in ("high", "low")]
        w3 = [sb(f"shared_w3_{x}", [P, SC, D], F16) for x in ("high", "low")]
        XPAD = WIN
        xT = [sb(f"xn_T_{x}", [P, KD, XPAD + B * L], F16) for x in ("high", "low")]
        mx = sb("w_max", [P, 12])
        pw = sb("w_pow", [P, 12])
        inv = sb("w_inv", [P, 12])
        scl = sb("w_scale", [P, 12])
        der = sb("w_derived", [P, 12])
        D_QE, D_QO, D_O, D_Y, D_HS, D_RY, D_RHS = range(7)
        bqkv = sb("bqkv_columns", [P, 3 * KD])
        bq, bk, bv = (bqkv[:, i * KD:(i + 1) * KD] for i in range(3))
        bqp = sb("bq_by_parity", [P, 2, KD])
        bias_tile = sb("out_bias", [P, D]); bv_out = sb("bv_times_wo", [B, D])
        eb = sb("expert_bias", [P, NE])
        logits = sb("router_logits", [P, NTOK, NE])
        gate = sb("gates", [P, 2, NTOK])
        slots = sb("slots", [P, 2, NTOK], U32)
        etab = sb("expert_offset_of_tile", [1, NT], I32)
        uT = [sb(f"u_T_{x}", [P, KD, B, NH], F16) for x in ("high", "low")]
        zero = sb("zeros", [P, D])

        arena = sb("arena", [P, (NE + 1) * EXPERT])
        at = [0]

        def cut(*dims, dt=F32):
            n = int(np.prod(dims))
            fl = n if dt == F32 else n // 2
            v = arena[:, at[0]:at[0] + fl]
            at[0] += fl
            if dt != F32:
                v = v.bitcast(dt)
            if len(dims) == 2:
                v = v.rearrange("p (a b) -> p a b", a=dims[0])
            if len(dims) == 3:
                v = v.rearrange("p (a b c) -> p a b c", a=dims[0], b=dims[1])
            return v

        E = [cut(4, 8, WIN) for _ in range(2)]
        route_area = arena[:, 0:2 * 4 * 8 * WIN]
        PT = cut(4, 4, P)
        QT = [cut(KD, TB * (WIN + 1)) for _ in range(2)]
        KT = cut(KD, L)
        VB = [cut(TB, 8, 32) for _ in range(2)]
        xr = [cut(TB, D) for _ in range(2)]
        xb = [cut(TB, D) for _ in range(2)]
        xnr = [cut(TB, D) for _ in range(2)]
        cT = [cut(KD, TB, P, dt=F16) for _ in range(2)]
        assert at[0] <= (NE + 1) * EXPERT - NTOK * D, at[0]
        xn = arena[:, (NE + 1) * EXPERT - NTOK * D:].rearrange("p (t d) -> p t d", t=NTOK)
        group_of = {e: ((e + 2) * EXPERT - ((NE + 1) * EXPERT - NTOK * D) - 1) // D // (NTOK // GROUPS) for e in range(E_EARLY, NE)}
        assert (E_EARLY + 1) * EXPERT <= (NE + 1) * EXPERT - NTOK * D
        ar16 = arena[:, :].bitcast(F16)

        work = sb("work", [P, 2080 + 2 * KD * SH])
        wa_raw = work[:, 0:4 * KD * D].rearrange("p (i k d) -> p i k d", i=4, k=KD)
        wr_raw = work[:, 2048:2048 + KD * NE].rearrange("p (k e) -> p k e", k=KD)
        w12_raw = work[:, 2080:2080 + 2 * KD * SH].rearrange("p (i k h) -> p i k h", i=2, k=KD)
        w3_raw = xn[:, NTOK - SC:, :]
        wat = [0]

        def wcut(n, dt=F32):
            v = work[:, wat[0]:wat[0] + n]
            wat[0] += n
            return v.bitcast(dt) if dt != F32 else v

        s_silu = [wcut(L) for _ in range(2)]
        s_h = [wcut(L) for _ in range(2)]
        s_hh = [[wcut(L // 2, F16) for _ in range(2)] for _ in range(2)]
        s_y = [wcut(TB * D).rearrange("p (t d) -> p t d", t=TB) for _ in range(2)]
        assert wat[0] <= 2080 + 2 * KD * SH
        xs = [wcut(2 * D).rearrange("p (t d) -> p t d", t=2) for _ in range(2)]
        assert wat[0] <= 2080 + 2 * KD * SH, wat[0]
        wat[0] = 0
        r_x = [[wcut(D, F16) for _ in range(2)] for _ in range(2)]
        r_silu = [wcut(RH) for _ in range(2)]
        r_h = [wcut(2 * RH) for _ in range(2)]
        r_hh = [[wcut(RH, F16) for _ in range(2)] for _ in range(2)]
        ys = [wcut(2 * D).rearrange("p (t d) -> p t d", t=2) for _ in range(2)]
        assert wat[0] <= 2080 + 2 * KD * SH, wat[0]

        gs = sb("global_p", [P, L])
        q0 = sb("global_q", [P, KD, NH])
        gp = sb("global_p_T", [P, TB, NH])
        rmx = sb("routed_w_max", [P, 3, NE])
        tick = sb("tick", [1, 16])
        st = sb("ln_stats", [P, TB, 6]); mv = sb("ln_mean_var", [P, TB, 2])
        ve = sb("ln_var_eps", [P, TB]); rstd = sb("ln_rstd", [P, TB]); nmr = sb("ln_shift", [P, TB])
        smx = sb("softmax_max", [P, 4, 8]); ssum = sb("softmax_sum", [P, 4, 8]); srec = sb("softmax_rec", [P, 4, 8])
        gmx = sb("global_neg_max", [NH, 1]); gsum = sb("global_sum", [NH, 1]); grec = sb("global_rec", [NH, 1])
        c0f = sb("ctx0_f32", [P, KD, B]); c0 = [sb(f"ctx0_{x}", [P, KD, B], F16) for x in ("high", "low")]
        c0m = sb("ctx0_masked", [P, B, NH]); out0 = sb("out0", [B, D])
        bvm = PT[:, 0, 0:KD, :]

        picked = arena[:, 0:2 * NTOK * D].rearrange("p (k t d) -> p k t d", k=2, t=NTOK)
        c_y = [arena[:, (2 * NTOK + b * TB) * D:(2 * NTOK + (b + 1) * TB) * D].rearrange("p (t d) -> p t d", t=TB)
               for b in range(B_FIRST)]

        ra = [route_area[:, i * 512:(i + 1) * 512].rearrange("p (t e) -> p t e", e=NE) for i in range(8)]
        sc_, sel, oh1, oh2, tmp = ra[:5]
        cum, posn, restart = (route_area[:, i * 512:(i + 1) * 512].rearrange("p (e t) -> p e t", e=NE) for i in (5, 6, 7))
        mx8 = arena[:, 4096:4352].rearrange("p (t e) -> p t e", e=8)
        ix8 = arena[:, 4352:4608].bitcast(U32).rearrange("p (t e) -> p t e", e=8)
        ixf = sb("top_indices_f32", [P, NTOK, 2])
        ohm = arena[:, 4608:4864].bitcast(F16).rearrange("p (e t) -> p e t", e=NE)
        tl = [sb(f"tiles_{i}", [P, NE]) for i in range(3)]
        slf = sb("slots_f32", [P, 2, NTOK])
        ecount = arena[0:1, 4864:4864 + NT * NE].rearrange("p (t e) -> p t e", e=NE)
        assert 4864 + NT * NE <= (E_ROUTE + 1) * EXPERT
        ef = sb("expert_of_tile", [1, NT])

        ps = ctx.enter_context(nc.psum_tensor("ps", [P, 8, 512], F32))
        S = ps[:, 0:4, :]
        G = ps[:, 4, :]

        def T(name, b):
            return ps[:, bank(name, b), :]

        s = {n: sem(n) for n in (
            "consts_in attn_w_in shared_w_in bias_in zeros_ready xs_zeroed "
            "attn_max attn_all_max shared_max shared_all_max routed_max routed_all_max "
            "scale_ready attn_high attn_low shared_high shared_low w3_low routed_high routed_low setup "
            "bias_psum bias_ready pads_ready "
            "x_in0 x_in1 ln_stats ln_mv ln_var ln_rstd ln_shift xn_made xn_kept xb_made xT_high "
            "unit_full act_empty dve_empty s_full s_max s_taken s_exp s_summed soft_sum vector_step routed_each p_ready "
            "q0_half q0_ready g_full g_max g_exp g_rec g_ready u_high ctx_high "
            "y1_stored0 y1_stored1 c0_full c0_ready out0_full out0_ready out0_added "
            "scores_ready route chosen_ready prefix_full slots_ready table_ready "
            "raw_in_early a_full silu_done h_done hh_high hh_low y_full y_in0 y_in1 y_done y2_stored0 y2_stored1 "
            "xs_in0 xs_in1 rx_full rx_high rx_low ab_full r_silu_done r_h_done rh_full rh_high rh_low "
            "ry_full ry_done ys_stored0 ys_stored1 "
            "mixed one_added out_stored").split()}
        scattered = [sem(f"scattered_{i}") for i in range(GROUPS)]
        raw_in_late = [sem(f"raw_in_late_{i}") for i in range(GROUPS)]
        last_picks = [sem(f"picked_in_tile_{NTOK - TB + i}") for i in range(TB)]
        base_in = [sem(f"base_in_{b}") for b in range(B_FIRST)]
        pick_in = [sem(f"picked_in_{b}") for b in range(B)]
        block = ctx.enter_context(nc.Block())

        SPLIT = ((0, 0), (1, 0), (0, 1))

        def pairs(eng, body, first, last):
            with eng.Fori(0, (last - first) // 2) as i:
                for j in range(2):
                    body(i * 2 + (first + j), (first + j) % 2)

        @block.sync
        def _(sp):
            sp.dma_start(xr[0], x_rows[0]).then_inc(s["x_in0"], 16)
            for i, c in enumerate("qkvo"):
                sp.dma_start(wa_raw[:, i], a[f"L0_attn_W{c}"].rearrange("(k p) d -> p k d", p=P)).then_inc(s["attn_w_in"], 16)
            sp.dma_start(wr_raw, a["L0_ffn_router_w"].rearrange("(k p) e -> p k e", p=P)).then_inc(s["attn_w_in"], 16)
            sp.dma_start(xr[1], x_rows[1]).then_inc(s["x_in1"], 16)
            for i, name in enumerate(("shared_w1", "shared_w2")):
                sp.dma_start(w12_raw[:, i], a[f"L0_ffn_{name}"].rearrange("o (k p) h -> p (o k) h", p=P)).then_inc(s["shared_w_in"], 16)
            sp.dma_start(w3_raw, a["L0_ffn_shared_w3"].rearrange("o (c p) d -> p (o c) d", p=P)).then_inc(s["shared_w_in"], 16)
            sp.wait_ge(s["zeros_ready"], 1)
            sp.dma_start(xs_dram.rearrange("(p a) d -> p a d", p=P),
                         zero[:, :].unsqueeze(1).to_broadcast([P, NT, D])).then_inc(s["xs_zeroed"], 16)

            def attention(n, par, load=True):
                if load:
                    sp.wait_ge(s["xn_made"], n + 1)
                    sp.wait_ge(s["xb_made"], n + 1)
                    sp.dma_start(xr[par], x_rows[n + 2] if isinstance(n, int) else
                                 x_rows[bass.ds(n + 2, 1)].rearrange("a p t d -> p (a t) d")).then_inc(s[f"x_in{par}"], 16)
                sp.wait_ge(s["dve_empty"], emptied("out1", n))
                sp.dma_start(y1_rows[n] if isinstance(n, int) else y1_rows[bass.ds(n, 1)].rearrange("a p t d -> p (a t) d"),
                             xb[par]).then_inc(s[f"y1_stored{par}"], 16)

            attention(0, 0)
            attention(1, 1)
            pairs(sp, attention, LOOP_FROM - 1, LOOP_TO - 1)
            for n in range(LOOP_TO - 1, B):
                attention(n, n % 2, load=n + 2 < B)

            def shared(b0, b1, before_last=None):
                def load(b, par):
                    sp.dma_start(s_y[par], y1_rows[b]).then_inc(s[f"y_in{par}"], 16)
                for b in range(b0, b1):
                    par = b % 2
                    if b == b0:
                        if b >= 2:
                            sp.wait_ge(s[f"y2_stored{par}"], 16 * (b // 2))
                        load(b, par)
                    if b + 1 < b1:
                        if b >= 1:
                            sp.wait_ge(s[f"y2_stored{1 - par}"], 16 * ((b + 1) // 2))
                        load(b + 1, 1 - par)
                    if before_last and b == b1 - 1:
                        before_last()
                    if b < B_FIRST:
                        sp.wait_ge(s["y_done"], b + 3)
                        sp.dma_start(y2_rows[b], s_y[par]).then_inc(s[f"y2_stored{par}"], 16)

            for par in range(2):
                sp.wait_ge(s[f"y1_stored{par}"], 16 * (B // 2))
            sp.wait_ge(s["out0_added"], 16)
            sp.wait_ge(s["shared_low"], 1)

            def raw_weights(experts, into):
                for e in experts:
                    raw = arena[:, (e + 1) * EXPERT:(e + 2) * EXPERT]
                    r12 = raw[:, 0:2 * KD * RH].rearrange("p (k i h) -> p k i h", k=KD, i=2)
                    sp.dma_start(r12[:, :, 0, :], a["L0_ffn_routed_w1"][e].rearrange("(k p) h -> p k h", p=P)).then_inc(into, 16)
                    sp.dma_start(r12[:, :, 1, :], a["L0_ffn_routed_w2"][e].rearrange("(k p) h -> p k h", p=P)).then_inc(into, 16)
                    sp.dma_start(raw[:, 2 * KD * RH:].rearrange("p (c d) -> p c d", d=D),
                                 a["L0_ffn_routed_w3"][e].rearrange("(c p) d -> p c d", p=P)).then_inc(into, 16)

            raw_weights(range(E_ROUTE, E_EARLY), s["raw_in_early"])
            shared(0, 1)
            sp.wait_ge(s["route"], 1)
            raw_weights(range(E_ROUTE), s["raw_in_early"])
            for i in range(GROUPS):
                if i in (0, 2):
                    shared(1 + i // 2, 2 + i // 2)
                sp.wait_ge(scattered[i], 16 * 2 * (NTOK // GROUPS))
                raw_weights([e for e in group_of if group_of[e] == i], raw_in_late[i])

            def load_rows(r, par):
                sp.dma_start(xs[par], xs_pairs[r] if isinstance(r, int) else
                             xs_pairs[bass.ds(r, 1)].rearrange("a p t d -> p (a t) d")).then_inc(s[f"xs_in{par}"], 16)

            def store_rows(r, par):
                sp.wait_ge(s["ry_done"], r + 1)
                sp.dma_start(ys_pairs[r] if isinstance(r, int) else
                             ys_pairs[bass.ds(r, 1)].rearrange("a p t d -> p (a t) d"), ys[par]).then_inc(s[f"ys_stored{par}"], 16)

            load_rows(0, 0)
            load_rows(1, 1)

            def third_rows():
                sp.wait_ge(s["rx_full"], 1)
                load_rows(2, 0)

            shared(3, B_FIRST, before_last=third_rows)

            def routed(r, par):
                sp.wait_ge(s["rx_full"], r - 1)
                load_rows(r, par)
                store_rows(r - LAG, 1 - par)

            for r in range(3, LAG + 1):
                sp.wait_ge(s["rx_full"], r - 1)
                load_rows(r, r % 2)
            store_rows(0, 0)
            pairs(sp, routed, LAG + 1, NR)
            for r in range(NR - LAG, NR):
                store_rows(r, r % 2)
            for par in range(2):
                sp.wait_ge(s[f"ys_stored{par}"], 16 * (NR // 2))
            def base(b):
                sp.dma_start(c_y[b], y2_rows[b]).then_inc(base_in[b], 16)

            base(0)
            for b in range(1, B_FIRST):
                base(b)
                sp.wait_ge(pick_in[b - 1], 16 * 2 * TB)
                if b <= B - B_FIRST:
                    last = B_FIRST + b - 1
                    sp.dma_start(s_y[last % 2], y1_rows[last]).then_inc(s[f"y_in{last % 2}"], 16)

            for b in range(B - 1):
                sp.wait_ge(s["mixed"], TB * (b + 1))
                sp.dma_start(out_rows[b], c_y[b] if b < B_FIRST else s_y[b % 2]).then_inc(s["out_stored"], 16)
            for part in range(2):
                sp.wait_ge(s["mixed"], TB * (B - 1) + TB // 2 * (part + 1))
                tiles = slice(TB // 2 * part, TB // 2 * (part + 1))
                sp.dma_start(out_rows[B - 1][:, tiles], s_y[(B - 1) % 2][:, tiles]).then_inc(s["out_stored"], 16)
            sp.wait_ge(s["out_stored"], 16 * (B + 1))

        @block.gpsimd
        def _(pool):
            def rstd_of(n):
                pool.wait_ge(s["ln_var"], n + 1)
                nc.gpsimd.tensor_tensor(rstd[:, :], ve[:, :], cf[:, C_PW:C_PW + TB], ALU.pow).then_inc(s["ln_rstd"], 1)

            def keep_rows(n, par):
                pool.wait_ge(s["xn_made"], n + 1)
                dst = xn[:, n * TB:(n + 1) * TB, :] if isinstance(n, int) else xn[:, bass.ds(n * TB, TB), :]
                nc.gpsimd.tensor_copy(dst, xnr[par]).then_inc(s["xn_kept"], 1)

            def normalise(n, par):
                pool.wait_ge(s["s_summed"], n + 1)
                e = E[par].rearrange("p g k c -> p (g k) c")
                r = srec[:, :, :].rearrange("p g k -> p (g k)").unsqueeze(2).to_broadcast([P, 32, WIN])
                nc.gpsimd.tensor_tensor(e, e, r, ALU.mult).then_inc(s["p_ready"], 1)

            def residual(n, par, stored=True):
                if stored:
                    pool.wait_ge(s[f"y1_stored{par}"], (n + (-par)) * 8)
                nc.gpsimd.tensor_tensor(xb[par], xr[par], bias_tile[:, :].unsqueeze(1).to_broadcast([P, TB, D]),
                                        ALU.add).then_inc(s["xb_made"], 1)

            pool.wait_ge(s["consts_in"], 32)
            rstd_of(0)
            pool.wait_ge(s["attn_max"], 2)
            nc.gpsimd.partition_all_reduce(pw[:, 0:5], mx[:, 0:5], P, RMAX).then_inc(s["attn_all_max"], 1)
            for x in xT:
                nc.gpsimd.memset(x[:, :, 0:XPAD], 0.0)
            for v in VB:
                nc.gpsimd.memset(v, 0.0)
            for c in cT:
                i = nc.gpsimd.memset(c, 0.0)
            i.then_inc(s["pads_ready"], 1)
            nc.gpsimd.memset(zero[:, :], 0.0).then_inc(s["zeros_ready"], 1)
            keep_rows(0, 0)
            pool.wait_ge(s["bias_ready"], 1)
            residual(0, 0, stored=False)
            rstd_of(1)
            keep_rows(1, 1)
            normalise(0, 0)
            residual(1, 1, stored=False)

            def turn(n, par):
                rstd_of(n + 1)
                keep_rows(n + 1, 1 - par)
                normalise(n, par)
                residual(n + 1, 1 - par)

            turn(1, 1)
            pool.wait_ge(s["shared_max"], 3)
            nc.gpsimd.partition_all_reduce(pw[:, 5:8], mx[:, 5:8], P, RMAX).then_inc(s["shared_all_max"], 1)
            turn(2, 0)
            pool.wait_ge(s["w3_low"], 1)
            pairs(pool, turn, LOOP_FROM, LOOP_TO)
            normalise(B - 1, 1)

            for par in range(2):
                pool.wait_ge(s[f"y1_stored{par}"], 16 * (B // 2))
            pool.wait_ge(s["out0_ready"], 1)
            pool.dma_start(y1_dram.rearrange("(b l) d -> b l d", l=L)[:, 0, :], out0[:, :],
                           accum_op=ALU.add).then_inc(s["out0_added"], 16)

            pool.wait_ge(s["xs_zeroed"], 16)
            pool.wait_ge(s["slots_ready"], 1)
            pool.wait_ge(s["xn_kept"], B)
            for t in range(NTOK):
                for k in range(2):
                    pool.indirect_dma_start(out=xs_dram, out_offset=bass.IndirectOffsetOnAxis(ap=slots[:, k, t:t + 1], axis=0),
                                            in_=xn[:, t, :], in_offset=None).then_inc(scattered[t // (NTOK // GROUPS)], 16)

            pool.wait_ge(s["routed_max"], 1)
            nc.gpsimd.partition_all_reduce(pw[:, 8:11], mx[:, 8:11], P, RMAX).then_inc(s["routed_all_max"], 1)

            for par in range(2):
                pool.wait_ge(s[f"ys_stored{par}"], 16 * (NR // 2))
            for t in range(NTOK):
                for k in range(2):
                    pool.indirect_dma_start(out=picked[:, k, t, :], out_offset=None, in_=ys_dram,
                                            in_offset=bass.IndirectOffsetOnAxis(ap=slots[:, k, t:t + 1], axis=0)
                                            ).then_inc(pick_in[t // TB] if t < NTOK - TB else last_picks[t % TB], 16)

        @block.scalar
        def _(act):
            ev = nc.scalar

            def split_high(dst, src, col, name):
                ev.activation(dst, src, ACT.Identity, scale=scl[:, col:col + 1]).then_inc(s[name], 1)

            act.dma_start(cf[:, :], a["const_f32"]).then_inc(s["consts_in"], 16)
            act.dma_start(ch[:, :], a["const_f16"]).then_inc(s["consts_in"], 16)
            act.dma_start(bqkv[:, :], a["bias_columns"]).then_inc(s["bias_in"], 16)
            act.dma_start(bias_tile[:, :], a["L0_attn_bo"].unsqueeze(0).to_broadcast([P, D])).then_inc(s["bias_in"], 16)
            act.dma_start(eb[:, :], a["L0_ffn_expert_bias"].unsqueeze(0).to_broadcast([P, NE])).then_inc(s["bias_in"], 16)

            def batch_of(n):
                return slice(n, n + 1) if isinstance(n, int) else bass.ds(n, 1)

            def columns(n):
                return slice(XPAD + n * L, XPAD + (n + 1) * L) if isinstance(n, int) else bass.ds(n * L + XPAD, L)

            def x_high(n):
                for k in range(KD):
                    act.wait_ge(s["unit_full"], made(f"xT{k}", n))
                    ev.activation(xT[0][:, k, columns(n)], T(f"xT{k}", n), ACT.Identity).then_inc(s["xT_high"], 1)

            def turn(n, par, now=True, prev=True, nxt=True, during_scores=None):
                if now:
                    act.wait_ge(s["unit_full"], made("router", n))
                    lsl = slice(n * TB, (n + 1) * TB) if isinstance(n, int) else bass.ds(n * TB, TB)
                    ev.activation(logits[:, lsl, :], T("router", n)[:, 0:TB * NE].rearrange("p (t e) -> p t e", e=NE),
                                  ACT.Identity, scale=inv[:, 4:5]).then_inc(s["act_empty"], 1)
                    act.wait_ge(s["unit_full"], made("q0", n))
                    for o in range(2):
                        q = ev.activation(QT[o][:, 0, :], T("q0", n)[:, 0:TB * (WIN + 1)], ACT.Identity,
                                          bias=bqp[:, o, 0:1], scale=der[:, D_QE + o:D_QE + o + 1])
                    q.then_inc(s["act_empty"], 1)
                if prev:
                    b = n + (-1)
                    act.wait_ge(s["unit_full"], made("p0", b))
                    ev.activation(gp, T("p0", b)[:, 0:TB * NH].rearrange("p (t e) -> p t e", e=NH), ACT.Identity).then_inc(s["act_empty"], 1)
                if now:
                    act.wait_ge(s["unit_full"], made("k0", n))
                    ev.activation(KT[:, 0, :], T("k0", n), ACT.Identity, bias=bk[:, 0:1], scale=inv[:, 1:2]).then_inc(s["act_empty"], 1)
                if prev:
                    act.wait_ge(s["unit_full"], made("u", b))
                    ev.activation(uT[0][:, :, batch_of(b), :].rearrange("p k o e -> p k (o e)"),
                                  T("u", b)[:, 0:KD * NH].rearrange("p (k e) -> p k e", e=NH), ACT.Identity).then_inc(s["u_high"], 1)
                if during_scores:
                    during_scores()
                if prev:
                    for j in (0, 2):
                        act.wait_ge(s["unit_full"], made(f"pT{j}", b))
                        ev.activation(PT[:, j], T(f"pT{j}", b).rearrange("p (g q) -> p g q", g=4), ACT.Identity).then_inc(s["act_empty"], 1)
                if nxt:
                    x_high(n + 1)
                if prev:
                    act.wait_ge(s["unit_full"], made("ctx", b))
                    ev.activation(cT[0][:, :, :, 1:1 + WIN], T("ctx", b).rearrange("p (m w q) -> p m w q", m=KD, w=TB),
                                  ACT.Identity).then_inc(s["ctx_high"], 1)
                if now:
                    act.wait_ge(s["s_taken"], n + 1)
                    e = E[par].rearrange("p g k c -> p (g k c)")
                    ev.activation(e, e, ACT.Exp).then_inc(s["s_exp"], 1)
                if now:
                    act.wait_ge(s["g_max"], n + 1)
                    ev.activation(gs[0:NH, :], G[0:NH, :], ACT.Exp, bias=gmx[:, :], accum_out=gsum[:, :]).then_inc(s["g_exp"], 1)

            x_high(0)
            act.wait_ge(s["attn_w_in"], 80)
            act.wait_ge(s["scale_ready"], 1)
            for i in range(4):
                split_high(wa[0][:, i], wa_raw[:, i], i, "attn_high")
            split_high(wr[0][:, :, :], wr_raw, 4, "attn_high")
            act.wait_ge(s["setup"], 1)
            act.wait_ge(s["pads_ready"], 1)
            turn(0, 0, prev=False)
            turn(1, 1)

            def shared_weights_high():
                act.wait_ge(s["scale_ready"], 2)
                split_high(w3[0][:, :, :], w3_raw, 7, "shared_high")
                for i in range(2):
                    split_high(w12[0][:, i], w12_raw[:, i], 5 + i, "shared_high")

            act.wait_ge(s["shared_w_in"], 48)
            turn(2, 0, during_scores=shared_weights_high)
            pairs(act, turn, LOOP_FROM, LOOP_TO)
            turn(B - 1, 1, nxt=False)
            turn(B, 0, now=False, nxt=False)

            ev.activation(sc_, logits[:, :, :], ACT.Sigmoid).then_inc(s["scores_ready"], 1)

            def chunk(b, c):
                n, q = b * SC + c, c % 2
                act.wait_ge(s["a_full"], n + 1)
                ev.activation(s_silu[q], ps[:, 2 * q, :], ACT.Silu, scale=inv[:, 5:6]).then_inc(s["silu_done"], 1)
                act.wait_ge(s["h_done"], n + 3)
                ev.activation(s_hh[0][q], s_h[q], ACT.Identity).then_inc(s["hh_high"], 1)

            def shared(b0, b1):
                with act.Fori(b0, b1) as b:
                    for c in range(SC):
                        chunk(b, c)

            act.wait_ge(s["shared_low"], 1)
            shared(0, B_SPLIT)
            with act.Fori(B_SPLIT, B_FIRST) as b:
                for c in range(SC):
                    chunk(b, c)
                    act.wait_ge(s["routed_low"], b * (2 * SC) + (2 * (c - B_SPLIT * SC) + 1))
                    raw = lambda lo, n: arena[:, bass.ds(b * (SC * EXPERT) + ((c + 1 - B_SPLIT * SC) * EXPERT + lo), n)]
                    high = lambda lo, n: ar16[:, bass.ds(b * (2 * SC * EXPERT) + (2 * (c - B_SPLIT * SC) * EXPERT + lo), n)]
                    for i in range(2):
                        h = ev.activation(high(0, 2 * KD * RH).rearrange("p (k i h) -> p k i h", k=KD, i=2)[:, :, i],
                                          raw(0, 2 * KD * RH).rearrange("p (k i h) -> p k i h", k=KD, i=2)[:, :, i],
                                          ACT.Identity, scale=scl[:, 8 + i:9 + i])
                    h.then_inc(s["routed_high"], 1)
                    ev.activation(high(2 * KD * RH, 2 * D), raw(2 * KD * RH, 2 * D), ACT.Identity,
                                  scale=scl[:, 10:11]).then_inc(s["routed_high"], 1)

            def x_high(r, par):
                act.wait_ge(s["rx_full"], r + 1)
                ev.activation(r_x[0][par], ps[:, 2 + par, :], ACT.Identity).then_inc(s["rx_high"], 1)

            def gated(r, par):
                for j in range(2):
                    act.wait_ge(s["ab_full"], 2 * r + j + 1)
                    ev.activation(r_silu[j], ps[:, j, 0:RH], ACT.Silu, scale=inv[:, 8:9]).then_inc(s["r_silu_done"], 1)

            def h_high(r, par):
                act.wait_ge(s["rh_full"], r + 1)
                ev.activation(r_hh[0][par], ps[:, 4 + par, :], ACT.Identity).then_inc(s["rh_high"], 1)

            def y_out(r, par, stored=True):
                act.wait_ge(s["ry_full"], r + 1)
                if stored:
                    act.wait_ge(s[f"ys_stored{par}"], (r + (-par)) * 8)
                ev.activation(ys[par].rearrange("p t d -> p (t d)"), ps[:, 6 + par, :], ACT.Identity,
                              scale=der[:, D_RY:D_RY + 1]).then_inc(s["ry_done"], 1)

            act.wait_ge(s["hh_low"], B_FIRST * SC)
            x_high(0, 0)
            for r in range(4):
                x_high(r + 1, (r + 1) % 2)
                gated(r, r % 2)
                if r == 1:
                    for par in range(2):
                        act.wait_ge(s[f"y2_stored{par}"], 16 * (B_FIRST // 2))
                if r >= 1:
                    h_high(r - 1, (r - 1) % 2)
                if r >= 2:
                    y_out(r - 2, r % 2, stored=False)

            def routed(r, par):
                x_high(r + 1, 1 - par)
                gated(r, par)
                h_high(r - 1, 1 - par)
                y_out(r - 2, par)

            pairs(act, routed, 4, NR - 2)
            routed(NR - 2, 0)
            gated(NR - 1, 1)
            h_high(NR - 2, 0)
            y_out(NR - 3, 1)
            h_high(NR - 1, 1)
            y_out(NR - 2, 0)
            y_out(NR - 1, 1)
            shared(B_FIRST, B)

        @block.vector
        def _(dve):
            v = nc.vector
            steps = [0]

            def link(i):
                steps[0] += 1
                i.then_inc(s["vector_step"], 1)
                dve.wait_ge(s["vector_step"], steps[0])

            marks = [0]

            def signal(name, n=1):
                marks[0] += 1
                v.memset(tick[:, marks[0]:marks[0] + 1], 0.0).then_inc(s[name], n)

            def scales(lo, hi, reduced):
                dve.wait_ge(s[reduced], 1)
                link(v.tensor_scalar(pw[:, lo:hi], pw[:, lo:hi], 2.0 ** -40, None, ALU.max))
                link(v.tensor_scalar(pw[:, lo:hi].bitcast(I32), pw[:, lo:hi].bitcast(I32), 0x7F800000, None, ALU.bitwise_and))
                link(v.tensor_scalar(inv[:, lo:hi], pw[:, lo:hi], 1.0 / TOP, None, ALU.mult))
                link(v.reciprocal(scl[:, lo:hi], inv[:, lo:hi]))

            def ln(n, par, kept):
                x = xr[par]
                dve.wait_ge(s[f"x_in{par}"], (n + (-par)) * 8 + 16)
                for t in range(TB):
                    i = v.bn_stats(st[:, t, :], x[:, t, :])
                i.then_inc(s["ln_stats"], 1)
                dve.wait_ge(s["ln_stats"], n + 1)
                v.memset(tick[:, 0:1], 0.0)
                for t in range(TB):
                    i = v.bn_aggr(mv[:, t, :], st[:, t, :])
                i.then_inc(s["ln_mv"], 1)
                dve.wait_ge(s["ln_mv"], n + 1)
                v.tensor_scalar(ve[:, :], mv[:, :, 1], EPS, None, ALU.add).then_inc(s["ln_var"], 1)
                dve.wait_ge(s["ln_rstd"], n + 1)
                v.scalar_tensor_tensor(out=nmr[:, :], in0=mv[:, :, 0], scalar=-1.0, in1=rstd[:, :],
                                       op0=ALU.mult, op1=ALU.mult).then_inc(s["ln_shift"], 1)
                dve.wait_ge(s["ln_shift"], n + 1)
                if kept:
                    dve.wait_ge(s["xn_kept"], n - 1)
                for t in range(TB):
                    i = v.tensor_scalar(xnr[par][:, t, :], x[:, t, :], rstd[:, t:t + 1], nmr[:, t:t + 1], ALU.mult, ALU.add)
                i.then_inc(s["xn_made"], 1)

            def batch_of(n):
                return slice(n, n + 1) if isinstance(n, int) else bass.ds(n, 1)

            def columns(n):
                return slice(XPAD + n * L, XPAD + (n + 1) * L) if isinstance(n, int) else bass.ds(n * L + XPAD, L)

            def x_low(n):
                for k in range(KD):
                    dve.wait_ge(s["xT_high"], n * 2 + (k + 1))
                    v.tensor_tensor(xT[1][:, k, columns(n)], T(f"xT{k}", n), xT[0][:, k, columns(n)], ALU.subtract).then_inc(s["dve_empty"], 1)

            def queries(n):
                dve.wait_ge(s["unit_full"], made("q1", n))
                for o in range(2):
                    i = v.tensor_scalar(QT[o][:, 1, :], T("q1", n)[:, 0:TB * (WIN + 1)], der[:, D_QE + o:D_QE + o + 1],
                                        bqp[:, o, 1:2], ALU.mult, ALU.add)
                i.then_inc(s["dve_empty"], 1)
                dve.wait_ge(s["act_empty"], emptied("q0", n))
                dve.wait_ge(s["dve_empty"], emptied("q1", n))
                hm = cf[:, C_HM:C_HM + KD * NH].rearrange("p (m h) -> p m h", h=NH)
                for m in range(KD):
                    i = v.tensor_scalar(q0[:, m, :], hm[:, m, :], QT[0][:, m, 0:1], None, ALU.mult)
                i.then_inc(s["q0_half"], 1)
                dve.wait_ge(s["q0_half"], n + 1)
                for m in range(KD):
                    i = v.scalar_tensor_tensor(out=q0[:, m, :], in0=hm[:, m, :], scalar=QT[1][:, m, 0:1], in1=q0[:, m, :],
                                               op0=ALU.mult, op1=ALU.add)
                i.then_inc(s["q0_ready"], 1)

            def keys(n):
                dve.wait_ge(s["unit_full"], made("k1", n))
                v.tensor_scalar(KT[:, 1, :], T("k1", n), inv[:, 1:2], bk[:, 1:2], ALU.mult, ALU.add).then_inc(s["dve_empty"], 1)

            def values(n, par):
                for c in range(2):
                    dve.wait_ge(s["unit_full"], made(f"v{c}", n))
                    src = T(f"v{c}", n).rearrange("p (w o j d) -> p w o j d", w=2, j=8, o=2)
                    for o in range(2):
                        for w in range(2):
                            i = v.tensor_copy(VB[par][64 * o:64 * o + 64, 2 * c + w, :, HD * o:HD * o + HD],
                                              src[64 * o:64 * o + 64, w, o, :, :])
                    i.then_inc(s["dve_empty"], 1)

            def turn(n, par, now=True, prev=True, nxt=True, kept=True, before_keys=None, during_scores=None):
                b = n + (-1)
                e = E[par].rearrange("p g k c -> p (g k) c")
                sv = S.rearrange("p g (k c) -> p (g k) c", c=WIN)
                flat = "p g k -> p (g k)"
                if now:
                    queries(n)
                if before_keys:
                    before_keys()
                if now:
                    keys(n)
                if prev:
                    dve.wait_ge(s["u_high"], b + 1)
                    v.tensor_tensor(uT[1][:, :, batch_of(b), :].rearrange("p k o e -> p k (o e)"),
                                    T("u", b)[:, 0:KD * NH].rearrange("p (k e) -> p k e", e=NH),
                                    uT[0][:, :, batch_of(b), :].rearrange("p k o e -> p k (o e)"), ALU.subtract).then_inc(s["dve_empty"], 1)
                if now:
                    values(n, par)
                if nxt:
                    ln(n + 1, 1 - par, kept)
                if during_scores:
                    during_scores()
                if now:
                    dve.wait_ge(s["s_full"], n + 1)
                    v.tensor_reduce(smx[:, :, :].rearrange(flat), sv, AX, ALU.max).then_inc(s["s_max"], 1)
                if prev:
                    for j in (1, 3):
                        dve.wait_ge(s["unit_full"], made(f"pT{j}", b))
                        v.tensor_copy(PT[:, j], T(f"pT{j}", b).rearrange("p (g q) -> p g q", g=4)).then_inc(s["dve_empty"], 1)
                if now:
                    dve.wait_ge(s["s_max"], n + 1)
                    v.tensor_tensor(e, sv, smx[:, :, :].rearrange(flat).unsqueeze(2).to_broadcast([P, 32, WIN]),
                                    ALU.subtract).then_inc(s["s_taken"], 1)
                if nxt:
                    x_low(n + 1)
                if prev:
                    dve.wait_ge(s["ctx_high"], b + 1)
                    src = T("ctx", b).rearrange("p (m w q) -> p m w q", m=KD, w=TB)
                    for m in range(KD):
                        i = v.tensor_tensor(cT[1][:, m, :, 1:1 + WIN], src[:, m], cT[0][:, m, :, 1:1 + WIN], ALU.subtract)
                    i.then_inc(s["dve_empty"], 1)
                if now:
                    dve.wait_ge(s["g_full"], n + 1)
                    v.tensor_reduce(gmx[:, :], G[0:NH, :], AX, ALU.max, negate=True).then_inc(s["g_max"], 1)
                    dve.wait_ge(s["g_exp"], n + 1)
                    v.reciprocal(grec[:, :], gsum[:, :]).then_inc(s["g_rec"], 1)
                    dve.wait_ge(s["g_rec"], n + 1)
                    v.tensor_scalar(gs[0:NH, :], gs[0:NH, :], grec[:, :], None, ALU.mult).then_inc(s["g_ready"], 1)
                if prev:
                    for c in range(2):
                        dve.wait_ge(s["unit_full"], made(f"out{c}", b))
                        dve.wait_ge(s["xb_made"], b + 1)
                        dst = xb[1 - par][:, 2 * c:2 * c + 2, :].rearrange("p t d -> p (t d)")
                        v.scalar_tensor_tensor(out=dst, in0=T(f"out{c}", b), scalar=der[:, D_O:D_O + 1], in1=dst,
                                               op0=ALU.mult, op1=ALU.add).then_inc(s["dve_empty"], 1)
                if now:
                    dve.wait_ge(s["s_exp"], n + 1)
                    v.tensor_reduce(ssum[:, :, :].rearrange(flat), e, AX, ALU.add).then_inc(s["soft_sum"], 1)
                    dve.wait_ge(s["soft_sum"], n + 1)
                    v.reciprocal(srec[:, :, :], ssum[:, :, :]).then_inc(s["s_summed"], 1)

            for name in ("h_done", "y_done"):
                signal(name, 2)

            ln(0, 0, False)
            dve.wait_ge(s["attn_w_in"], 80)
            v.tensor_reduce(mx[:, 0:4], wa_raw.rearrange("p i k d -> p i (k d)"), AX, ALU.max,
                            apply_absolute_value=True).then_inc(s["attn_max"], 1)
            v.tensor_reduce(mx[:, 4:5], wr_raw.rearrange("p k e -> p (k e)"), AX, ALU.max,
                            apply_absolute_value=True).then_inc(s["attn_max"], 1)
            x_low(0)
            scales(0, 5, "attn_all_max")
            signal("scale_ready")
            dve.wait_ge(s["consts_in"], 32)
            dve.wait_ge(s["bias_in"], 48)
            for o, c in ((0, C_EVEN), (1, C_ODD)):
                link(v.tensor_scalar(der[:, D_QE + o:D_QE + o + 1], cf[:, c:c + 1], inv[:, 0:1], HD ** -0.5, ALU.mult, ALU.mult))
                link(v.tensor_scalar(bqp[:, o, :], bq[:, :], cf[:, c:c + 1], HD ** -0.5, ALU.mult, ALU.mult))
            link(v.tensor_tensor(der[:, D_O:D_O + 1], inv[:, 2:3], inv[:, 3:4], ALU.mult))
            for m in range(KD):
                link(v.tensor_scalar(bvm[:, m, :], cf[:, C_TOK:C_TOK + P], bv[:, m:m + 1], None, ALU.mult))
            signal("setup")
            for i in range(4):
                dve.wait_ge(s["attn_high"], i + 1)
                v.scalar_tensor_tensor(out=wa[1][:, i].rearrange("p k d -> p (k d)"), in0=wa_raw[:, i].rearrange("p k d -> p (k d)"),
                                       scalar=scl[:, i:i + 1], in1=wa[0][:, i].rearrange("p k d -> p (k d)"),
                                       op0=ALU.mult, op1=ALU.subtract)
            dve.wait_ge(s["attn_high"], 5)
            v.scalar_tensor_tensor(out=wr[1][:, :, :], in0=wr_raw, scalar=scl[:, 4:5], in1=wr[0][:, :, :],
                                   op0=ALU.mult, op1=ALU.subtract).then_inc(s["attn_low"], 1)
            dve.wait_ge(s["bias_psum"], 1)
            link(v.tensor_tensor(bias_tile[:, :], ps[:, 4, 0:D], bias_tile[:, :], ALU.add))
            v.tensor_copy(bv_out[:, :], ps[0:B, 4, D:2 * D]).then_inc(s["bias_ready"], 1)
            dve.wait_ge(s["pads_ready"], 1)
            turn(0, 0, prev=False, kept=False)

            def largest_shared(col, w):
                v.tensor_reduce(mx[:, col:col + 1], w, mybir.AxisListType.XY, ALU.max,
                                apply_absolute_value=True).then_inc(s["shared_max"], 1)

            dve.wait_ge(s["shared_w_in"], 48)
            turn(1, 1, before_keys=lambda: largest_shared(5, w12_raw[:, 0]),
                 during_scores=lambda: largest_shared(6, w12_raw[:, 1]))
            largest_shared(7, w3_raw)

            def shared_scales():
                scales(5, 8, "shared_all_max")
                link(v.tensor_scalar(der[:, D_HS:D_HS + 1], scl[:, 5:6], 2.0 ** -15, None, ALU.mult))
                link(v.tensor_tensor(der[:, D_Y:D_Y + 1], inv[:, 5:6], inv[:, 6:7], ALU.mult))
                link(v.tensor_scalar(der[:, D_Y:D_Y + 1], der[:, D_Y:D_Y + 1], inv[:, 7:8], 2.0 ** 15, ALU.mult, ALU.mult))
                signal("scale_ready")

            def shared_low(low, raw, high, col, order):
                flat = "p a b -> p (a b)"
                dve.wait_ge(s["shared_high"], order)
                return v.scalar_tensor_tensor(out=low.rearrange(flat), in0=raw.rearrange(flat), scalar=scl[:, col:col + 1],
                                              in1=high.rearrange(flat), op0=ALU.mult, op1=ALU.subtract)

            turn(2, 0, before_keys=shared_scales, during_scores=lambda: shared_low(w3[1][:, :, :], w3_raw, w3[0][:, :, :], 7, 1)
                 .then_inc(s["w3_low"], 1))
            pairs(dve, turn, LOOP_FROM, LOOP_TO)
            turn(B - 1, 1, nxt=False, before_keys=lambda: shared_low(w12[1][:, 0], w12_raw[:, 0], w12[0][:, 0], 5, 2),
                 during_scores=lambda: shared_low(w12[1][:, 1], w12_raw[:, 1], w12[0][:, 1], 6, 3).then_inc(s["shared_low"], 1))
            turn(B, 0, now=False, nxt=False)

            def gated_product(b, c):
                n, q = b * SC + c, c % 2
                dve.wait_ge(s["silu_done"], n + 1)
                v.scalar_tensor_tensor(out=s_h[q], in0=ps[:, 2 * q + 1, :], scalar=der[:, D_HS:D_HS + 1], in1=s_silu[q],
                                       op0=ALU.mult, op1=ALU.mult).then_inc(s["h_done"], 1)

            def h_low_part(b, c):
                n, q = b * SC + c, c % 2
                dve.wait_ge(s["hh_high"], n + 1)
                v.tensor_tensor(s_hh[1][q], s_h[q], s_hh[0][q], ALU.subtract).then_inc(s["hh_low"], 1)

            def chunk(b, c):
                gated_product(b, c)
                h_low_part(b, c)

            def shared_out(b, par):
                dve.wait_ge(s["y_full"], b + 1)
                dve.wait_ge(s[f"y_in{par}"], (b + (-par)) * 8 + 16)
                y = s_y[par].rearrange("p t d -> p (t d)")
                v.scalar_tensor_tensor(out=y, in0=ps[:, 4 + 2 * par:6 + 2 * par, :].rearrange("p a d -> p (a d)"),
                                       scalar=der[:, D_Y:D_Y + 1], in1=y, op0=ALU.mult, op1=ALU.add).then_inc(s["y_done"], 1)

            before = ps[:, 6, :].rearrange("p (e t) -> p e t", e=NE)
            total = ps[:, 7, :].rearrange("p (e t) -> p e t", e=NE)
            need, ends, first = (x[:, :] for x in tl)
            by_token = "p e t -> p t e"

            def best_scores():
                dve.wait_ge(s["scores_ready"], 1)
                link(v.tensor_tensor(sel, sc_, eb[:, :].unsqueeze(1).to_broadcast([P, NTOK, NE]), ALU.add))
                for t in range(NTOK):
                    i = v.max(mx8[:, t, :], sel[:, t, :])
                link(i)

            def best_experts():
                for t in range(NTOK):
                    i = v.max_index(ix8[:, t, :], mx8[:, t, :], sel[:, t, :])
                link(i)
                link(v.tensor_copy(ixf[:, :, :], ix8[:, :, 0:2]))

            def one_hots():
                ie = cf[:, C_IE:C_IE + NE].unsqueeze(1).to_broadcast([P, NTOK, NE])
                for k, oh in ((0, oh1), (1, oh2)):
                    link(v.tensor_tensor(oh, ie, ixf[:, :, k:k + 1].to_broadcast([P, NTOK, NE]), ALU.is_equal))
                v.tensor_tensor(ohm.rearrange(by_token), oh1, oh2, ALU.add).then_inc(s["chosen_ready"], 1)

            def gates(k, oh):
                link(v.tensor_tensor(tmp, oh, sc_, ALU.mult))
                link(v.tensor_reduce(gate[:, k, :], tmp, AX, ALU.add))

            def groups():
                link(v.memset(restart, 1.0))
                link(v.memset(restart[:, :, 0:1], 0.0))
                dve.wait_ge(s["prefix_full"], 2)
                flat = "p e t -> p (e t)"
                link(v.tensor_tensor_scan(cum.rearrange(flat), restart.rearrange(flat), total.rearrange(flat), 0.0, ALU.mult, ALU.add))
                link(v.tensor_scalar(need, cum[:, :, NTOK - 1], P - 1.0, 1.0 / P, ALU.add, ALU.mult))
                link(v.tensor_scalar(need, need, -0.5 + 0.5 / P, 2.0 ** 23, ALU.add, ALU.add))
                link(v.tensor_scalar(need, need, -(2.0 ** 23), None, ALU.add))
                link(v.tensor_tensor_scan(ends, restart[:, 0, 1:1 + NE], need, 0.0, ALU.mult, ALU.add))
                link(v.tensor_tensor(first, ends, need, ALU.subtract))
                link(v.tensor_scalar(first, first, float(P), None, ALU.mult))

            def positions():
                link(v.tensor_tensor(posn, cum, total, ALU.subtract))
                link(v.tensor_tensor(posn, before, posn, ALU.add))
                link(v.tensor_tensor(posn, posn, first.unsqueeze(2).to_broadcast([P, NE, NTOK]), ALU.add))

            def slots_of_tokens():
                for k, oh in ((0, oh1), (1, oh2)):
                    link(v.tensor_tensor(tmp, oh, posn.rearrange(by_token), ALU.mult))
                    link(v.tensor_reduce(slf[:, k, :], tmp, AX, ALU.add))
                v.tensor_copy(slots[:, :, :], slf[:, :, :]).then_inc(s["slots_ready"], 1)

            def tiles_of_experts():
                link(v.tensor_tensor(ecount[:, :, :], ends[0:1].unsqueeze(1).to_broadcast([1, NT, NE]),
                                     cf[0:1, C_IS:C_IS + NT].unsqueeze(2).to_broadcast([1, NT, NE]), ALU.is_le))

            def expert_table():
                link(v.tensor_reduce(ef[:, :], ecount[:, :, :], AX, ALU.add))
                link(v.tensor_scalar(ef[:, :], ef[:, :], NE - 1.0, 2.0 * EXPERT, ALU.min, ALU.mult))
                v.tensor_copy(etab[:, :], ef[:, :]).then_inc(s["table_ready"], 1)
                signal("route")

            chunk(0, 0)
            dve.wait_ge(s["c0_full"], 1)
            for m in range(KD):
                src = ps[:, 6, m * P:(m + 1) * P].rearrange("p (b h) -> p b h", h=NH)
                link(v.tensor_tensor(c0m[:, :, :], src, cf[:, C_HM + m * NH:C_HM + (m + 1) * NH].unsqueeze(1).to_broadcast([P, B, NH]), ALU.mult))
                link(v.tensor_reduce(c0f[:, m, :], c0m[:, :, :], AX, ALU.add))
            link(v.tensor_copy(c0[0][:, :, :], c0f[:, :, :]))
            v.tensor_tensor(c0[1][:, :, :], c0f[:, :, :], c0[0][:, :, :], ALU.subtract).then_inc(s["c0_ready"], 1)
            chunk(0, 1)
            dve.wait_ge(s["out0_full"], 1)
            v.scalar_tensor_tensor(out=out0[:, :], in0=ps[0:B, 7, 0:D], scalar=der[0:B, D_O:D_O + 1], in1=bv_out[:, :],
                                   op0=ALU.mult, op1=ALU.add).then_inc(s["out0_ready"], 1)
            best_scores()
            chunk(0, 2)
            best_experts()
            chunk(0, 3)
            one_hots()
            chunk(0, 4)
            chunk(0, 5)
            groups()
            chunk(0, 6)
            positions()
            chunk(0, 7)
            slots_of_tokens()
            shared_out(0, 0)
            for c in range(SC):
                chunk(1, c)
                if c == 0:
                    gates(0, oh1)
                if c == 1:
                    gates(1, oh2)
                if c == 2:
                    tiles_of_experts()
                if c == 3:
                    expert_table()
            shared_out(1, 1)

            def largest(e):
                if e >= E_EARLY:
                    dve.wait_ge(raw_in_late[group_of[e]], 48 * list(group_of.values()).count(group_of[e]))
                raw = arena[:, (e + 1) * EXPERT:(e + 2) * EXPERT]
                r12 = raw[:, 0:2 * KD * RH].rearrange("p (k i h) -> p i k h", k=KD, i=2)
                v.tensor_reduce(rmx[:, 0:2, e], r12, mybir.AxisListType.XY, ALU.max, apply_absolute_value=True).then_inc(s["routed_each"], 1)
                v.tensor_reduce(rmx[:, 2:3, e], raw[:, 2 * KD * RH:], AX, ALU.max, apply_absolute_value=True).then_inc(s["routed_each"], 1)

            def routed_scales():
                dve.wait_ge(s["routed_each"], 2 * NE)
                v.tensor_reduce(mx[:, 8:11], rmx[:, :, :], AX, ALU.max).then_inc(s["routed_max"], 1)
                scales(8, 11, "routed_all_max")
                link(v.tensor_scalar(der[:, D_RHS:D_RHS + 1], scl[:, 8:9], 2.0 ** -15, None, ALU.mult))
                link(v.tensor_tensor(der[:, D_RY:D_RY + 1], inv[:, 8:9], inv[:, 9:10], ALU.mult))
                link(v.tensor_scalar(der[:, D_RY:D_RY + 1], der[:, D_RY:D_RY + 1], inv[:, 10:11], 2.0 ** 15, ALU.mult, ALU.mult))
                signal("routed_low", 2)

            dve.wait_ge(s["raw_in_early"], 48 * E_EARLY)
            for c in range(SC):
                chunk(2, c)
                largest(c)
            shared_out(2, 0)
            for c in range(SC):
                chunk(3, c)
                if c < 6:
                    largest(SC + c)
                if c >= 5 and c < 7:
                    largest(SC + c + 1)
            routed_scales()
            shared_out(3, 1)

            def w12_low(e):
                raw = arena[:, (e + 1) * EXPERT:(e + 2) * EXPERT]
                hi, lo = (ar16[:, (2 * e + w) * EXPERT:(2 * e + w + 1) * EXPERT] for w in range(2))
                dve.wait_ge(s["routed_low"], 2 * e + 2)
                dve.wait_ge(s["routed_high"], 2 * e + 1)
                for i in range(2):
                    l, r, h = (z[:, 0:2 * KD * RH].rearrange("p (k i h) -> p k i h", k=KD, i=2)[:, :, i] for z in (lo, raw, hi))
                    x = v.scalar_tensor_tensor(out=l, in0=r, scalar=scl[:, 8 + i:9 + i], in1=h, op0=ALU.mult, op1=ALU.subtract)
                x.then_inc(s["routed_low"], 1)

            def w3_low(e):
                raw = arena[:, (e + 1) * EXPERT:(e + 2) * EXPERT]
                hi, lo = (ar16[:, (2 * e + w) * EXPERT:(2 * e + w + 1) * EXPERT] for w in range(2))
                dve.wait_ge(s["routed_high"], 2 * e + 2)
                v.scalar_tensor_tensor(out=lo[:, 2 * KD * RH:], in0=raw[:, 2 * KD * RH:], scalar=scl[:, 10:11],
                                       in1=hi[:, 2 * KD * RH:], op0=ALU.mult, op1=ALU.subtract).then_inc(s["routed_low"], 1)

            for e in range(NE):
                b, c = B_SPLIT + e // SC, e % SC
                gated_product(b, c)
                if e >= 1:
                    w3_low(e - 1)
                h_low_part(b, c)
                w12_low(e)
                if e == SC - 1:
                    shared_out(b, b % 2)
            w3_low(NE - 1)

            def x_low(r, par):
                dve.wait_ge(s["rx_high"], r + 1)
                v.tensor_tensor(r_x[1][par], ps[:, 2 + par, :], r_x[0][par], ALU.subtract).then_inc(s["rx_low"], 1)

            def gated(r, par):
                for j in range(2):
                    dve.wait_ge(s["r_silu_done"], 2 * r + j + 1)
                    v.scalar_tensor_tensor(out=r_h[par][:, j * RH:(j + 1) * RH], in0=ps[:, j, RH:2 * RH], scalar=der[:, D_RHS:D_RHS + 1],
                                           in1=r_silu[j], op0=ALU.mult, op1=ALU.mult).then_inc(s["r_h_done"], 1)

            def h_low(r, par):
                dve.wait_ge(s["rh_high"], r + 1)
                v.tensor_tensor(r_hh[1][par], ps[:, 4 + par, :], r_hh[0][par], ALU.subtract).then_inc(s["rh_low"], 1)

            x_low(0, 0)
            shared_out(B_FIRST - 1, 1)
            x_low(1, 1)
            gated(0, 0)

            def routed(r, par):
                x_low(r + 1, 1 - par)
                gated(r, par)
                h_low(r - 1, 1 - par)

            routed(1, 1)
            pairs(dve, routed, 2, NR - 2)
            routed(NR - 2, 0)
            gated(NR - 1, 1)
            h_low(NR - 2, 0)
            h_low(NR - 1, 1)

            def combine(t):
                b = t // TB
                y = (c_y[b] if b < B_FIRST else s_y[b % 2])[:, t % TB, :]
                if b == B - 1:
                    dve.wait_ge(last_picks[t % TB], 16 * 2)
                elif t % TB == 0:
                    dve.wait_ge(pick_in[b], 16 * 2 * TB)
                    if b < B_FIRST:
                        dve.wait_ge(base_in[b], 16)
                v.scalar_tensor_tensor(out=y, in0=picked[:, 0, t, :], scalar=gate[:, 0, t:t + 1], in1=y,
                                       op0=ALU.mult, op1=ALU.add).then_inc(s["one_added"], 1)
                dve.wait_ge(s["one_added"], t + 1)
                v.scalar_tensor_tensor(out=y, in0=picked[:, 1, t, :], scalar=gate[:, 1, t:t + 1], in1=y,
                                       op0=ALU.mult, op1=ALU.add).then_inc(s["mixed"], 1)

            for b in range(B_FIRST, B):
                for c in range(SC):
                    half = (b - B_FIRST) * SC + c - 3
                    gated_product(b, c)
                    if half >= 0:
                        combine(2 * half)
                    h_low_part(b, c)
                    if half >= 0:
                        combine(2 * half + 1)
                shared_out(b, b % 2)
            dve.wait_ge(s["y_done"], B + 2)
            for t in range(2 * (2 * SC - 3), NTOK):
                combine(t)

        @block.tensor
        def _(pe):
            mm = nc.tensor.matmul

            def claim(name, b):
                last = last_in_bank(name, b)
                if last:
                    pe.wait_ge(s["act_empty" if last[0] == "A" else "dve_empty"], last[1])

            def columns(n, lo=0, size=L):
                return slice(XPAD + n * L + lo, XPAD + n * L + lo + size) if isinstance(n, int) else bass.ds(n * L + (XPAD + lo), size)

            def x_transposed(n, par):
                pe.wait_ge(s["xn_made"], n + 1)
                for k in range(KD):
                    claim(f"xT{k}", n)
                    for t in range(TB):
                        i = nc.tensor.transpose(T(f"xT{k}", n)[:, t * P:(t + 1) * P], xnr[par][:, t, k * P:(k + 1) * P], ident)
                    i.then_inc(s["unit_full"], 1)

            def router(n):
                claim("router", n)
                pe.wait_ge(s["dve_empty"], emptied("xT1", n))
                for t in range(TB):
                    for j, (x, w) in enumerate(((0, 0), (0, 1), (1, 0))):
                        for k in range(KD):
                            i = mm(T("router", n)[:, t * NE:(t + 1) * NE], xT[x][:, k, columns(n, t * P, P)], wr[w][:, k, :],
                                   start=(j == 0 and k == 0), stop=(j == 2 and k == KD - 1))
                i.then_inc(s["unit_full"], 1)

            def queries(n):
                for m in range(KD):
                    claim(f"q{m}", n)
                    for j, (w, x) in enumerate(SPLIT):
                        for k in range(KD):
                            rhs = xT[x][:, k, columns(n)].rearrange("p (w c) -> p w c", w=TB)[:, :, 0:WIN + 1]
                            i = mm(T(f"q{m}", n)[:, 0:TB * (WIN + 1)].rearrange("p (w c) -> p w c", w=TB),
                                   wa[w][:, 0, k, m * P:(m + 1) * P], rhs, start=(j == 0 and k == 0), stop=(j == 2 and k == KD - 1))
                    i.then_inc(s["unit_full"], 1)

            def keys(n):
                for m in range(KD):
                    claim(f"k{m}", n)
                    for j, (w, x) in enumerate(SPLIT):
                        for k in range(KD):
                            i = mm(T(f"k{m}", n), wa[w][:, 1, k, m * P:(m + 1) * P], xT[x][:, k, columns(n)],
                                   start=(j == 0 and k == 0), stop=(j == 2 and k == KD - 1))
                    i.then_inc(s["unit_full"], 1)

            def values(n):
                for c in range(2):
                    claim(f"v{c}", n)
                    for w2 in range(2):
                        o = (2 * c + w2) * STRIDE + 1
                        for odd in range(2):
                            rows = P - 1 + odd
                            dst = T(f"v{c}", n)[0:rows, w2 * D + odd * P:w2 * D + (odd + 1) * P].rearrange("p (j d) -> p j d", d=HD)
                            for j, (w, x) in enumerate(SPLIT):
                                for k in range(KD):
                                    i = mm(dst, xT[x][:, k, columns(n, o - WIN * odd, rows)],
                                           wa[w][:, 2, k, :].rearrange("p (j o d) -> p o j d", o=2, d=HD)[:, odd],
                                           start=(j == 0 and k == 0), stop=(j == 2 and k == KD - 1))
                    i.then_inc(s["unit_full"], 1)

            def local_scores(n, first):
                pe.wait_ge(s["act_empty"], emptied("k0", n))
                pe.wait_ge(s["dve_empty"], emptied("k1", n))
                if not first:
                    pe.wait_ge(s["s_taken"], n)
                for w2 in range(0, TB, 2):
                    for m in range(KD):
                        for o in range(2):
                            for g in range(4):
                                for w in (w2, w2 + 1):
                                    row = slice(32 * g, 32 * g + 32)
                                    col = (((w // 2) * 2 + m) * 2 + o) * WIN
                                    i = mm(S[64 * (w % 2):64 * (w % 2) + 64, g, col:col + WIN],
                                           QT[o][row, m, w * (WIN + 1) + 1:(w + 1) * (WIN + 1)],
                                           KT[row, m, w * STRIDE + 1:w * STRIDE + 1 + WIN], start=True, stop=True)
                i.then_inc(s["s_full"], 1)

            def global_scores(n, first):
                pe.wait_ge(s["q0_ready"], n + 1)
                pe.wait_ge(*((s["bias_ready"], 1) if first else (s["g_exp"], n)))
                for m in range(KD):
                    i = mm(G[0:NH, :], q0[:, m, :], KT[:, m, :], start=(m == 0), stop=(m == KD - 1))
                i.then_inc(s["g_full"], 1)

            def global_p(b):
                claim("p0", b)
                pe.wait_ge(s["g_ready"], b + 1)
                for t in range(TB):
                    i = mm(T("p0", b)[:, t * NH:(t + 1) * NH], gs[0:NH, t * P:(t + 1) * P], ident[0:NH, 0:NH], start=True, stop=True)
                i.then_inc(s["unit_full"], 1)

            def global_u(b, par):
                claim("u", b)
                pe.wait_ge(s["act_empty"], emptied("p0", b))
                for k in range(KD):
                    for t in range(TB):
                        i = mm(T("u", b)[:, k * NH:(k + 1) * NH], xnr[par][:, t, k * P:(k + 1) * P], gp[:, t, :],
                               start=(t == 0), stop=(t == TB - 1))
                i.then_inc(s["unit_full"], 1)

            def p_transposed(b, par):
                pe.wait_ge(s["p_ready"], b + 1)
                for j in range(4):
                    claim(f"pT{j}", b)
                    for g in range(4):
                        src = E[par][:, g, 2 * j:2 * j + 2, :].rearrange("p o c -> p (o c)")
                        i = nc.tensor.transpose(T(f"pT{j}", b)[:, g * P:(g + 1) * P], src, ident)
                    i.then_inc(s["unit_full"], 1)

            def context(b, par):
                claim("ctx", b)
                pe.wait_ge(s["act_empty"], emptied("pT2", b))
                pe.wait_ge(s["dve_empty"], emptied("pT3", b))
                for m in range(KD):
                    for w in range(TB):
                        for g in range(4):
                            i = mm(T("ctx", b)[32 * g:32 * g + 32, (m * TB + w) * WIN:(m * TB + w + 1) * WIN],
                                   VB[par][:, w, 4 * m + g, :], PT[:, (w // 2) * 2 + m, g, (w % 2) * WIN:(w % 2 + 1) * WIN],
                                   start=True, stop=True)
                i.then_inc(s["unit_full"], 1)

            def out_rows_of(b):
                pe.wait_ge(s["dve_empty"], emptied("ctx", b))
                for c in range(2):
                    claim(f"out{c}", b)
                    for t2 in range(2):
                        for j, (w, x) in enumerate(SPLIT):
                            for m in range(KD):
                                i = mm(T(f"out{c}", b)[:, t2 * D:(t2 + 1) * D], cT[x][:, m, 2 * c + t2, :], wa[w][:, 3, m, :],
                                       start=(j == 0 and m == 0), stop=(j == 2 and m == KD - 1))
                    i.then_inc(s["unit_full"], 1)

            def turn(n, par, now=True, prev=True, nxt=True, first=False):
                b = n + (-1)
                if now:
                    router(n)
                    queries(n)
                if prev:
                    global_p(b)
                if now:
                    keys(n)
                if prev:
                    global_u(b, 1 - par)
                if now:
                    values(n)
                    local_scores(n, first)
                if prev:
                    p_transposed(b, 1 - par)
                if nxt:
                    x_transposed(n + 1, 1 - par)
                if prev:
                    context(b, 1 - par)
                if now:
                    global_scores(n, first)
                if prev:
                    out_rows_of(b)

            pe.wait_ge(s["consts_in"], 32)
            x_transposed(0, 0)
            pe.wait_ge(s["attn_w_in"], 80)
            pe.wait_ge(s["setup"], 1)
            for m in range(KD):
                mm(ps[:, 4, 0:D], bvm[:, m, :], wa_raw[:, 3, m, :], start=(m == 0), stop=(m == KD - 1))
            for m in range(KD):
                i = mm(ps[0:B, 4, D:2 * D], bvm[:, m, 1:1 + B], wa_raw[:, 3, m, :], start=(m == 0), stop=(m == KD - 1))
            i.then_inc(s["bias_psum"], 1)
            pe.wait_ge(s["attn_low"], 1)
            pe.wait_ge(s["pads_ready"], 1)
            turn(0, 0, prev=False, first=True)
            turn(1, 1)
            turn(2, 0)
            pairs(pe, turn, LOOP_FROM, LOOP_TO)
            turn(B - 1, 1, nxt=False)

            def up(b, c):
                n, q = b * SC + c, c % 2
                pe.wait_ge(s["h_done"], n + 1)
                bsl = slice(XPAD + b * L, XPAD + (b + 1) * L) if isinstance(b, int) else bass.ds(b * L + XPAD, L)
                for i2 in range(2):
                    for j, (w, x) in enumerate(SPLIT):
                        for k in range(KD):
                            i = mm(ps[:, 2 * q + i2, :], w12[w][:, i2, k, c * P:(c + 1) * P], xT[x][:, k, bsl],
                                   start=(j == 0 and k == 0), stop=(j == 2 and k == KD - 1))
                i.then_inc(s["a_full"], 1)

            def down(b, par, c):
                n, q = b * SC + c, c % 2
                if c == 0:
                    pe.wait_ge(s["y_done"], b + 1)
                for j, (x, w) in enumerate(((0, 0), (0, 1), (1, 0))):
                    if j == 0:
                        pe.wait_ge(s["hh_high"], n + 1)
                    if j == 2:
                        pe.wait_ge(s["hh_low"], n + 1)
                    for t in range(TB):
                        i = mm(ps[:, 4 + 2 * par + t // 2, (t % 2) * D:(t % 2 + 1) * D], s_hh[x][q][:, t * P:(t + 1) * P], w3[w][:, c, :],
                               start=(c == 0 and j == 0 and t % 2 == 0), stop=(c == SC - 1 and j == 2), skip_group_check=True)
                if c == SC - 1:
                    i.then_inc(s["y_full"], 1)

            def batch(b, par, last=False):
                for c in range(SC):
                    if c < SC - 1:
                        up(b, c + 1)
                    elif not last:
                        up(b + 1, 0)
                    down(b, par, c)

            global_p(B - 1)
            global_u(B - 1, 1)
            pe.wait_ge(s["s_taken"], B)
            pe.wait_ge(s["shared_low"], 1)
            up(0, 0)
            p_transposed(B - 1, 1)
            context(B - 1, 1)
            up(0, 1)
            out_rows_of(B - 1)

            pe.wait_ge(s["dve_empty"], emptied("out1", B - 1))
            for m in range(KD):
                for j, (w, x) in enumerate(SPLIT):
                    for k in range(KD):
                        i = mm(ps[:, 6, m * P:(m + 1) * P], wa[w][:, 2, k, m * P:(m + 1) * P],
                               uT[x][:, k, :, :].rearrange("p b h -> p (b h)"), start=(j == 0 and k == 0), stop=(j == 2 and k == KD - 1))
            i.then_inc(s["c0_full"], 1)
            down(0, 0, 0)
            pe.wait_ge(s["c0_ready"], 1)
            for j, (w, x) in enumerate(SPLIT):
                for m in range(KD):
                    i = mm(ps[0:B, 7, 0:D], c0[x][:, m, :], wa[w][:, 3, m, :], start=(j == 0 and m == 0), stop=(j == 2 and m == KD - 1))
            i.then_inc(s["out0_full"], 1)
            for c in range(1, SC):
                up(c // (SC - 1), (c + 1) % SC)
                down(0, 0, c)
                if c == 4:
                    pe.wait_ge(s["chosen_ready"], 1)
                    pe.wait_ge(s["out0_ready"], 1)
                    for i_ in range(2):
                        mm(ps[:, 6 + i_, :], ch[:, i_ * P:(i_ + 1) * P], ohm[:, :, :].rearrange("p e t -> p (e t)"),
                           start=True, stop=True).then_inc(s["prefix_full"], 1)
            pe.wait_ge(s["slots_ready"], 1)
            batch(1, 1)
            pairs(pe, batch, 2, B_FIRST - 2)
            batch(B_FIRST - 2, 0)

            def x_transposed(r, par, free=True):
                if free:
                    pe.wait_ge(s["rx_low"], r - 1)
                pe.wait_ge(s[f"xs_in{par}"], (r + (-par)) * 8 + 16)
                for j in range(2):
                    for k in range(KD):
                        at_ = (2 * j + k) * P
                        i = nc.tensor.transpose(ps[:, 2 + par, at_:at_ + P], xs[par][:, j, k * P:(k + 1) * P], ident)
                i.then_inc(s["rx_full"], 1)

            def experts_of(r):
                both = etab[0:1, 2 * r:2 * r + 2] if isinstance(r, int) else etab[0:1, bass.ds(r * 2, 2)]
                return nc.values_load_multi_w_load_instructions(
                    both, engines=[mybir.EngineType.PE], min_val=0, max_val=2 * EXPERT * (NE - 1),
                    skip_runtime_bounds_check_because="the table was clamped to the last expert when it was made")[1]

            def weights_at(e, lo, n):
                return ar16[:, lo:lo + 2 * (NE - 1) * EXPERT + n][:, bass.ds(e, n)]

            def gate_up(r, par, free=True, experts=None):
                experts = experts or experts_of(r)
                pe.wait_ge(s["rx_low"], r + 1)
                for j in range(2):
                    if free:
                        pe.wait_ge(s["r_h_done"], 2 * r + j - 1)
                    e = experts[j]
                    for n, (x, w) in enumerate(((0, 0), (0, 1), (1, 0))):
                        for k in range(KD):
                            at_ = (2 * j + k) * P
                            i = mm(ps[:, j, :], r_x[x][par][:, at_:at_ + P], weights_at(e, w * EXPERT + k * 2 * RH, 2 * RH),
                                   start=(n == 0 and k == 0), stop=(n == 2 and k == KD - 1))
                    i.then_inc(s["ab_full"], 1)

            def h_transposed(r, par, free=True):
                if free:
                    pe.wait_ge(s["rh_low"], r - 1)
                pe.wait_ge(s["r_h_done"], 2 * r + 2)
                for k in range(2 * RH // P):
                    i = nc.tensor.transpose(ps[:, 4 + par, k * P:(k + 1) * P], r_h[par][:, k * P:(k + 1) * P], ident)
                i.then_inc(s["rh_full"], 1)

            def routed_down(r, par, free=True, experts=None):
                experts = experts or experts_of(r)
                if free:
                    pe.wait_ge(s["ry_done"], r - 1)
                pe.wait_ge(s["rh_low"], r + 1)
                for j in range(2):
                    e = experts[j]
                    for n, (x, w) in enumerate(((0, 0), (0, 1), (1, 0))):
                        for k in range(RH // P):
                            at_ = (2 * j + k) * P
                            i = mm(ps[:, 6 + par, j * D:(j + 1) * D], r_hh[x][par][:, at_:at_ + P],
                                   weights_at(e, w * EXPERT + 2 * KD * RH + k * D, D),
                                   start=(n == 0 and k == 0), stop=(n == 2 and k == RH // P - 1))
                i.then_inc(s["ry_full"], 1)

            b = B_FIRST - 1
            for c in range(SC - 1):
                up(b, c + 1)
                down(b, 1, c)
            pe.wait_ge(s["h_done"], B_FIRST * SC + 2)
            x_transposed(0, 0, free=False)
            down(b, 1, SC - 1)
            x_transposed(1, 1, free=False)
            pe.wait_ge(s["routed_low"], 2 * NE + 2)
            pe.wait_ge(s["table_ready"], 1)
            for r in range(4):
                if r >= 1:
                    x_transposed(r + 1, (r + 1) % 2)
                gate_up(r, r % 2, free=r >= 1)
                if r == 1:
                    pe.wait_ge(s["y_done"], B_FIRST + 2)
                if r >= 1:
                    h_transposed(r - 1, (r - 1) % 2, free=r >= 3)
                if r >= 2:
                    routed_down(r - 2, r % 2, free=False)

            def routed(r, par, free=True):
                up_experts = experts_of(r)
                x_transposed(r + 1, 1 - par)
                gate_up(r, par, experts=up_experts)
                down_experts = experts_of(r - 2)
                h_transposed(r - 1, 1 - par)
                routed_down(r - 2, par, free, experts=down_experts)

            pairs(pe, routed, 4, NR - 2)
            routed(NR - 2, 0)
            gate_up(NR - 1, 1)
            h_transposed(NR - 2, 0)
            routed_down(NR - 3, 1)
            h_transposed(NR - 1, 1)
            routed_down(NR - 2, 0)
            up(B_FIRST, 0)
            routed_down(NR - 1, 1)
            pe.wait_ge(s["ry_done"], NR)
            batch(B_FIRST, 0)
            batch(B - 1, 1, last=True)


_INS = ['L0_attn_hidden_states', 'L0_attn_Wq', 'L0_attn_bq', 'L0_attn_Wk', 'L0_attn_bk', 'L0_attn_Wv', 'L0_attn_bv',
        'L0_attn_Wo', 'L0_attn_bo', 'L0_ffn_router_w', 'L0_ffn_expert_bias', 'L0_ffn_shared_w1', 'L0_ffn_shared_w2',
        'L0_ffn_shared_w3', 'L0_ffn_routed_w1', 'L0_ffn_routed_w2', 'L0_ffn_routed_w3']


def kernel(**inputs):
    import numpy as _np
    import concourse.bacc as _bacc
    from concourse import mybir as _mybir
    from concourse.bass_utils import run_bass_kernel_spmd as _run

    nc = _bacc.Bacc("TRN2", target_bir_lowering=False, num_devices=1)
    arrays, args = {}, {}
    f32, f16 = constants()
    given = {name: _np.ascontiguousarray(inputs[name]) for name in _INS}
    columns = _np.ascontiguousarray(_np.stack([given[f"L0_attn_b{c}"].reshape(KD, P) for c in "qkv"]).reshape(3 * KD, P).T)
    for name, x in {**given, "bias_columns": columns, "const_f32": f32, "const_f16": f16}.items():
        arrays[f"in_{name}_dram"] = x
        args[name] = nc.dram_tensor(f"in_{name}_dram", x.shape, _mybir.dt.from_np(x.dtype), kind="ExternalInput").ap()
    out = nc.dram_tensor("out_0_dram", (B, L, D), _mybir.dt.float32, kind="ExternalOutput").ap()
    moe_layer(nc, args, out)
    r = _run(nc, [arrays], core_ids=[0])
    return r.results[0]["out_0_dram"]
```
